# Optimizing a Trainium2 kernel written in Bass

```python
import numpy as np
import jax
import jax.numpy as jnp

def _softmax(x, axis=-1):
    return jax.nn.softmax(x, axis=axis)

def _gelu(x):
    return jax.nn.gelu(x, approximate=True)

def _silu(x):
    return jax.nn.silu(x)

def _sigmoid(x):
    return jax.nn.sigmoid(x)

def _layernorm(x, axis=-1, eps=1e-05):
    m = jnp.mean(x, axis=axis, keepdims=True)
    v = jnp.var(x, axis=axis, keepdims=True)
    return (x - m) / jnp.sqrt(v + eps)

def _scatter_add(tgt, idx, src, axis=0):
    return tgt.at[idx].add(src)

def _segment_sum(src, seg, n):
    return jax.ops.segment_sum(src, seg, n)
kernel_name = 'mk_flamingo_gated_d2_seqx_r4_4f5c08'

def setup_inputs(seed: int=0):
    np.random.seed(seed)
    _w = jnp.asarray

    def _rec_inputs():
        import jax
        import jax.numpy as jnp
        _rk = jax.random.key(seed)
        x = -0.0005533 + 1 * jax.random.normal(jax.random.fold_in(_rk, 1), (8, 100, 256), jnp.float32)
        _lenS = 100 - jax.random.randint(jax.random.fold_in(_rk, 7), (8,), 0, max(1, 100 // 4) + 1, jnp.int32)
        _lenS2 = 361 - jax.random.randint(jax.random.fold_in(_rk, 8), (8,), 0, max(1, 361 // 4) + 1, jnp.int32)
        _ctx_1024P = jax.random.normal(jax.random.fold_in(_rk, 11), (8, 16, 256), jnp.float32)
        _ctx_1024c = jax.random.dirichlet(jax.random.fold_in(_rk, 511), 0.3 * jnp.ones((16,), jnp.float32), (8, 361))
        _ctx_1024t = jnp.einsum('bsk,bkd->bsd', _ctx_1024c, _ctx_1024P)
        _ctx_1024t = _ctx_1024t * jax.lax.rsqrt(jnp.mean(jnp.square(_ctx_1024t)) + 1e-12) * 0.953939
        ctx_1024 = 0.00222621 + 0.99962 * (_ctx_1024t + 0.3 * jax.random.normal(jax.random.fold_in(_rk, 611), (8, 361, 256), jnp.float32))
        _g = jax.random.normal(jax.random.fold_in(_rk, 9001), (2, 2), jnp.float32)
        _g = jnp.sign(_g) * jnp.maximum(jnp.abs(_g), 1.0) + (_g == 0) * 1.0
        g_xattn = _g[0]
        g_ffn = _g[1]
        return (x, ctx_1024, g_xattn, g_ffn)
    x, ctx_1024, g_xattn, g_ffn = _rec_inputs()

    def _L0_xattn_setup():
        import jax, jax.numpy as jnp
        import numpy as np
        NX = 256
        N_HEAD = 16
        CS_SELF_ATTN_MASK_PROB = 1.0
        HISTORY_SEQ_LEN = 0
        CONTEXT_ATTN_BIAS = -2.0
        NEG = 10000.0

        def _split_heads(t, H):
            B, S, D = t.shape
            return t.reshape(B, S, H, D // H).transpose(0, 2, 1, 3)
        key = jax.random.key(seed)
        ks = jax.random.split(key, 8)
        B, T, Tc = (4, 224, 128)
        s = 0.02
        return {'x': jax.random.normal(ks[0], (B, T, NX), jnp.float32), 'context_seq': jax.random.normal(ks[1], (B, Tc, NX), jnp.float32), 'w_ref': jax.random.normal(ks[2], (NX, 2 * NX), jnp.float32) * s, 'b_ref': jnp.zeros((2 * NX,), jnp.float32), 'w_attn': jax.random.normal(ks[3], (NX, 3 * NX), jnp.float32) * s, 'b_attn': jnp.zeros((3 * NX,), jnp.float32), 'w_proj': jax.random.normal(ks[4], (NX, NX), jnp.float32) * s, 'b_proj': jnp.zeros((NX,), jnp.float32)}
    _L0_xattn_all = _L0_xattn_setup()
    _L0_xattn_in = {k: v for k, v in _L0_xattn_all.items() if k in ('w_ref', 'b_ref', 'w_attn', 'b_attn', 'w_proj', 'b_proj')}
    del _L0_xattn_all

    def _L0_ffn_setup():
        import jax, jax.numpy as jnp
        import numpy as np
        QMAX = 127.0

        def _ste_round(v):
            return v + jax.lax.stop_gradient(jnp.round(v) - v)

        def _act_fake_quant(x, clip_factor):
            scale = jax.nn.sigmoid(clip_factor) * jnp.max(jnp.abs(x)) / QMAX
            return jnp.clip(_ste_round(x / scale), -QMAX - 1.0, QMAX) * scale

        def _weight_fake_quant(w):
            scale = jnp.max(jnp.abs(w), axis=1, keepdims=True) / QMAX
            return jnp.clip(_ste_round(w / scale), -QMAX - 1.0, QMAX) * scale
        key = jax.random.key(seed)
        k1, k2, k3, k4 = jax.random.split(key, 4)
        B, S, H, I = (8, 2048, 256, 704)
        return {'x': jax.random.normal(k1, (B, S, H), dtype=jnp.float32), 'clip_x': jnp.full((1,), 4.0, dtype=jnp.float32), 'clip_down': jnp.full((1,), 4.0, dtype=jnp.float32), 'w_gate': jax.random.normal(k2, (I, H), dtype=jnp.float32) * 0.02, 'w_up': jax.random.normal(k3, (I, H), dtype=jnp.float32) * 0.02, 'w_down': jax.random.normal(k4, (H, I), dtype=jnp.float32) * 0.02}
    _L0_ffn_all = _L0_ffn_setup()
    _L0_ffn_in = {k: v for k, v in _L0_ffn_all.items() if k in ('clip_x', 'clip_down', 'w_gate', 'w_up', 'w_down')}
    del _L0_ffn_all

    def _L1_xattn_setup():
        import jax, jax.numpy as jnp
        import numpy as np
        D_MODEL = 256
        H = 16
        D_K = D_MODEL // H
        WINDOW = 64
        NEG = -1000000000.0

        def _local_mask(seq_len: int, window_size: int) -> jnp.ndarray:
            left = (window_size - 1) // 2
            right = window_size - 1 - left
            row = jnp.arange(seq_len)[:, None]
            col = jnp.arange(seq_len)[None, :]
            return (col >= row - left) & (col <= row + right)
        key = jax.random.key(seed)
        ks = jax.random.split(key, 12)
        B, S = (1, 1024)
        scale = 1.0 / np.sqrt(D_MODEL)
        inp = {'q': jax.random.normal(ks[0], (B, S, D_MODEL), dtype=jnp.float32), 'k': jax.random.normal(ks[1], (B, S, D_MODEL), dtype=jnp.float32), 'v': jax.random.normal(ks[2], (B, S, D_MODEL), dtype=jnp.float32), 'w_q': jax.random.normal(ks[3], (D_MODEL, D_MODEL), dtype=jnp.float32) * scale, 'b_q': jnp.zeros((D_MODEL,), dtype=jnp.float32), 'w_k': jax.random.normal(ks[4], (D_MODEL, D_MODEL), dtype=jnp.float32) * scale, 'b_k': jnp.zeros((D_MODEL,), dtype=jnp.float32), 'w_v': jax.random.normal(ks[5], (D_MODEL, D_MODEL), dtype=jnp.float32) * scale, 'b_v': jnp.zeros((D_MODEL,), dtype=jnp.float32), 'w_o': jax.random.normal(ks[6], (D_MODEL, D_MODEL), dtype=jnp.float32) * scale, 'b_o': jnp.zeros((D_MODEL,), dtype=jnp.float32)}
        return inp
    _L1_xattn_all = _L1_xattn_setup()
    _L1_xattn_in = {k: v for k, v in _L1_xattn_all.items() if k in ('w_q', 'b_q', 'w_k', 'b_k', 'w_v', 'b_v', 'w_o', 'b_o')}
    del _L1_xattn_all

    def _L1_ffn_setup():
        import jax, jax.numpy as jnp
        import numpy as np
        D_MODEL = 256
        D_FF = 1024
        N_EXPERTS = 8
        B, T = (4, 512)
        key = jax.random.key(seed)
        ks = jax.random.split(key, 7)
        s_in = 1.0 / np.sqrt(D_MODEL)
        s_ff = 1.0 / np.sqrt(D_FF)
        x = jax.random.normal(ks[0], (B, T, D_MODEL), dtype=jnp.float32)
        gate_w = jax.random.uniform(ks[1], (D_MODEL, N_EXPERTS), jnp.float32, -s_in, s_in)
        gate_b = jax.random.uniform(ks[2], (N_EXPERTS,), jnp.float32, -s_in, s_in)
        w1 = jax.random.uniform(ks[3], (N_EXPERTS, D_MODEL, D_FF), jnp.float32, -s_in, s_in)
        b1 = jax.random.uniform(ks[4], (N_EXPERTS, D_FF), jnp.float32, -s_in, s_in)
        w2 = jax.random.uniform(ks[5], (N_EXPERTS, D_FF, D_MODEL), jnp.float32, -s_ff, s_ff)
        b2 = jax.random.uniform(ks[6], (N_EXPERTS, D_MODEL), jnp.float32, -s_ff, s_ff)
        return {'x': x, 'gate_w': gate_w, 'gate_b': gate_b, 'w1': w1, 'b1': b1, 'w2': w2, 'b2': b2}
    _L1_ffn_all = _L1_ffn_setup()
    _L1_ffn_in = {k: v for k, v in _L1_ffn_all.items() if k in ('gate_w', 'gate_b', 'w1', 'b1', 'w2', 'b2')}
    del _L1_ffn_all
    return {'x': x, 'ctx_1024': ctx_1024, 'g_xattn': g_xattn, 'g_ffn': g_ffn, 'L0_xattn_w_ref': _L0_xattn_in['w_ref'], 'L0_xattn_b_ref': _L0_xattn_in['b_ref'], 'L0_xattn_w_attn': _L0_xattn_in['w_attn'], 'L0_xattn_b_attn': _L0_xattn_in['b_attn'], 'L0_xattn_w_proj': _L0_xattn_in['w_proj'], 'L0_xattn_b_proj': _L0_xattn_in['b_proj'], 'L0_ffn_clip_x': _L0_ffn_in['clip_x'], 'L0_ffn_clip_down': _L0_ffn_in['clip_down'], 'L0_ffn_w_gate': _L0_ffn_in['w_gate'], 'L0_ffn_w_up': _L0_ffn_in['w_up'], 'L0_ffn_w_down': _L0_ffn_in['w_down'], 'L1_xattn_w_q': _L1_xattn_in['w_q'], 'L1_xattn_b_q': _L1_xattn_in['b_q'], 'L1_xattn_w_k': _L1_xattn_in['w_k'], 'L1_xattn_b_k': _L1_xattn_in['b_k'], 'L1_xattn_w_v': _L1_xattn_in['w_v'], 'L1_xattn_b_v': _L1_xattn_in['b_v'], 'L1_xattn_w_o': _L1_xattn_in['w_o'], 'L1_xattn_b_o': _L1_xattn_in['b_o'], 'L1_ffn_gate_w': _L1_ffn_in['gate_w'], 'L1_ffn_gate_b': _L1_ffn_in['gate_b'], 'L1_ffn_w1': _L1_ffn_in['w1'], 'L1_ffn_b1': _L1_ffn_in['b1'], 'L1_ffn_w2': _L1_ffn_in['w2'], 'L1_ffn_b2': _L1_ffn_in['b2']}

def reference(x, ctx_1024, g_xattn, g_ffn, L0_xattn_w_ref, L0_xattn_b_ref, L0_xattn_w_attn, L0_xattn_b_attn, L0_xattn_w_proj, L0_xattn_b_proj, L0_ffn_clip_x, L0_ffn_clip_down, L0_ffn_w_gate, L0_ffn_w_up, L0_ffn_w_down, L1_xattn_w_q, L1_xattn_b_q, L1_xattn_w_k, L1_xattn_b_k, L1_xattn_w_v, L1_xattn_b_v, L1_xattn_w_o, L1_xattn_b_o, L1_ffn_gate_w, L1_ffn_gate_b, L1_ffn_w1, L1_ffn_b1, L1_ffn_w2, L1_ffn_b2):
    import jax
    import jax.numpy as jnp

    def _L0_xattn_ref(x, context_seq, w_ref, b_ref, w_attn, b_attn, w_proj, b_proj):
        import jax, jax.numpy as jnp
        import numpy as np
        NX = 256
        N_HEAD = 16
        CS_SELF_ATTN_MASK_PROB = 1.0
        HISTORY_SEQ_LEN = 0
        CONTEXT_ATTN_BIAS = -2.0
        NEG = 10000.0

        def _split_heads(t, H):
            B, S, D = t.shape
            return t.reshape(B, S, H, D // H).transpose(0, 2, 1, 3)
        B, T, _ = x.shape
        Tc = context_seq.shape[1]
        S = Tc + T
        Dh = NX // N_HEAD
        qkv = x @ w_attn + b_attn
        q, k, v = jnp.split(qkv, 3, axis=2)
        kv_ctx = context_seq @ w_ref + b_ref
        kc, vc = jnp.split(kv_ctx, 2, axis=2)
        key = jnp.concatenate([kc, k], axis=1)
        value = jnp.concatenate([vc, v], axis=1)
        qh = _split_heads(q, N_HEAD)
        kh = _split_heads(key, N_HEAD)
        vh = _split_heads(value, N_HEAD)
        w = jnp.einsum('bhtd,bhsd->bhts', qh, kh) / jnp.sqrt(jnp.float32(Dh))
        b = jnp.tri(T, S, k=S - T, dtype=w.dtype)
        w = w * b - NEG * (1.0 - b)
        i = jnp.arange(T)[:, None]
        j = jnp.arange(S)[None, :]
        stm = jnp.where(j == i, 0.0, 1.0).astype(w.dtype)
        w = w * stm - NEG * (1.0 - stm)
        ctx_mask = (j[0] < Tc).astype(w.dtype)
        w = w + CONTEXT_ATTN_BIAS * ctx_mask
        probs = jax.nn.softmax(w, axis=-1)
        a = jnp.einsum('bhts,bhsd->bhtd', probs, vh)
        a = a.transpose(0, 2, 1, 3).reshape(B, T, NX)
        return a @ w_proj + b_proj

    def _L0_ffn_ref(x, clip_x, clip_down, w_gate, w_up, w_down):
        import jax, jax.numpy as jnp
        import numpy as np
        QMAX = 127.0

        def _ste_round(v):
            return v + jax.lax.stop_gradient(jnp.round(v) - v)

        def _act_fake_quant(x, clip_factor):
            scale = jax.nn.sigmoid(clip_factor) * jnp.max(jnp.abs(x)) / QMAX
            return jnp.clip(_ste_round(x / scale), -QMAX - 1.0, QMAX) * scale

        def _weight_fake_quant(w):
            scale = jnp.max(jnp.abs(w), axis=1, keepdims=True) / QMAX
            return jnp.clip(_ste_round(w / scale), -QMAX - 1.0, QMAX) * scale
        xq = _act_fake_quant(x, clip_x[0])
        gate = jnp.einsum('bsh,ih->bsi', xq, _weight_fake_quant(w_gate))
        up = jnp.einsum('bsh,ih->bsi', xq, _weight_fake_quant(w_up))
        h = _act_fake_quant(jax.nn.silu(gate) * up, clip_down[0])
        return jnp.einsum('bsi,hi->bsh', h, _weight_fake_quant(w_down))

    def _L1_xattn_ref(q, k, v, w_q, b_q, w_k, b_k, w_v, b_v, w_o, b_o):
        import jax, jax.numpy as jnp
        import numpy as np
        D_MODEL = 256
        H = 16
        D_K = D_MODEL // H
        WINDOW = 64
        NEG = -1000000000.0

        def _local_mask(seq_len: int, window_size: int) -> jnp.ndarray:
            left = (window_size - 1) // 2
            right = window_size - 1 - left
            row = jnp.arange(seq_len)[:, None]
            col = jnp.arange(seq_len)[None, :]
            return (col >= row - left) & (col <= row + right)
        B, Sq, _ = q.shape
        Sk = k.shape[1]
        query = (q @ w_q.T + b_q).reshape(B, Sq, H, D_K).transpose(0, 2, 1, 3)
        key = (k @ w_k.T + b_k).reshape(B, Sk, H, D_K).transpose(0, 2, 1, 3)
        value = (v @ w_v.T + b_v).reshape(B, Sk, H, D_K).transpose(0, 2, 1, 3)
        scores = jnp.einsum('bhqd,bhkd->bhqk', query, key) / jnp.sqrt(jnp.asarray(D_K, dtype=query.dtype))
        if Sq == Sk:
            mask = _local_mask(Sq, WINDOW)
            scores = jnp.where(mask[None, None], scores, jnp.asarray(NEG, scores.dtype))
        attn = jax.nn.softmax(scores, axis=-1)
        x = jnp.einsum('bhqk,bhkd->bhqd', attn, value)
        x = x.transpose(0, 2, 1, 3).reshape(B, Sq, D_MODEL)
        return x @ w_o.T + b_o

    def _L1_ffn_ref(x, gate_w, gate_b, w1, b1, w2, b2):
        import jax, jax.numpy as jnp
        import numpy as np
        D_MODEL = 256
        D_FF = 1024
        N_EXPERTS = 8
        B, T = (4, 512)
        logits = jnp.einsum('btd,de->bte', x, gate_w) + gate_b
        scores = jax.nn.softmax(logits, axis=-1)
        top2_scores, top2_idx = jax.lax.top_k(scores, 2)
        onehot = jax.nn.one_hot(top2_idx, N_EXPERTS, dtype=x.dtype)
        comb = jnp.einsum('btr,btre->bte', top2_scores, onehot)
        h = jax.nn.relu(jnp.einsum('btd,edf->ebtf', x, w1) + b1[:, None, None, :])
        y = jnp.einsum('ebtf,efd->ebtd', h, w2) + b2[:, None, None, :]
        out = jnp.einsum('bte,ebtd->btd', comb, y)
        return out
    x = x + jnp.tanh(g_xattn[0]) * _L0_xattn_ref(_layernorm(x, axis=-1), ctx_1024, L0_xattn_w_ref, L0_xattn_b_ref, L0_xattn_w_attn, L0_xattn_b_attn, L0_xattn_w_proj, L0_xattn_b_proj)
    x = x + jnp.tanh(g_ffn[0]) * _L0_ffn_ref(_layernorm(x, axis=-1), L0_ffn_clip_x, L0_ffn_clip_down, L0_ffn_w_gate, L0_ffn_w_up, L0_ffn_w_down)
    x = x + jnp.tanh(g_xattn[1]) * _L1_xattn_ref(_layernorm(x, axis=-1), ctx_1024, ctx_1024, L1_xattn_w_q, L1_xattn_b_q, L1_xattn_w_k, L1_xattn_b_k, L1_xattn_w_v, L1_xattn_b_v, L1_xattn_w_o, L1_xattn_b_o)
    x = x + jnp.tanh(g_ffn[1]) * _L1_ffn_ref(_layernorm(x, axis=-1), L1_ffn_gate_w, L1_ffn_gate_b, L1_ffn_w1, L1_ffn_b1, L1_ffn_w2, L1_ffn_b2)
    return x

_drawn_inputs = setup_inputs


def setup_inputs(seed=0):
    import zlib

    import numpy as np

    out = dict(_drawn_inputs(seed))
    spreads = {'g_ffn': (-1.0, 0.6),
     'L0_xattn_b_ref': (0.0, 0.615),
     'L0_xattn_b_attn': (0.0, 0.652),
     'L0_xattn_b_proj': (0.0, 0.1),
     'L1_xattn_b_q': (0.0, 0.417),
     'L1_xattn_b_k': (0.0, 2.0),
     'L1_xattn_b_v': (0.0, 0.1),
     'L1_xattn_b_o': (0.0, 0.1)}
    factors = {'L0_xattn_w_ref': 2.758,
     'L0_xattn_w_attn': 8.0,
     'L1_ffn_gate_b': 5.475,
     'L1_ffn_b1': 8.0,
     'L1_ffn_b2': 8.0,
     'L0_ffn_w_gate': 2.682}
    for name, (base, spread) in spreads.items():
        noise = np.random.default_rng([zlib.crc32(name.encode()), seed]).standard_normal(out[name].shape)
        drawn = base * np.exp(spread * noise) if base else spread * noise
        out[name] = jnp.asarray(drawn.astype(out[name].dtype))
    for name, factor in factors.items():
        out[name] = (out[name] * factor).astype(out[name].dtype)
    return out
```

```python
from contextlib import ExitStack

import concourse.bass as bass
from concourse import mybir

ALU = mybir.AluOpType
ACT = mybir.ActivationFunctionType
F32 = mybir.dt.float32
F16 = mybir.dt.float16
X = mybir.AxisListType.X
XY = mybir.AxisListType.XY

P = 128
WS = 16.0
MAGIC = 12582912.0
EPS = 1e-5
QMAX = 127.0
BIG = 32768.0


def flamingo(nc, x, ctx_seq, g_xattn, g_ffn,
             w_ref, b_ref, w_attn, b_attn, w_proj, b_proj,
             clip_x, clip_down, w_gate, w_up, w_down,
             w_q, b_q, w_k, b_k, w_v, b_v, w_o, b_o,
             gate_w, gate_b, w1, b1, w2, b2, out):
    B, T, D = x.shape
    TC = ctx_seq.shape[1]
    NT = B * T
    H = 16
    DH = D // H
    KC = D // P
    NTILE = -(-NT // P)
    LAST = NT - (NTILE - 1) * P
    FULL = NTILE - 1
    S0 = T + TC
    NI = w_gate.shape[0]
    NIB = -(-NI // P)
    LASTI = NI - (NIB - 1) * P
    E = w1.shape[0]
    DF = w1.shape[2]
    FC = DF // P
    CH = -(-TC // 3)
    CSZ = [CH, (TC - CH) // 2, (TC - CH) // 2]
    COFF = [0, CSZ[0], CSZ[0] + CSZ[1]]
    KROWS = 4 * DH
    SCALE = DH ** -0.5 / (WS * WS)
    CTX_BIAS = -2.0
    VW = DH + 1
    HM = H // 2
    HG = 4
    GW = HG * VW
    VS = GW + VW
    WIDE0 = 512
    TT = [(t * P, P if t < FULL else LAST) for t in range(NTILE)]
    xf = x.rearrange("b t d -> (b t) d")
    of = out.rearrange("b t d -> (b t) d")

    q_dram = nc.dram_tensor("q_scratch", (2, KC, P, NT), F16, kind="Internal").ap()
    sk_dram = nc.dram_tensor("own_key_scratch", (2, KC, P, NT), F16, kind="Internal").ap()
    k_dram = [nc.dram_tensor(f"k{l}_scratch", (B, 2, KC, P, TC), F16, kind="Internal").ap() for l in range(2)]
    v1_dram = nc.dram_tensor("v1_scratch", (B, CH, 3 * H * VW), F32, kind="Internal").ap()

    top = ExitStack()
    with top:
        def sb(name, shape, dt=F32, es=top):
            return es.enter_context(nc.sbuf_tensor(name, shape, dt))

        def sem(name):
            return top.enter_context(nc.semaphore(name))

        PS = top.enter_context(nc.psum_tensor("PS", [P, 8, 512], F32))
        wide = [PS[:, 2 * w:2 * w + 2, :].rearrange("p a n -> p (a n)") for w in range(4)]
        sm_bank = [PS[:, 0, :], PS[:, 1, :]]
        st_bank = [PS[:, 2, :], PS[:, 3, :]]
        pv_bank = PS[:, 4, :]
        misc = [PS[:, 5, :], PS[:, 6, :], PS[:, 7, :]]

        xr = sb("xr", [P, NTILE, D])
        xn = sb("xn", [P, NTILE, D])
        xTh = sb("xTh", [P, KC, NT], F16)
        xTl = sb("xTl", [P, KC, NT], F16)
        ident = sb("ident", [P, P])
        ones = sb("ones", [P, P])
        stats = sb("stats", [P, NTILE, 6])
        mv = sb("mv", [P, NTILE, 2])
        veps = sb("veps", [P, NTILE])
        rstd = sb("rstd", [P, NTILE])
        mhalf = sb("mhalf", [P, NTILE])
        gts = sb("gts", [P, 4])
        tg = sb("tg", [P, 4])
        tgs = sb("tgs", [P, 4])
        clips = sb("clips", [P, 2])
        clipt = sb("clipt", [P, 2])
        bcol = sb("bcol", [P, 5, 2])
        brow = sb("brow", [P, 3, D])
        bpr = sb("bpr", [P, 2, D])
        gbr = sb("gbr", [P, E])
        b1c = sb("b1c", [P, E, FC])
        b2r = sb("b2r", [E, D])
        gwr = sb("gwr", [P, KC, E])
        gwh = sb("gwh", [P, KC, E], F16)
        gwl = sb("gwl", [P, KC, E], F16)
        wph = sb("wph", [P, 2, KC, D], F16)
        wpl = sb("wpl", [P, 2, KC, D], F16)
        w1kh = sb("w1kh", [P, 2, KC, D], F16)
        w1kl = sb("w1kl", [P, 2, KC, D], F16)
        aTh = sb("aTh", [P, KC, NT], F16)
        aTl = sb("aTl", [P, KC, NT], F16)
        magic = sb("magic", [P, 2])
        small = sb("small", [P, 8])
        row1 = sb("row1", [1, 1])

        s_x = sem("x_loaded")
        s_pad = sem("padding_cleared")
        s_bias = sem("biases_loaded")
        s_biasp = sem("biases_scaled")
        s_wr = [sem(f"raw_weights_loaded{k}") for k in range(4)]
        s_const = sem("constants_made")
        s_zero = sem("values_padding_cleared")
        s_tanh = sem("gates_through_tanh")
        s_dve = sem("vector_step")
        s_var = sem("variances_taken")
        s_rstd = sem("rstd_made")
        s_xn = sem("rows_normalised")
        s_wh8 = sem("raw_weights_high_half")
        s_split = sem("weights_split")
        s_wd = sem("wide_product_done")
        s_wh = sem("wide_high_half_done")
        s_wf = sem("wide_tile_freed")
        s_ctx = [sem(f"context_loaded{p}") for p in range(2)]
        s_md = sem("misc_product_done")
        s_mh = sem("misc_high_half_done")
        s_mf = sem("misc_bank_freed")
        s_smd = sem("score_rows_done")
        s_smf = sem("score_max_taken")
        s_std = sem("score_columns_done")
        s_exp = sem("exponentials_done")
        s_msk = sem("masks_done")
        s_mb = sem("masks_begun")
        s_pvd = sem("head_values_done")
        s_ev = sem("outcome_copied")
        s_tvd = sem("outcome_turned")
        s_rd = sem("denominators_inverted")
        s_nrm = sem("heads_normalised")
        s_ks = [[sem(f"stack_loaded{p}{m}") for m in range(2)] for p in range(2)]
        s_nm = [sem(f"max_row_loaded{p}") for p in range(2)]
        s_kw = [[sem(f"k{l}_written{p}") for p in range(2)] for l in range(2)]
        s_qw = sem("queries_written")
        s_v1w = [sem(f"v1_written{p}") for p in range(2)]
        s_vc = [sem(f"v1_loaded{p}") for p in range(2)]
        s_out = sem("output_written")

        def split3(pe, out_ap, lh, ll, rh, rl, first, last):
            nc.tensor.matmul(out_ap, lh, rh, start=first, stop=False)
            nc.tensor.matmul(out_ap, lh, rl, start=False, stop=False)
            return nc.tensor.matmul(out_ap, ll, rh, start=False, stop=last)

        def layernorm_stats(dve):
            for t in range(NTILE):
                nc.vector.bn_stats(stats[:, t, :], xr[:, t, :]).then_inc(s_dve, 1)
            step[0] += NTILE
            dve.wait_ge(s_dve, step[0])
            for t in range(NTILE):
                nc.vector.bn_aggr(mv[:, t, :], stats[:, t, :]).then_inc(s_dve, 1)
            step[0] += NTILE
            dve.wait_ge(s_dve, step[0])
            nc.vector.tensor_scalar(veps[:, :], mv[:, :, 1], EPS, None, ALU.add).then_inc(s_var, 1)

        def layernorm_rows(dve, k):
            dve.wait_ge(s_rstd, k + 1)
            for t in range(NTILE):
                nc.vector.tensor_scalar(xn[:, t, :], xr[:, t, :], mv[:, t, 0:1], rstd[:, t:t + 1],
                                        ALU.subtract, ALU.mult).then_inc(s_xn, 1)

        def pool_rstd(pool, k):
            pool.wait_ge(s_var, k + 1)
            nc.gpsimd.tensor_tensor(rstd[:, :], veps[:, :], mhalf[:, :], ALU.pow).then_inc(s_rstd, 1)

        def transpose_rows(pe, n, kc):
            for t, (t0, tn) in enumerate(TT):
                last = nc.tensor.transpose(wide[n % 4][:, t0:t0 + tn], xn[0:tn, t, kc * P:(kc + 1) * P],
                                           ident[0:tn, 0:tn])
            last.then_inc(s_wd, 1)

        def project_T(pe, n, wh, wl, mb):
            for t0, t1 in ((0, WIDE0), (WIDE0, NT)):
                for kc in range(KC):
                    last = split3(pe, wide[n % 4][:, t0:t1], wh[:, kc, mb * P:(mb + 1) * P],
                                  wl[:, kc, mb * P:(mb + 1) * P], xTh[:, kc, t0:t1], xTl[:, kc, t0:t1],
                                  kc == 0, kc == KC - 1)
            last.then_inc(s_wd, 1)

        def wide_hi(act, n, dst, bias=None):
            act.wait_ge(s_wd, n + 1)
            src = wide[n % 4][:, 0:NT]
            if bias is None:
                nc.scalar.activation(dst, src, ACT.Copy).then_inc(s_wh, 1)
            else:
                nc.scalar.activation(dst, src, ACT.Identity, bias=bias).then_inc(s_wh, 1)

        def wide_lo(dve, n, hi, dst, bias=None, nh=None):
            dve.wait_ge(s_wh, (n if nh is None else nh) + 1)
            src = wide[n % 4][:, 0:NT]
            if bias is None:
                nc.vector.tensor_tensor(dst, src, hi, ALU.subtract).then_inc(s_wf, 1)
            else:
                nc.vector.scalar_tensor_tensor(out=dst, in0=src, scalar=bias, in1=hi, op0=ALU.add,
                                               op1=ALU.subtract).then_inc(s_wf, 1)

        step = [0]

        es_att = top.enter_context(ExitStack())
        bigid = sb("bigid", [T, T], F16, es_att)
        maskv = sb("maskv", [T, 2 * T], F16, es_att)
        KSa = sb("KS", [P, 2, H, S0], F16, es_att)
        KS = [KSa[0:KROWS + 1, p] for p in range(2)]
        QS = [sb(f"QS{p}", [KROWS + 1, H, T], F16, es_att) for p in range(2)]
        PT = sb("PT", [P, 4, H, T], F32, es_att)
        qh = sb("qh", [P, KC, NT], F16, es_att)
        ql = sb("ql", [P, KC, NT], F16, es_att)
        aallw = sb("aall", [P, B, D], F32, es_att)
        aall = aallw[0:T]
        mx = [sb(f"mx{p}", [T, H], F32, es_att) for p in range(2)]
        nm = [sb(f"nm{p}", [H, T], F16, es_att) for p in range(2)]
        rden = sb("rden", [T, H], F32, es_att)
        pvs = sb("pvs", [GW, H // HG * T], F32, es_att)
        Vc = [sb(f"Vc{p}", [CH, 3, H, VS], F32, es_att) for p in range(2)]

        es_a = es_att.enter_context(ExitStack())
        cn = [sb(f"cn{p}", [CH, 3, D], F32, es_a) for p in range(2)]
        cTh = [sb(f"cTh{p}", [P, KC, TC], F16, es_a) for p in range(2)]
        cTl = [sb(f"cTl{p}", [P, KC, TC], F16, es_a) for p in range(2)]
        kc_ = [[sb(f"kc{l}{p}", [P, 2, KC, TC], F16, es_a) for p in range(2)] for l in range(2)]
        V1s = [xn[0:CH, :, :].rearrange("p t d -> p (t d)")[:, p * 3 * H * VW:(p + 1) * 3 * H * VW].rearrange(
            "p (c h v) -> p c h v", c=3, h=H) for p in range(2)]
        skh, skl = aTh, aTl
        Vs = sb("Vs", [T, B, H, VW], F32, es_a)
        wah = sb("wah", [P, KC, 3 * D], F16, es_a)
        wal = sb("wal", [P, KC, 3 * D], F16, es_a)
        wrh = sb("wrh", [P, KC, D], F16, es_a)
        wrl = sb("wrl", [P, KC, D], F16, es_a)
        wvh = sb("wvh", [P, KC, 2, D], F16, es_a)
        wvl = sb("wvl", [P, KC, 2, D], F16, es_a)
        PTf = PT[:, :, :, :].rearrange("p c h t -> p c (h t)")
        r_attn = PTf[:, 0, 0:KC * 3 * D].rearrange("p (k n) -> p k n", k=KC)
        r_ref = PTf[:, 1, 0:KC * 2 * D].rearrange("p (k n) -> p k n", k=KC)
        r_proj = PTf[:, 1, KC * 2 * D:KC * 3 * D].rearrange("p (k n) -> p k n", k=KC)
        r_l1 = [PTf[:, 2, m * KC * D:(m + 1) * KC * D].rearrange("p (k n) -> p k n", k=KC) for m in range(3)]
        r_l1.append(PTf[:, 3, 0:KC * D].rearrange("p (k n) -> p k n", k=KC))

        MBANK = [2, 0, 1, 2, 0, 1, 2, 0, 1, 0]
        UT, UK, UN, UV = 0, 2, 6, 7
        SMH = [2, 1, 2, 1, 2, 1, 2, 1, 2, 1, 1, 0, 0, 0, 0, 0]
        TKS = {0: 0, 1: 1, 3: 2, 4: 3, 6: 4, 7: 5}
        NSTEP = 12

        def pe_T(pe, j, o, kc, n):
            p = o % 2
            if kc == 0:
                pe.wait_ge(s_ctx[p], 32 * (j + o // 2 + 1))
            if not (isinstance(n, int) and n < 2):
                pe.wait_ge(s_mf, n - 1)
            bank = misc[MBANK[UT + kc]]
            for c in range(3):
                last = nc.tensor.transpose(bank[:, COFF[c]:COFF[c] + CSZ[c]],
                                           cn[p][0:CSZ[c], c, kc * P:(kc + 1) * P], ident[0:CSZ[c], 0:CSZ[c]])
            last.then_inc(s_md, 1)

        def pe_K(pe, j, o, k, n, nT):
            p, l, mb = o % 2, k // 2, k % 2
            pe.wait_ge(s_mf, nT + 1)
            wh, wl = (wrh, wrl) if l == 0 else (w1kh[:, 0], w1kl[:, 0])
            bank = misc[MBANK[UK + k]][:, 0:TC]
            if k > 1:
                pe.wait_ge(s_mf, n - 1)
            for kc in range(KC):
                last = split3(pe, bank, wh[:, kc, mb * P:(mb + 1) * P], wl[:, kc, mb * P:(mb + 1) * P],
                              cTh[p][:, kc, :], cTl[p][:, kc, :], kc == 0, kc == KC - 1)
            last.then_inc(s_md, 1)

        def pe_V(pe, j, o, c, n):
            p = o % 2
            pe.wait_ge(s_mf, n - 1)
            bank = misc[MBANK[UV + c]][0:CSZ[c], :]
            sl = slice(COFF[c], COFF[c] + CSZ[c])
            for kc in range(KC):
                last = split3(pe, bank, cTh[p][:, kc, sl], cTl[p][:, kc, sl],
                              wvh[:, kc, :, :].rearrange("p l n -> p (l n)"),
                              wvl[:, kc, :, :].rearrange("p l n -> p (l n)"), kc == 0, kc == KC - 1)
            last.then_inc(s_md, 1)

        def pe_SM(pe, j, o, h, layer, smn):
            p = o % 2
            if h % HM == 0:
                nd = NDS[layer]
                pe.wait_ge(s_ks[p][h // HM], 16 * nd * (j + o // 2 + 1) + KSB[layer])
            idx = 2 * H * j + H * o + h + smn
            if not (isinstance(idx, int) and idx < 2):
                pe.wait_ge(s_smf, idx - 1)
            bank = sm_bank[h % 2]
            if layer == 0:
                nc.tensor.matmul(bank[0:T, 0:S0], QS[p][0:KROWS, h, :], KS[p][0:KROWS, h, :],
                                 start=True, stop=False)
                nc.tensor.matmul(bank[0:T, 0:2 * T], bigid[:, :], maskv[:, :], start=False, stop=True
                                 ).then_inc(s_smd, 1)
            else:
                nc.tensor.matmul(bank[0:T, 0:TC], QS[p][0:KROWS, h, :], KS[p][0:KROWS, h, 0:TC],
                                 start=True, stop=True).then_inc(s_smd, 1)

        def pe_N(pe, j, o, smn, n, freed):
            p = o % 2
            pe.wait_ge(s_smf, 2 * H * j + H * (o + 1) + smn)
            pe.wait_ge(s_mf, freed)
            nc.tensor.transpose(misc[MBANK[UN]][0:H, 0:T], mx[p][:, :], ident[0:T, 0:T]).then_inc(s_md, 1)

        def pe_ST(pe, j, o, t, layer, stn, nmc):
            p = o % 2
            nch = 4 - layer
            g, c = t // nch, t % nch
            if t == 0:
                pe.wait_ge(s_nm[p], 16 * (j + o // 2 + 1) + nmc)
            if t >= 2:
                idx = 2 * (H // HG) * nch * j + (H // HG) * nch * o + t + stn
                pe.wait_ge(s_exp, idx - 1)
            bank = st_bank[t % 2]
            if layer == 0:
                k0, kn = (0, T) if c == 0 else (T + COFF[c - 1], CSZ[c - 1])
            else:
                k0, kn = COFF[c], CSZ[c]
            for i in range(HG):
                h = g * HG + i
                last = nc.tensor.matmul(bank[0:kn, i * T:(i + 1) * T], KS[p][:, h, k0:k0 + kn],
                                        QS[p][:, h, :], start=True, stop=True)
            last.then_inc(s_std, 1)

        def pe_PV(pe, j, o, h, layer, stn, mkn, nrn):
            p = o % 2
            nch = 4 - layer
            g = h // HG
            if h % HG == 0:
                per = (H // HG) * nch
                pe.wait_ge(s_exp, 2 * per * j + per * o + nch * (g + 1) + stn)
                if layer == 0:
                    pe.wait_ge(s_msk, 2 * (H // HG) * j + (H // HG) * o + g + 1)
                else:
                    if g == 0:
                        pe.wait_ge(s_vc[p], 16 * (j + o // 2 + 1))
            if h == 0 and (isinstance(j, int) or layer == 1) and not (isinstance(j, int) and 2 * j + o + nrn == 0):
                pe.wait_ge(s_nrm, 2 * j + o + nrn)
            i = h % HG
            dst = pv_bank[0:GW, g * T:(g + 1) * T]
            for c in range(nch):
                if layer == 0:
                    kn = T if c == 0 else CSZ[c - 1]
                    v = VSB[p][:, :, :] if c == 0 else Vc[p][0:kn, c - 1, :, :]
                else:
                    kn = CSZ[c]
                    v = Vc[p][0:kn, c, :, :]
                w0 = g * HG * VS + i * GW
                last = nc.tensor.matmul(dst, v.rearrange("p h v -> p (h v)")[:, w0:w0 + GW], PT[0:kn, c, h, :],
                                        start=(i == 0 and c == 0), stop=(i == HG - 1 and c == nch - 1))
            last.then_inc(s_pvd, 1)

        def pe_turn(pe, j, o, bsum):
            pe.wait_ge(s_ev, 2 * j + o + 1 + bsum)
            for g in range(H // HG):
                last = nc.tensor.transpose(pv_bank[0:T, g * GW:(g + 1) * GW], pvs[:, g * T:(g + 1) * T],
                                           ident[0:GW, 0:GW])
            last.then_inc(s_tvd, 1)

        def act_hi_T(act, j, o, kc, n):
            act.wait_ge(s_md, n + 1)
            nc.scalar.activation(cTh[o % 2][:, kc, :], misc[MBANK[UT + kc]][:, 0:TC], ACT.Copy).then_inc(s_mh, 1)

        def act_hi_K(act, j, o, k, n):
            p, l, mb = o % 2, k // 2, k % 2
            act.wait_ge(s_md, n + 1)
            nc.scalar.activation(kc_[l][p][:, 0, mb, :], misc[MBANK[UK + k]][:, 0:TC], ACT.Identity,
                                 bias=bcol[:, 2 + l, mb:mb + 1]).then_inc(s_mh, 1)

        def act_exp(act, j, o, t, layer, stn):
            nch = 4 - layer
            g, c = t // nch, t % nch
            idx = 2 * (H // HG) * nch * j + (H // HG) * nch * o + t + stn
            act.wait_ge(s_std, idx + 1)
            if layer == 0:
                kn, bias = (T, 0.0) if c == 0 else (CSZ[c - 1], ctxb[0:CSZ[c - 1], 0:1])
            else:
                kn, bias = CSZ[c], 0.0
            nc.scalar.activation(PT[0:kn, c, g * HG:(g + 1) * HG, :].rearrange("p h t -> p (h t)"),
                                 st_bank[t % 2][0:kn, 0:HG * T], ACT.Exp, scale=SCALE, bias=bias
                                 ).then_inc(s_exp, 1)

        def act_evac(act, j, o, bsum):
            act.wait_ge(s_pvd, H * (2 * j + o + 1 + bsum))
            nc.scalar.activation(pvs[:, :], pv_bank[0:GW, 0:H // HG * T], ACT.Copy).then_inc(s_ev, 1)

        def dve_lo_T(dve, j, o, kc, n, nh):
            p = o % 2
            dve.wait_ge(s_mh, nh + 1)
            nc.vector.tensor_tensor(cTl[p][:, kc, :], misc[MBANK[UT + kc]][:, 0:TC], cTh[p][:, kc, :],
                                    ALU.subtract).then_inc(s_mf, 1)

        def dve_lo_K(dve, j, o, k, n, nh):
            p, l, mb = o % 2, k // 2, k % 2
            dve.wait_ge(s_mh, nh + 1)
            nc.vector.scalar_tensor_tensor(out=kc_[l][p][:, 1, mb, :], in0=misc[MBANK[UK + k]][:, 0:TC],
                                           scalar=bcol[:, 2 + l, mb:mb + 1], in1=kc_[l][p][:, 0, mb, :],
                                           op0=ALU.add, op1=ALU.subtract).then_inc(s_mf, 1)

        def dve_V(dve, j, o, c, n):
            p = o % 2
            dve.wait_ge(s_md, n + 1)
            kn = CSZ[c]
            bank = misc[MBANK[UV + c]][0:kn, :].rearrange("p (l h d) -> p l h d", l=2, h=H)
            row = brow[0:kn, 1:3, :].rearrange("p l (h d) -> p l h d", h=H)
            nc.vector.tensor_tensor(Vc[p][0:kn, c, :, 0:DH], bank[:, 0], row[:, 0], ALU.add)
            nc.vector.tensor_tensor(V1s[p][0:kn, c, :, 0:DH], bank[:, 1], row[:, 1], ALU.add).then_inc(s_mf, 1)

        def dve_max(dve, j, o, h, layer, smn):
            p = o % 2
            dve.wait_ge(s_smd, 2 * H * j + H * o + h + smn + 1)
            nc.vector.tensor_reduce(mx[p][:, h:h + 1], sm_bank[h % 2][0:T, 0:(S0 if layer == 0 else TC)], X,
                                    ALU.max).then_inc(s_smf, 1)

        def dve_N(dve, j, o, n):
            p = o % 2
            dve.wait_ge(s_md, n + 1)
            nc.vector.tensor_scalar(nm[p][:, :], misc[MBANK[UN]][0:H, 0:T], -1.0 / (WS * WS), None,
                                    ALU.mult).then_inc(s_mf, 1)

        def dve_norm(dve, j, o, bsum):
            dve.wait_ge(s_tvd, 2 * j + o + 1 + bsum)
            pv = pv_bank[0:T, 0:H * VW].rearrange("p (h v) -> p h v", h=H)
            nc.vector.reciprocal(rden[:, :], pv[:, :, DH]).then_inc(s_rd, 1)
            dve.wait_ge(s_rd, 2 * j + o + 1 + bsum)
            nc.vector.tensor_tensor(aall[:, bass.ds(2 * j + o, 1), :].rearrange("p a (h d) -> p (a h) d", h=H),
                                    pv[:, :, 0:DH], rden[:, :].unsqueeze(2).to_broadcast([T, H, DH]),
                                    ALU.mult).then_inc(s_nrm, 1)
            
        NDS = [12, 8]
        KSB = [0, 16 * 12 * (B // 2)]
        VSB = [sb(f"VSB{p}", [T, H, VS], F32, es_a) for p in range(2)]
        ctxb = sb("ctxb", [P, 1], F32, es_a)
        s_vsb = [sem(f"own_values_staged{p}") for p in range(2)]
        NBL0 = B

        def sp_ctx(sp, j, o):
            p = o % 2
            b = 2 * j + o
            src = ctx_seq[bass.ds(b, 1), :, :].rearrange("a t d -> (a t) d")
            sp.dma_start(cn[p][:, 0, :], src[0:CH, :]).then_inc(s_ctx[p], 16)
            sp.dma_start(cn[p][0:CSZ[1], 1:3, :], src[CH:TC, :].rearrange("(c t) d -> t c d", c=2)
                         ).then_inc(s_ctx[p], 16)

        def sp_stack0(sp, j, o, mb):
            p = o % 2
            hs = slice(mb * HM, (mb + 1) * HM)
            b = 2 * j + o
            for s, (q, k) in enumerate(((0, 0), (0, 1), (1, 0), (1, 1))):
                rows = slice(s * DH, (s + 1) * DH)
                qs = q_dram[q, mb, :, bass.ds(b * T, T)]
                ks = sk_dram[k, mb, :, bass.ds(b * T, T)]
                kx = k_dram[0][bass.ds(b, 1), k, mb, :, :].rearrange("b p t -> (b p) t")
                for dst, src in ((QS[p][rows, hs, :], qs), (KS[p][rows, hs, 0:T], ks), (KS[p][rows, hs, T:S0], kx)):
                    sp.dma_start(dst, src.rearrange("(h d) t -> d h t", h=HM)).then_inc(s_ks[p][mb], 16)

        def sp_keys_out(sp, j, o, l):
            p = o % 2
            sp.dma_start(k_dram[l][bass.ds(2 * j + o, 1)].rearrange("b s k p t -> p (b s k) t"),
                         kc_[l][p][:, :, :, :].rearrange("p s k t -> p (s k) t")).then_inc(s_kw[l][p], 16)

        def sp_stack1(sp, j, o, mb):
            p = o % 2
            hs = slice(mb * HM, (mb + 1) * HM)
            b = 2 * j + o
            for s, (q, k) in enumerate(((0, 0), (0, 1), (1, 0), (1, 1))):
                rows = slice(s * DH, (s + 1) * DH)
                kx = k_dram[1][bass.ds(b, 1), k, mb, :, :].rearrange("b p t -> (b p) t")
                qs = q_dram[q, mb, :, bass.ds(b * T, T)]
                for dst, src in ((KS[p][rows, hs, 0:TC], kx), (QS[p][rows, hs, :], qs)):
                    sp.dma_start(dst, src.rearrange("(h d) t -> d h t", h=HM)).then_inc(s_ks[p][mb], 16)

        with nc.Block() as block:

            @block.sync
            def _(sp):
                sp.dma_start(xr[:, 0:FULL, :], xf[0:FULL * P, :].rearrange("(t p) d -> p t d", p=P)).then_inc(s_x, 16)
                sp.wait_ge(s_pad, 1)
                sp.dma_start(xr[0:LAST, FULL, :], xf[FULL * P:NT, :]).then_inc(s_x, 16)
                sp.dma_start(r_attn, w_attn.rearrange("(k p) n -> p k n", p=P)).then_inc(s_wr[0], 16)
                sp_ctx(sp, 0, 0)
                sp.dma_start(r_ref, w_ref.rearrange("(k p) n -> p k n", p=P)).then_inc(s_wr[1], 16)
                sp.dma_start(r_proj, w_proj.rearrange("(k p) n -> p k n", p=P)).then_inc(s_wr[1], 16)
                for m, w in enumerate((w_k, w_v, w_q, w_o)):
                    sp.dma_start(r_l1[m], w.rearrange("(k p) n -> p k n", p=P)).then_inc(s_wr[2], 16)
                sp_ctx(sp, 0, 1)

                for mb in range(KC):
                    sp.wait_ge(s_wf, 3 + mb)
                    for k, src in enumerate((qh, ql)):
                        sp.dma_start(q_dram[k, mb], src[:, mb, :]).then_inc(s_qw, 16)
                for mb in range(KC):
                    sp.wait_ge(s_wf, 5 + mb)
                    for k, src in enumerate((skh, skl)):
                        sp.dma_start(sk_dram[k, mb], src[:, mb, :]).then_inc(s_qw, 16)
                for o in range(2):
                    sp.wait_ge(s_mf, 6 * o + 4)
                    sp_keys_out(sp, 0, o, 0)
                    if o == 0:
                        sp.wait_ge(s_qw, 16 * 8)
                    sp.wait_ge(s_kw[0][o], 16)
                    for mb in range(KC):
                        sp_stack0(sp, 0, o, mb)
                    sp.wait_ge(s_mf, 6 * o + 6)
                    sp_keys_out(sp, 0, o, 1)
                sp.wait_ge(s_zero, 1)
                sp.dma_start(VSB[0][:, :, 0:VW], Vs[:, 0, :, :]).then_inc(s_vsb[0], 16)
                sp.wait_ge(s_mf, 15)
                sp.dma_start(v1_dram[0], V1s[0][:, :, :, :].rearrange("p c h v -> p (c h v)")).then_inc(s_v1w[0], 16)
                sp.wait_ge(s_mf, 16)
                sp.dma_start(QS[0][KROWS:KROWS + 1, :, :], nm[0][:, :]).then_inc(s_nm[0], 16)

                def round0(j, u, keys, nxt):
                    n0 = 16 + 10 * (2 * j + u)
                    p = u % 2
                    n1 = n0 + (UN if keys else 0)
                    if keys:
                        sp_ctx(sp, j, u + 2)
                    if nxt:
                        sp.wait_ge(s_std, 16 * (2 * j + u) + 8)
                        sp.dma_start(VSB[1 - p][:, :, 0:VW], Vs[:, bass.ds(2 * j + u + 1, 1), :, :].rearrange(
                            "p a h v -> p (a h) v")).then_inc(s_vsb[1 - p], 16)
                    if keys:
                        sp.wait_ge(s_mf, n0 + 4)
                        sp_keys_out(sp, j, u + 2, 0)
                        sp.wait_ge(s_mf, n0 + 6)
                        sp_keys_out(sp, j, u + 2, 1)
                        sp.wait_ge(s_kw[0][p], 16 * (j + 2))
                        sp_stack0(sp, j, u + 2, 0)
                    if nxt:
                        sp.wait_ge(s_mf, n1 + 1)
                        sp.dma_start(QS[1 - p][KROWS:KROWS + 1, :, :], nm[1 - p][:, :]).then_inc(s_nm[1 - p], 16)
                    if keys:
                        sp.wait_ge(s_std, 16 * (2 * j + u + 1))
                        sp_stack0(sp, j, u + 2, 1)
                    if nxt:
                        sp.wait_ge(s_mf, n1 + 4)
                        sp.dma_start(v1_dram[bass.ds(2 * j + u + 1, 1)].rearrange("b p n -> (b p) n"),
                                     V1s[1 - p][:, :, :, :].rearrange("p c h v -> p (c h v)")).then_inc(s_v1w[1 - p], 16)

                with sp.Fori(0, B // 2 - 1) as j:
                    for u in range(2):
                        round0(j, u, True, True)
                round0(B // 2 - 1, 0, False, True)
                for p in range(2):
                    for l in range(2):
                        sp.wait_ge(s_kw[l][p], 16 * B // 2)
                    sp.wait_ge(s_v1w[p], 16 * B // 2)

            @block.gpsimd
            def _(pool):
                nc.gpsimd.memset(xr[:, FULL, :], 0.0).then_inc(s_pad, 1)
                nc.gpsimd.memset(ident[:, :], 0.0)
                nc.gpsimd.memset(bigid[:, :], 0.0)
                nc.gpsimd.memset(maskv[:, :], 0.0)
                nc.gpsimd.memset(mhalf[:, :], -0.5)
                nc.gpsimd.memset(ones[:, :], 1.0)
                nc.gpsimd.memset(ctxb[:, :], CTX_BIAS)
                nc.gpsimd.memset(magic[:, 0:1], MAGIC)
                nc.gpsimd.memset(magic[:, 1:2], -MAGIC).then_inc(s_const, 1)
                pool.wait_ge(s_const, 1)
                nc.gpsimd.affine_select(out=ident[:, :], in_=ident[:, :], compare_op=ALU.not_equal, fill=1.0,
                                        base=0, pattern=[[-1, P]], channel_multiplier=1).then_inc(s_const, 1)
                nc.gpsimd.affine_select(out=bigid[:, :], in_=bigid[:, :], compare_op=ALU.not_equal, fill=BIG,
                                        base=0, pattern=[[-1, T]], channel_multiplier=1).then_inc(s_const, 1)
                nc.gpsimd.affine_select(out=maskv[:, 0:T], in_=maskv[:, 0:T], compare_op=ALU.is_ge, fill=-BIG,
                                        base=0, pattern=[[-1, T]], channel_multiplier=1).then_inc(s_const, 1)
                nc.gpsimd.affine_select(out=maskv[:, T:2 * T], in_=maskv[:, T:2 * T], compare_op=ALU.not_equal,
                                        fill=-BIG, base=0, pattern=[[-1, T]], channel_multiplier=1
                                        ).then_inc(s_const, 1)
                pool_rstd(pool, 0)
                for p in range(2):
                    nc.gpsimd.memset(Vc[p][:, :, :, :], 0.0)
                    last = nc.gpsimd.memset(VSB[p][:, :, :], 0.0)
                last.then_inc(s_zero, 1)

                def masks(j, u):
                    for g in range(H // HG):
                        hs = slice(g * HG, (g + 1) * HG)
                        pool.wait_ge(s_exp, 16 * (2 * j + u) + 4 * g + 2)
                        pool.sem_inc(s_mb, 1)
                        nc.gpsimd.affine_select(out=PT[0:T, 0, hs, :], in_=PT[0:T, 0, hs, :], compare_op=ALU.is_ge,
                                                fill=0.0, base=0, pattern=[[0, HG], [1, T]], channel_multiplier=-1)
                        nc.gpsimd.affine_select(out=PT[0:T, 1, hs, :], in_=PT[0:T, 1, hs, :],
                                                compare_op=ALU.not_equal, fill=0.0, base=0,
                                                pattern=[[0, HG], [-1, T]], channel_multiplier=1).then_inc(s_msk, 1)

                with pool.Fori(0, B // 2) as j:
                    for u in range(2):
                        masks(j, u)

            @block.scalar
            def _(act):
                for k, (dst, src) in enumerate((
                        (gts[:, 0:2], g_xattn.partition_broadcast(P)), (gts[:, 2:4], g_ffn.partition_broadcast(P)),
                        (clips[:, 0:1], clip_x.partition_broadcast(P)), (clips[:, 1:2], clip_down.partition_broadcast(P)),
                        (bcol[:, 0, :], b_attn[0:D].rearrange("(k p) -> p k", p=P)),
                        (bcol[:, 1, :], b_attn[D:2 * D].rearrange("(k p) -> p k", p=P)),
                        (bcol[:, 2, :], b_ref[0:D].rearrange("(k p) -> p k", p=P)),
                        (bcol[:, 3, :], b_k.rearrange("(k p) -> p k", p=P)),
                        (bcol[:, 4, :], b_q.rearrange("(k p) -> p k", p=P)),
                        (brow[:, 0, :], b_attn[2 * D:3 * D].partition_broadcast(P)),
                        (brow[:, 1, :], b_ref[D:2 * D].partition_broadcast(P)),
                        (brow[:, 2, :], b_v.partition_broadcast(P)),
                        (bpr[:, 0, :], b_proj.partition_broadcast(P)), (bpr[:, 1, :], b_o.partition_broadcast(P)),
                        (gbr[:, :], gate_b.partition_broadcast(P)),
                        (b1c[:, :, :], b1.rearrange("e (p f) -> p e f", p=P)), (b2r[:, :], b2),
                        (gwr[:, :, :], gate_w.rearrange("(k p) e -> p k e", p=P)))):
                    act.dma_start(dst, src, allow_slow_non_contiguous=4 <= k <= 8).then_inc(s_bias, 16)
                act.wait_ge(s_bias, 16 * 18)
                nc.scalar.activation(tg[:, :], gts[:, :], ACT.Tanh)
                nc.scalar.activation(clipt[:, :], clips[:, :], ACT.Tanh, scale=0.5).then_inc(s_tanh, 1)
                act.wait_ge(s_wr[0], 16)
                nc.scalar.activation(wah[:, :, :], r_attn, ACT.Copy, scale=WS).then_inc(s_wh8, 1)
                for kc in range(KC):
                    wide_hi(act, kc, xTh[:, kc, :])
                act.wait_ge(s_wr[1], 32)
                nc.scalar.activation(wrh[:, :, :], r_ref[:, :, 0:D], ACT.Copy, scale=WS)
                nc.scalar.activation(wvh[:, :, 0, :], r_ref[:, :, D:2 * D], ACT.Copy, scale=WS)
                nc.scalar.activation(wph[:, 0, :, :], r_proj, ACT.Copy, scale=WS)
                nc.scalar.activation(gwh[:, :, :], gwr[:, :, :], ACT.Copy, scale=WS).then_inc(s_wh8, 1)
                act.wait_ge(s_biasp, 1)
                for mb in range(KC):
                    wide_hi(act, 2 + mb, qh[:, mb, :], bcol[:, 0, mb:mb + 1])
                for mb in range(KC):
                    wide_hi(act, 4 + mb, skh[:, mb, :], bcol[:, 1, mb:mb + 1])
                for n, dsts in ((8, (w1kh[:, 0], wvh[:, :, 1])), (9, (w1kh[:, 1], wph[:, 1]))):
                    act.wait_ge(s_wd, n + 1)
                    for i, dst in enumerate(dsts):
                        last = nc.scalar.activation(dst, wide[n % 4][:, 512 * i:512 * i + 512].rearrange(
                            "p (k n) -> p k n", k=KC), ACT.Copy, scale=WS)
                    last.then_inc(s_wh, 1)

                for o in range(2):
                    for kc in range(KC):
                        act_hi_T(act, 0, o, kc, 6 * o + kc)
                    for k in range(4):
                        act_hi_K(act, 0, o, k, 6 * o + 2 + k)

                act.wait_ge(s_wf, 10)
                act.wait_ge(s_split, 1)

                def round0(j, u, keys):
                    n0 = 16 + 10 * (2 * j + u)
                    for t in range(16):
                        act_exp(act, j, u, t, 0, 0)
                        if keys and t in TKS:
                            k = TKS[t]
                            if k < 2:
                                act_hi_T(act, j, u + 2, k, n0 + k)
                            else:
                                act_hi_K(act, j, u + 2, k - 2, n0 + k)
                    act_evac(act, j, u, 0)

                with act.Fori(0, B // 2 - 1) as j:
                    for u in range(2):
                        round0(j, u, True)
                for u in range(2):
                    round0(B // 2 - 1, u, False)

            @block.tensor
            def _(pe):
                pe.wait_ge(s_const, 5)
                pe.wait_ge(s_xn, NTILE)
                for kc in range(KC):
                    transpose_rows(pe, kc, kc)
                pe.wait_ge(s_split, 1)
                pe.wait_ge(s_wf, 2)
                for mb in range(KC):
                    project_T(pe, 2 + mb, wah, wal, mb)
                for mb in range(KC):
                    pe.wait_ge(s_wf, 4 + mb - 3)
                    project_T(pe, 4 + mb, wah, wal, KC + mb)
                for n in range(2):
                    pe.wait_ge(s_wf, 6 + n - 3)
                    for i in range(4):
                        b = 4 * n + i
                        for kc in range(KC):
                            last = split3(pe, wide[(6 + n) % 4][0:T, i * D:(i + 1) * D],
                                          xTh[:, kc, b * T:(b + 1) * T], xTl[:, kc, b * T:(b + 1) * T],
                                          wah[:, kc, 2 * D:3 * D], wal[:, kc, 2 * D:3 * D], kc == 0, kc == KC - 1)
                    last.then_inc(s_wd, 1)
                pe.wait_ge(s_wr[2], 64)
                for n in range(2):
                    pe.wait_ge(s_wf, 8 + n - 3)
                    for i in range(2):
                        for kc in range(KC):
                            for ob in range(KC):
                                o0 = 512 * i + kc * D + ob * P
                                last = nc.tensor.transpose(wide[(8 + n) % 4][:, o0:o0 + P],
                                                           r_l1[2 * n + i][:, ob, kc * P:(kc + 1) * P], ident[:, :])
                    last.then_inc(s_wd, 1)
                pe.wait_ge(s_wf, 10)
                for o in range(2):
                    n0 = 6 * o
                    for kc in range(KC):
                        pe_T(pe, 0, o, kc, n0 + kc)
                    for k in range(4):
                        pe_K(pe, 0, o, k, n0 + 2 + k, n0 + 1)
                for c in range(3):
                    pe_V(pe, 0, 0, c, 12 + c)
                for h in range(H):
                    pe_SM(pe, 0, 0, h, 0, 0)
                pe_N(pe, 0, 0, 0, 15, 15)
                pe.wait_ge(s_mf, 16)

                def round0(j, u, keys, nxt):
                    n0 = 16 + 10 * (2 * j + u)
                    h = 0
                    for t in range(16):
                        if t == 4:
                            pe.wait_ge(s_vsb[u], 16 * (j + 1))
                        pe_ST(pe, j, u, t, 0, 0, 0)
                        if keys and t in TKS:
                            k = TKS[t]
                            if k < 2:
                                pe_T(pe, j, u + 2, k, n0 + k)
                            else:
                                pe_K(pe, j, u + 2, k - 2, n0 + k, n0 + 1)
                        if nxt:
                            for _ in range(SMH[t]):
                                pe_SM(pe, j, u + 1, h, 0, 0)
                                h += 1
                        if t >= 4:
                            pe_PV(pe, j, u, t - 4, 0, 0, 0, 0)
                        if nxt and t == NSTEP:
                            n1 = n0 + (UN if keys else 0)
                            pe_N(pe, j, u + 1, 0, n1, n1 - 1)
                    for i in range(4):
                        pe_PV(pe, j, u, 12 + i, 0, 0, 0, 0)
                        if nxt and i == 0:
                            pe_V(pe, j, u + 1, 0, n1 + 1)
                    if nxt:
                        for c in (1, 2):
                            pe_V(pe, j, u + 1, c, n1 + 1 + c)
                    pe_turn(pe, j, u, 0)

                with pe.Fori(0, B // 2 - 1) as j:
                    for u in range(2):
                        round0(j, u, True, True)
                round0(B // 2 - 1, 0, False, True)
                round0(B // 2 - 1, 1, False, False)

            @block.vector
            def _(dve):
                dve.wait_ge(s_x, 32)
                layernorm_stats(dve)
                layernorm_rows(dve, 0)
                dve.wait_ge(s_wh8, 1)
                nc.vector.scalar_tensor_tensor(out=wal[:, :, :], in0=r_attn, scalar=WS, in1=wah[:, :, :],
                                               op0=ALU.mult, op1=ALU.subtract)
                for kc in range(KC):
                    wide_lo(dve, kc, xTh[:, kc, :], xTl[:, kc, :])
                dve.wait_ge(s_wh8, 2)
                for dst, src, hi in ((wrl[:, :, :], r_ref[:, :, 0:D], wrh[:, :, :]),
                                     (wvl[:, :, 0, :], r_ref[:, :, D:2 * D], wvh[:, :, 0, :]),
                                     (wpl[:, 0, :, :], r_proj, wph[:, 0, :, :]),
                                     (gwl[:, :, :], gwr[:, :, :], gwh[:, :, :])):
                    last = nc.vector.scalar_tensor_tensor(out=dst, in0=src, scalar=WS, in1=hi, op0=ALU.mult,
                                                          op1=ALU.subtract)
                last.then_inc(s_split, 1)
                dve.wait_ge(s_tanh, 1)
                nc.vector.tensor_scalar(tgs[:, :], tg[:, :], 1.0 / WS, None, ALU.mult)
                nc.vector.tensor_scalar(clipt[:, :], clipt[:, :], 1.0, 0.5 / QMAX, ALU.add, ALU.mult)
                nc.vector.tensor_scalar(b1c[:, :, :], b1c[:, :, :], WS, None, ALU.mult)
                nc.vector.tensor_scalar(brow[:, :, :], brow[:, :, :], WS, None, ALU.mult)
                nc.vector.tensor_scalar(bcol[:, :, :], bcol[:, :, :], WS, None, ALU.mult).then_inc(s_biasp, 1)
                for p in range(2):
                    nc.vector.memset(KS[p][KROWS:KROWS + 1, :, :], WS * WS)
                    nc.vector.memset(V1s[p][:, :, :, DH:VW], WS)
                nc.vector.memset(Vs[:, :, :, DH:VW], WS)
                dve.wait_ge(s_zero, 1)
                for p in range(2):
                    nc.vector.memset(Vc[p][:, :, :, DH:VW], WS)
                dve.wait_ge(s_biasp, 1)
                for mb in range(KC):
                    wide_lo(dve, 2 + mb, qh[:, mb, :], ql[:, mb, :], bcol[:, 0, mb:mb + 1])
                for mb in range(KC):
                    wide_lo(dve, 4 + mb, skh[:, mb, :], skl[:, mb, :], bcol[:, 1, mb:mb + 1])
                for n in range(2):
                    dve.wait_ge(s_wd, 6 + n + 1)
                    for i in range(4):
                        last = nc.vector.tensor_tensor(
                            Vs[:, 4 * n + i, :, 0:DH],
                            wide[(6 + n) % 4][0:T, i * D:(i + 1) * D].rearrange("p (h d) -> p h d", h=H),
                            brow[0:T, 0, :].rearrange("p (h d) -> p h d", h=H), ALU.add)
                    last.then_inc(s_wf, 1)
                for n, dsts in ((8, ((w1kh[:, 0], w1kl[:, 0]), (wvh[:, :, 1], wvl[:, :, 1]))),
                                (9, ((w1kh[:, 1], w1kl[:, 1]), (wph[:, 1], wpl[:, 1])))):
                    dve.wait_ge(s_wh, n + 1 - 2)
                    for i, (hi, lo) in enumerate(dsts):
                        last = nc.vector.scalar_tensor_tensor(
                            out=lo, in0=wide[n % 4][:, 512 * i:512 * i + 512].rearrange("p (k n) -> p k n", k=KC),
                            scalar=WS, in1=hi, op0=ALU.mult, op1=ALU.subtract)
                    last.then_inc(s_wf, 1)
                for o in range(2):
                    for kc in range(KC):
                        dve_lo_T(dve, 0, o, kc, 6 * o + kc, 6 * o + kc)
                    for k in range(4):
                        dve_lo_K(dve, 0, o, k, 6 * o + 2 + k, 6 * o + 2 + k)
                for c in range(3):
                    dve_V(dve, 0, 0, c, 12 + c)
                for h in range(H):
                    dve_max(dve, 0, 0, h, 0, 0)
                dve_N(dve, 0, 0, 15)

                def round0(j, u, keys, nxt):
                    i = 2 * j + u
                    n0 = 16 + 10 * i
                    nh0 = 12 + 6 * i
                    h = 0
                    for t in range(16):
                        if keys and t in TKS:
                            k = TKS[t]
                            if k == 2 and not (isinstance(j, int) and i < 2):
                                pass
                            if k < 2:
                                dve_lo_T(dve, j, u + 2, k, n0 + k, nh0 + k)
                            else:
                                dve_lo_K(dve, j, u + 2, k - 2, n0 + k, nh0 + k)
                        if nxt:
                            for _ in range(SMH[t]):
                                dve_max(dve, j, u + 1, h, 0, 0)
                                h += 1
                        if nxt and t == NSTEP:
                            n1 = n0 + (UN if keys else 0)
                            dve_N(dve, j, u + 1, n1)
                    if nxt:
                        for c in range(3):
                            dve_V(dve, j, u + 1, c, n1 + 1 + c)
                    dve_norm(dve, j, u, 0)

                with dve.Fori(0, B // 2 - 1) as j:
                    for u in range(2):
                        round0(j, u, True, True)
                round0(B // 2 - 1, 0, False, True)
                round0(B // 2 - 1, 1, False, False)

        PLAN = (["a0", "a1", "p0", "p1", "g0", "g1", "u0", "u1", "d0", "d1", "sd", "xm", "xb", "x0", "x1"]
                + [f"{m}{ib}" for ib in range(NIB) for m in ("gate", "up")]
                + ["hm", "hb", "y0", "y1", "q_x0", "q_x1", "q0", "q1",
                   "o_a0", "o_a1", "o_p0", "o_p1", "m_x0", "m_x1", "rt", "ct", "b0", "b1"])
        U = {name: 10 + k for k, name in enumerate(PLAN)}
        HALVES = ["a0", "a1", "q_x0", "q_x1", "q0", "q1", "o_a0", "o_a1", "m_x0", "m_x1"]
        UH = {name: 8 + k for k, name in enumerate(HALVES)}

        def W(name):
            return wide[U[name] % 4]

        def pe_free(pe, name):
            pe.wait_ge(s_wf, U[name] - 3)

        def pe_attT(pe, kc, name):
            pe_free(pe, name)
            for b in range(B):
                o0 = 512 * (b // 4) + (b % 4) * T
                last = nc.tensor.transpose(W(name)[:, o0:o0 + T], aall[:, b, kc * P:(kc + 1) * P], ident[0:T, 0:T])
            last.then_inc(s_wd, 1)

        def act_attT(act, kc, name):
            act.wait_ge(s_wd, U[name] + 1)
            src = W(name).rearrange("p (a n) -> p a n", a=2)[:, :, 0:4 * T]
            nc.scalar.activation(aTh[:, kc, :].rearrange("p (a n) -> p a n", a=2), src, ACT.Copy).then_inc(s_wh, 1)

        def dve_attT(dve, kc, name):
            dve.wait_ge(s_wh, UH[name] + 1)
            src = W(name).rearrange("p (a n) -> p a n", a=2)[:, :, 0:4 * T]
            nc.vector.tensor_tensor(aTl[:, kc, :].rearrange("p (a n) -> p a n", a=2), src,
                                    aTh[:, kc, :].rearrange("p (a n) -> p a n", a=2), ALU.subtract).then_inc(s_wf, 1)

        def pe_out_proj(pe, l, names):
            for t, (t0, tn) in enumerate(TT):
                if t % 4 == 0:
                    pe_free(pe, names[t // 4])
                o0 = (t % 4) * D
                for kc in range(KC):
                    last = split3(pe, W(names[t // 4])[0:tn, o0:o0 + D], aTh[:, kc, t0:t0 + tn],
                                  aTl[:, kc, t0:t0 + tn], wph[:, l, kc, :], wpl[:, l, kc, :], kc == 0, kc == KC - 1)
                if t % 4 == 3 or t == FULL:
                    last.then_inc(s_wd, 1)

        def tile_groups(name0, name1):
            return [(name0, P, 0, 4), (name1, P, 4, FULL), (name1, LAST, FULL, NTILE)]

        def dve_bias_in(dve, l):
            nc.vector.tensor_scalar(bpr[:, l, :], bpr[:, l, :], tg[:, l:l + 1], None, ALU.mult).then_inc(s_dve, 1)
            step[0] += 1
            dve.wait_ge(s_dve, step[0])
            nc.vector.tensor_tensor(xr[:, :, :], xr[:, :, :], bpr[:, l:l + 1, :].to_broadcast([P, NTILE, D]),
                                    ALU.add).then_inc(s_dve, 1)
            step[0] += 1
            dve.wait_ge(s_dve, step[0])

        def dve_residual(dve, names, scalar):
            for name, rows, t0, t1 in tile_groups(*names):
                dve.wait_ge(s_wd, U[name] + 1)
                o0 = (t0 % 4) * D
                ins = nc.vector.scalar_tensor_tensor(
                    out=xr[0:rows, t0:t1, :], in0=W(name)[0:rows, o0:o0 + (t1 - t0) * D].rearrange(
                        "p (t d) -> p t d", d=D), scalar=scalar[0:rows, :], in1=xr[0:rows, t0:t1, :],
                    op0=ALU.mult, op1=ALU.add)
                if t1 in (4, NTILE):
                    ins.then_inc(s_wf, 1)
                    dve.wait_ge(s_wf, U[name] + 1)
                else:
                    ins.then_inc(s_dve, 1)
                    step[0] += 1
                    dve.wait_ge(s_dve, step[0])

        def pe_max_bcast(pe, nm_, nb_, k):
            pe.wait_ge(s_am, k)
            pe_free(pe, nm_)
            nc.tensor.transpose(W(nm_)[0:1, 0:P], small[:, 2:3], ident[:, :]).then_inc(s_wd, 1)
            pe.wait_ge(s_wf, U[nm_] + 1)
            nc.tensor.matmul(W(nb_)[:, 0:1], ones[0:1, :], row1[:, :], start=True, stop=True).then_inc(s_wd, 1)

        def dve_max_bcast(dve, nm_, nb_, clip, col):
            dve.wait_ge(s_wd, U[nm_] + 1)
            nc.vector.tensor_reduce(row1[:, :], W(nm_)[0:1, 0:P], X, ALU.max).then_inc(s_wf, 1)
            dve.wait_ge(s_wd, U[nb_] + 1)
            nc.vector.tensor_scalar(small[:, col:col + 1], W(nb_)[:, 0:1], clip, None, ALU.mult).then_inc(s_wf, 1)
            dve.wait_ge(s_wf, U[nb_] + 1)
            nc.vector.reciprocal(small[:, col + 1:col + 2], small[:, col:col + 1]).then_inc(s_dve, 1)
            step[0] += 1
            dve.wait_ge(s_dve, step[0])


        es_a.close()
        es_f = es_att.enter_context(ExitStack())
        rg = sb("rg", [P, NIB, D], F32, es_f)
        ru = sb("ru", [P, NIB, D], F32, es_f)
        rd_ = sb("rd_", [P, KC, NI], F32, es_f)
        wgT = sb("wgT", [P, KC, NI], F16, es_f)
        wuT = sb("wuT", [P, KC, NI], F16, es_f)
        wdT = sb("wdT", [P, NIB, D], F16, es_f)
        wm = sb("wm", [P, 2 * NIB + KC], F32, es_f)
        winv = sb("winv", [P, 2 * NIB + KC], F32, es_f)
        dgd = sb("dgd", [P, KC, P], F32, es_f)
        sdb = sb("sdb", [P, D], F32, es_f)
        th = [sb(f"th{k}", [P, NT], F32, es_f) for k in range(2)]
        hid = PTf[:, 0:3, :].rearrange("p c n -> p (c n)")[:, 0:NIB * NT].rearrange("p (i n) -> p i n", i=NIB)
        hq = sb("hq", [P, NIB, NT], F16, es_f)
        fac = sb("fac", [P, 4, NIB], F32, es_f)
        hmx = sb("hmx", [P, NIB], F32, es_f)
        s_fw = sem("block_weights_loaded")
        s_fs = sem("block_weight_scales_made")
        s_fq = sem("block_weights_rounded")
        s_am = sem("row_maxima_taken")
        s_sc = sem("scale_made")
        s_th = sem("tanh_made")
        s_hq = sem("hidden_rounded")
        s_hz = sem("hidden_in_fp16")
        s_xq = sem("rows_rounded")

        with nc.Block() as block:

            @block.sync
            def _(sp):
                FI = (NIB - 1) * P
                for dst, src in ((rg, w_gate), (ru, w_up)):
                    sp.dma_start(dst[:, 0:NIB - 1, :], src[0:FI, :].rearrange("(i p) d -> p i d", p=P)).then_inc(s_fw, 16)
                    sp.dma_start(dst[0:LASTI, NIB - 1, :], src[FI:NI, :]).then_inc(s_fw, 16)
                sp.dma_start(rd_[:, :, :], w_down.rearrange("(k p) n -> p k n", p=P)).then_inc(s_fw, 16)

            @block.gpsimd
            def _(pool):
                pool_rstd(pool, 1)

            @block.scalar
            def _(act):
                for kc in range(KC):
                    act_attT(act, kc, f"a{kc}")
                act.wait_ge(s_fs, 1)
                for r, base in ((rg, 0), (ru, NIB)):
                    for ib in range(NIB):
                        n = P if ib < NIB - 1 else LASTI
                        nc.scalar.activation(r[0:n, ib, :], r[0:n, ib, :], ACT.Identity, bias=magic[0:n, 0:1],
                                             scale=winv[0:n, base + ib:base + ib + 1]).then_inc(s_fq, 1)
                for k in range(KC):
                    nc.scalar.activation(rd_[:, k, :], rd_[:, k, :], ACT.Identity, bias=magic[:, 0:1],
                                         scale=winv[:, 2 * NIB + k:2 * NIB + k + 1]).then_inc(s_fq, 1)
                act.wait_ge(s_sc, 1)
                for ib in range(NIB):
                    n = P if ib < NIB - 1 else LASTI
                    act.wait_ge(s_wd, U[f"gate{ib}"] + 1)
                    if ib >= 2:
                        act.wait_ge(s_wf, U[f"up{ib - 2}"] + 1)
                    nc.scalar.activation(th[ib % 2][0:n, :], W(f"gate{ib}")[0:n, 0:NT], ACT.Tanh,
                                         scale=fac[0:n, 0, ib:ib + 1]).then_inc(s_th, 1)
                for ib in range(NIB):
                    n = P if ib < NIB - 1 else LASTI
                    act.wait_ge(s_hq, ib + 1)
                    nc.scalar.activation(hq[0:n, ib, :], hid[0:n, ib, :], ACT.Identity, bias=magic[0:n, 1:2]
                                         ).then_inc(s_hz, 1)

            @block.tensor
            def _(pe):
                for kc in range(KC):
                    pe_attT(pe, kc, f"a{kc}")
                pe.wait_ge(s_wf, U["a1"] + 1)
                pe_out_proj(pe, 0, ("p0", "p1"))
                for m, r, base in (("g", rg, 0), ("u", ru, NIB)):
                    pe.wait_ge(s_fq, base + NIB)
                    for kc in range(KC):
                        pe_free(pe, f"{m}{kc}")
                        for ib in range(NIB):
                            n = P if ib < NIB - 1 else LASTI
                            last = nc.tensor.transpose(W(f"{m}{kc}")[:, ib * P:ib * P + n],
                                                       r[0:n, ib, kc * P:(kc + 1) * P], ident[0:n, 0:n])
                        last.then_inc(s_wd, 1)
                pe.wait_ge(s_fq, 2 * NIB + KC)
                for ib in range(NIB):
                    n = P if ib < NIB - 1 else LASTI
                    name = f"d{ib // 4}"
                    if ib % 4 == 0:
                        pe_free(pe, name)
                    for k in range(KC):
                        o0 = (ib % 4) * D + k * P
                        last = nc.tensor.transpose(W(name)[0:n, o0:o0 + P], rd_[:, k, ib * P:ib * P + n], ident[:, :])
                    if ib in (3, NIB - 1):
                        last.then_inc(s_wd, 1)
                pe_free(pe, "sd")
                for k in range(KC):
                    last = nc.tensor.matmul(W("sd")[:, k * P:(k + 1) * P], ones[:, :], dgd[:, k, :],
                                            start=True, stop=True)
                last.then_inc(s_wd, 1)
                pe_max_bcast(pe, "xm", "xb", 1)
                pe.wait_ge(s_xq, 1)
                for kc in range(KC):
                    pe_free(pe, f"x{kc}")
                    transpose_rows(pe, U[f"x{kc}"], kc)
                pe.wait_ge(s_wf, U["x1"] + 1)
                for ib in range(NIB):
                    n = P if ib < NIB - 1 else LASTI
                    for m, wt in (("gate", wgT), ("up", wuT)):
                        name = f"{m}{ib}"
                        pe_free(pe, name)
                        for t0, t1 in ((0, WIDE0), (WIDE0, NT)):
                            for kc in range(KC):
                                last = nc.tensor.matmul(W(name)[0:n, t0:t1], wt[:, kc, ib * P:ib * P + n],
                                                        xTh[:, kc, t0:t1], start=(kc == 0), stop=(kc == KC - 1))
                        last.then_inc(s_wd, 1)
                pe_max_bcast(pe, "hm", "hb", 2)
                pe_free(pe, "y1")
                for ib in range(NIB):
                    n = P if ib < NIB - 1 else LASTI
                    pe.wait_ge(s_hz, ib + 1)
                    for t, (t0, tn) in enumerate(TT):
                        last = nc.tensor.matmul(W(f"y{t // 4}")[0:tn, (t % 4) * D:(t % 4 + 1) * D],
                                                hq[0:n, ib, t0:t0 + tn], wdT[0:n, ib, :],
                                                start=(ib == 0 and t % 2 == 0), stop=(ib == NIB - 1),
                                                skip_group_check=True)
                        if ib == NIB - 1 and t in (3, FULL):
                            last.then_inc(s_wd, 1)

            @block.vector
            def _(dve):
                def link(ins):
                    ins.then_inc(s_dve, 1)
                    step[0] += 1
                    dve.wait_ge(s_dve, step[0])

                link(nc.vector.memset(small[:, :], 0.0))
                nc.vector.memset(wm[:, :], 1.0)
                dve_bias_in(dve, 0)
                for kc in range(KC):
                    dve_attT(dve, kc, f"a{kc}")
                dve.wait_ge(s_fw, 16 * 5)
                for r, base in ((rg, 0), (ru, NIB)):
                    nc.vector.tensor_reduce(wm[:, base:base + NIB - 1], r[:, 0:NIB - 1, :], X, ALU.max,
                                            apply_absolute_value=True)
                    nc.vector.tensor_reduce(wm[0:LASTI, base + NIB - 1:base + NIB], r[0:LASTI, NIB - 1:NIB, :], X,
                                            ALU.max, apply_absolute_value=True)
                link(nc.vector.tensor_reduce(wm[:, 2 * NIB:], rd_[:, :, :], X, ALU.max, apply_absolute_value=True))
                link(nc.vector.tensor_scalar(wm[:, :], wm[:, :], 1.0 / QMAX, None, ALU.mult))
                nc.vector.reciprocal(winv[:, :], wm[:, :]).then_inc(s_fs, 1)
                for k in range(KC):
                    nc.vector.tensor_scalar(dgd[:, k, :], ident[:, :], wm[:, 2 * NIB + k:2 * NIB + k + 1], None, ALU.mult)
                dve_residual(dve, ("p0", "p1"), tgs[:, 0:1])
                layernorm_stats(dve)
                layernorm_rows(dve, 1)
                dve.wait_ge(s_xn, 2 * NTILE)
                nc.vector.tensor_reduce(small[:, 2:3], xn[:, :, :], XY, ALU.max, apply_absolute_value=True
                                        ).then_inc(s_am, 1)
                for m, wt in (("g", wgT), ("u", wuT)):
                    for kc in range(KC):
                        dve.wait_ge(s_wd, U[f"{m}{kc}"] + 1)
                        nc.vector.tensor_scalar(wt[:, kc, :], W(f"{m}{kc}")[:, 0:NI], -MAGIC, None, ALU.add
                                                ).then_inc(s_wf, 1)
                dve.wait_ge(s_wd, U["d0"] + 1)
                nc.vector.tensor_scalar(wdT[:, 0:4, :].rearrange("p i d -> p (i d)"), W("d0")[:, 0:4 * D], -MAGIC, None,
                                        ALU.add).then_inc(s_wf, 1)
                dve.wait_ge(s_wd, U["d1"] + 1)
                nc.vector.tensor_scalar(wdT[:, 4, :], W("d1")[:, 0:D], -MAGIC, None, ALU.add)
                nc.vector.tensor_scalar(wdT[0:LASTI, 5, :], W("d1")[0:LASTI, D:2 * D], -MAGIC, None, ALU.add
                                        ).then_inc(s_wf, 1)
                dve.wait_ge(s_wd, U["sd"] + 1)
                nc.vector.tensor_copy(sdb[:, :], W("sd")[:, 0:D]).then_inc(s_wf, 1)
                dve_max_bcast(dve, "xm", "xb", clipt[:, 0:1], 4)
                link(nc.vector.tensor_scalar(xn[:, :, :], xn[:, :, :], small[:, 5:6], MAGIC, ALU.mult, ALU.add))
                nc.vector.tensor_scalar(xn[:, :, :], xn[:, :, :], MAGIC + QMAX, MAGIC - QMAX - 1.0, ALU.min, ALU.max
                                        ).then_inc(s_xq, 1)
                link(nc.vector.tensor_scalar(fac[:, 0, :], wm[:, 0:NIB], small[:, 4:5], 0.5, ALU.mult, ALU.mult))
                nc.vector.tensor_scalar(fac[:, 1, :], wm[:, NIB:2 * NIB], small[:, 4:5], None, ALU.mult).then_inc(s_sc, 1)
                dve.wait_ge(s_sc, 1)
                link(nc.vector.tensor_tensor(fac[:, 2, :], fac[:, 0, :], fac[:, 1, :], ALU.mult))
                for kc in range(KC):
                    dve.wait_ge(s_wd, U[f"x{kc}"] + 1)
                    nc.vector.tensor_scalar(xTh[:, kc, :], W(f"x{kc}")[:, 0:NT], -MAGIC, None, ALU.add).then_inc(s_wf, 1)
                link(nc.vector.memset(hmx[:, :], 0.0))
                for ib in range(NIB):
                    n = P if ib < NIB - 1 else LASTI
                    dve.wait_ge(s_th, ib + 1)
                    nc.vector.scalar_tensor_tensor(out=hid[0:n, ib, :], in0=th[ib % 2][0:n, :], scalar=1.0,
                                                   in1=W(f"gate{ib}")[0:n, 0:NT], op0=ALU.add, op1=ALU.mult
                                                   ).then_inc(s_wf, 1)
                    dve.wait_ge(s_wf, U[f"gate{ib}"] + 1)
                    dve.wait_ge(s_wd, U[f"up{ib}"] + 1)
                    nc.vector.scalar_tensor_tensor(out=hid[0:n, ib, :], in0=hid[0:n, ib, :],
                                                   scalar=fac[0:n, 2, ib:ib + 1], in1=W(f"up{ib}")[0:n, 0:NT],
                                                   op0=ALU.mult, op1=ALU.mult).then_inc(s_wf, 1)
                    dve.wait_ge(s_wf, U[f"up{ib}"] + 1)
                    link(nc.vector.tensor_reduce(hmx[0:n, ib:ib + 1], hid[0:n, ib, :], X, ALU.max,
                                                 apply_absolute_value=True))
                nc.vector.tensor_reduce(small[:, 2:3], hmx[:, :], X, ALU.max).then_inc(s_am, 1)
                dve_max_bcast(dve, "hm", "hb", clipt[:, 1:2], 6)
                for ib in range(NIB):
                    n = P if ib < NIB - 1 else LASTI
                    link(nc.vector.tensor_scalar(hid[0:n, ib, :], hid[0:n, ib, :], small[0:n, 7:8], MAGIC,
                                                 ALU.mult, ALU.add))
                    nc.vector.tensor_scalar(hid[0:n, ib, :], hid[0:n, ib, :], MAGIC + QMAX, MAGIC - QMAX - 1.0,
                                            ALU.min, ALU.max).then_inc(s_hq, 1)
                link(nc.vector.tensor_scalar(sdb[:, :], sdb[:, :], small[:, 6:7], tg[:, 2:3], ALU.mult, ALU.mult))
                for name, rows, t0, t1 in tile_groups("y0", "y1"):
                    dve.wait_ge(s_wd, U[name] + 1)
                    o0 = (t0 % 4) * D
                    ins = nc.vector.tensor_tensor(
                        xn[0:rows, t0:t1, :], W(name)[0:rows, o0:o0 + (t1 - t0) * D].rearrange("p (t d) -> p t d", d=D),
                        sdb[0:rows, :].unsqueeze(1).to_broadcast([rows, t1 - t0, D]), ALU.mult)
                    if t1 in (4, NTILE):
                        ins.then_inc(s_wf, 1)
                        dve.wait_ge(s_wf, U[name] + 1)
                    else:
                        link(ins)
                    link(nc.vector.tensor_tensor(xr[0:rows, t0:t1, :], xr[0:rows, t0:t1, :], xn[0:rows, t0:t1, :],
                                                 ALU.add))

        es_f.close()
        es_m = es_att.enter_context(ExitStack())
        w1r = sb("w1r", [P, KC, DF], F32, es_m)
        w2r = sb("w2r", [P, FC, D], F32, es_m)
        w1h = [sb(f"w1h{p}", [P, KC, FC, P], F16, es_m) for p in range(2)]
        w1l = [sb(f"w1l{p}", [P, KC, FC, P], F16, es_m) for p in range(2)]
        w2h = [sb(f"w2h{p}", [P, FC, D], F16, es_m) for p in range(2)]
        w2l = [sb(f"w2l{p}", [P, FC, D], F16, es_m) for p in range(2)]
        s_w1 = sem("expert_w1_loaded")
        s_w2 = sem("expert_w2_loaded")
        s_w1h = sem("expert_w1_high_half")
        s_w2h = sem("expert_w2_high_half")
        s_w1l = sem("expert_w1_split")
        s_w2l = sem("expert_w2_split")
        SMN, STN, NBN = H * B, 16 * B, B
        MN = 80
        SMH1 = [2, 2, 2, 1, 2, 1, 2, 1, 2, 1, 0, 0]
        NSTEP1 = 11
        PVH1 = [0, 0, 0, 2, 1, 1, 2, 1, 1, 2, 1, 1]
        NST1 = 12
        QB = 16 * 8

        def sp_w1(sp, e):
            sp.dma_start(w1r[:, :, :], w1[bass.ds(e, 1)].rearrange("e (k p) n -> p (e k) n", p=P)).then_inc(s_w1, 16)

        def sp_w2(sp, e):
            sp.dma_start(w2r[:, :, :], w2[bass.ds(e, 1)].rearrange("e (p f) n -> p (e f) n", f=FC)).then_inc(s_w2, 16)

        def act_w1(act, e, p):
            act.wait_ge(s_w1, 16 * (e + 1))
            nc.scalar.activation(w1h[p][:, :, :, :], w1r[:, :, :].rearrange("p k (m c) -> p k c m", c=FC), ACT.Copy,
                                 scale=WS).then_inc(s_w1h, 1)

        def act_w2(act, e, p):
            act.wait_ge(s_w2, 16 * (e + 1))
            nc.scalar.activation(w2h[p][:, :, :].rearrange("p c n -> p (c n)"), w2r[:, :, :].rearrange("p c n -> p (c n)"),
                                 ACT.Copy, scale=WS).then_inc(s_w2h, 1)

        def dve_w1(dve, e, p):
            dve.wait_ge(s_w1h, e + 1)
            for k in range(KC):
                last = nc.vector.scalar_tensor_tensor(
                    out=w1l[p][:, k, :, :], in0=w1r[:, k, :].rearrange("p (m c) -> p c m", c=FC), scalar=WS,
                    in1=w1h[p][:, k, :, :], op0=ALU.mult, op1=ALU.subtract)
            last.then_inc(s_w1l, 1)

        def dve_w2(dve, e, p):
            dve.wait_ge(s_w2h, e + 1)
            nc.vector.scalar_tensor_tensor(out=w2l[p][:, :, :].rearrange("p c n -> p (c n)"),
                                           in0=w2r[:, :, :].rearrange("p c n -> p (c n)"), scalar=WS,
                                           in1=w2h[p][:, :, :].rearrange("p c n -> p (c n)"), op0=ALU.mult,
                                           op1=ALU.subtract).then_inc(s_w2l, 1)

        with nc.Block() as block:

            @block.sync
            def _(sp):
                sp_w1(sp, 0)
                sp_w2(sp, 0)
                sp.dma_start(Vc[0][:, :, :, 0:VW].rearrange("p c h v -> p (c h) v"),
                             v1_dram[0].rearrange("p (n v) -> p n v", v=VW)).then_inc(s_vc[0], 16)
                for mb in range(KC):
                    sp.wait_ge(s_wf, U[f"q{mb}"] + 1)
                    for k, src in enumerate((qh, ql)):
                        sp.dma_start(q_dram[k, mb], src[:, mb, :]).then_inc(s_qw, 16)
                sp.wait_ge(s_qw, QB + 16 * 4)
                for o in range(2):
                    for mb in range(KC):
                        sp_stack1(sp, 0, o, mb)
                sp.wait_ge(s_w1l, 1)
                sp_w1(sp, 1)
                sp.wait_ge(s_mf, MN + 1)
                sp.dma_start(QS[0][KROWS:KROWS + 1, :, :], nm[0][:, :]).then_inc(s_nm[0], 16)

                def round1(j, u, keys, nxt):
                    p = u % 2
                    i = 2 * j + u
                    if nxt:
                        sp.wait_ge(s_std, STN + NST1 * i + 6)
                        sp.dma_start(Vc[1 - p][:, :, :, 0:VW].rearrange("p c h v -> p (c h) v"),
                                     v1_dram[bass.ds(i + 1, 1)].rearrange("b p (n v) -> (b p) n v", v=VW)
                                     ).then_inc(s_vc[1 - p], 16)
                    if keys:
                        sp_stack1(sp, j, u + 2, 0)
                    if nxt:
                        sp.wait_ge(s_mf, MN + i + 2)
                        sp.dma_start(QS[1 - p][KROWS:KROWS + 1, :, :], nm[1 - p][:, :]).then_inc(s_nm[1 - p], 16)
                    if keys:
                        sp.wait_ge(s_std, STN + NST1 * (i + 1))
                        sp_stack1(sp, j, u + 2, 1)

                with sp.Fori(0, B // 2 - 1) as j:
                    for u in range(2):
                        round1(j, u, True, True)
                round1(B // 2 - 1, 0, False, True)

            @block.gpsimd
            def _(pool):
                pool_rstd(pool, 2)

            @block.scalar
            def _(act):
                for kc in range(KC):
                    wide_hi(act, U[f"q_x{kc}"], xTh[:, kc, :])
                for mb in range(KC):
                    wide_hi(act, U[f"q{mb}"], qh[:, mb, :], bcol[:, 4, mb:mb + 1])
                act_w1(act, 0, 0)
                act_w2(act, 0, 0)

                def round1(j, o, first):
                    for t in range(NST1):
                        act_exp(act, j, o, t, 1, STN)
                    act_evac(act, j, o, NBN)

                round1(0, 0, True)
                with act.Fori(0, B // 2 - 1) as j:
                    for o in (1, 2):
                        round1(j, o, False)
                round1(B // 2 - 1, 1, False)
                act_w1(act, 1, 1)

            @block.tensor
            def _(pe):
                pe.wait_ge(s_xn, 3 * NTILE)
                for kc in range(KC):
                    pe_free(pe, f"q_x{kc}")
                    transpose_rows(pe, U[f"q_x{kc}"], kc)
                pe.wait_ge(s_wf, U["q_x1"] + 1)
                for mb in range(KC):
                    pe_free(pe, f"q{mb}")
                    project_T(pe, U[f"q{mb}"], w1kh[:, 1], w1kl[:, 1], mb)
                pe.wait_ge(s_wf, U["q1"] + 1)
                for h in range(H):
                    pe_SM(pe, 0, 0, h, 1, SMN)
                pe_N(pe, 0, 0, SMN, MN, MN)

                def round1(j, o, first, nxt):
                    i = 2 * j + o
                    h = hv = 0
                    for t in range(NST1):
                        pe_ST(pe, j, o, t, 1, STN, 16 * (B // 2))
                        if t == 1 and not first:
                            pe_turn(pe, j, o - 1, NBN)
                        if nxt:
                            for _ in range(SMH1[t]):
                                pe_SM(pe, j, o + 1, h, 1, SMN)
                                h += 1
                            if t == NSTEP1:
                                pe_N(pe, j, o + 1, SMN, MN + i + 1, MN + i + 1)
                        for _ in range(PVH1[t]):
                            pe_PV(pe, j, o, hv, 1, STN, 0, NBN)
                            hv += 1
                    for _ in range(H - hv):
                        pe_PV(pe, j, o, hv, 1, STN, 0, NBN)
                        hv += 1

                round1(0, 0, True, True)
                with pe.Fori(0, B // 2 - 1) as j:
                    for o in (1, 2):
                        round1(j, o, False, True)
                round1(B // 2 - 1, 1, False, False)
                pe_turn(pe, B // 2 - 1, 1, NBN)

            @block.vector
            def _(dve):
                layernorm_stats(dve)
                layernorm_rows(dve, 2)
                for kc in range(KC):
                    wide_lo(dve, U[f"q_x{kc}"], xTh[:, kc, :], xTl[:, kc, :], None, UH[f"q_x{kc}"])
                for mb in range(KC):
                    wide_lo(dve, U[f"q{mb}"], qh[:, mb, :], ql[:, mb, :], bcol[:, 4, mb:mb + 1], UH[f"q{mb}"])
                dve_w1(dve, 0, 0)
                dve_w2(dve, 0, 0)
                for h in range(H):
                    dve_max(dve, 0, 0, h, 1, SMN)
                dve_N(dve, 0, 0, MN)

                def round1(j, o, first, nxt):
                    i = 2 * j + o
                    for h in range(H):
                        if nxt:
                            dve_max(dve, j, o + 1, h, 1, SMN)
                        if h == 1 and not first:
                            dve_norm(dve, j, o - 1, NBN)
                    if nxt:
                        dve_N(dve, j, o + 1, MN + i + 1)

                round1(0, 0, True, True)
                with dve.Fori(0, B // 2 - 1) as j:
                    for o in (1, 2):
                        round1(j, o, False, True)
                round1(B // 2 - 1, 1, False, False)
                dve_norm(dve, B // 2 - 1, 1, NBN)
                dve_w1(dve, 1, 1)

        lg = sb("lg", [P, NTILE, E])
        sc = sb("sc", [P, NTILE, E])
        rk = sb("rk", [P, NTILE, E])
        red = sb("red", [P, NTILE])
        cmp_ = sb("cmp", [P, NTILE, E, E])
        eqq = sb("eqq", [P, NTILE, E, E])
        low = sb("low", [P, E, E])
        cs = sb("cs", [P, NTILE, E])
        cT = sb("cT", [E, NT])
        hA = PTf.rearrange("p c n -> p (c n)").bitcast(F16)
        hB = KSa[:, :, :, :].rearrange("p a h s -> p (a h s)")
        hTh, hTl = ([h_[:, k * FC * NT:(k + 1) * FC * NT].rearrange("p (f n) -> p f n", f=FC) for h_ in (hA, hB)]
                    for k in range(2))
        af = aallw[:, :, :].rearrange("p b d -> p (b d)")
        rr = [af[:, 0:NT], af[:, NT:2 * NT], qh[:, :, :].rearrange("p k n -> p (k n)").bitcast(F32)]
        YR = 4
        YB = 3
        s_ex = sem("logits_through_exp")
        s_lg = sem("logits_ready")
        s_low = sem("order_mask_made")
        s_cb = sem("router_done")
        s_hd = sem("hidden_product_done")
        s_r = sem("hidden_through_relu")
        s_hh = sem("hidden_high_half")
        s_hl = sem("hidden_split")
        s_yd = sem("expert_product_done")
        s_ya = sem("expert_product_added")
        s_acc = sem("residual_ready")

        with nc.Block() as block:

            @block.sync
            def _(sp):
                def round_w(e, first, second):
                    if first:
                        sp.wait_ge(s_w1l, e + 2)
                        sp_w1(sp, e + 2)
                    if second:
                        sp.wait_ge(s_w2l, e + 1)
                        sp_w2(sp, e + 1)

                with sp.Fori(0, E // 2 - 1) as j:
                    for u in range(2):
                        round_w(2 * j + u, True, True)
                round_w(E - 2, False, True)
                for t, (t0, tn) in enumerate(TT):
                    sp.wait_ge(s_ya, YB + NTILE * (E - 1) + t + 1)
                    sp.dma_start(of[t0:t0 + tn, :], xr[0:tn, t, :]).then_inc(s_out, 16)
                sp.wait_ge(s_out, 16 * NTILE)

            @block.gpsimd
            def _(pool):
                nc.gpsimd.memset(low[:, :, :], 1.0).then_inc(s_low, 1)
                pool.wait_ge(s_low, 1)
                nc.gpsimd.affine_select(out=low[:, :, :], in_=low[:, :, :], compare_op=ALU.is_gt, fill=0.0, base=0,
                                        pattern=[[1, E], [-1, E]], channel_multiplier=0).then_inc(s_low, 1)
                pool_rstd(pool, 3)

                def lows(j, u, n0):
                    for f in range(FC):
                        n = n0 + f
                        pool.wait_ge(s_hh, n + 1)
                        nc.gpsimd.tensor_tensor(hTl[u][:, f, :], rr[f % 3][:, :], hTh[u][:, f, :], ALU.subtract
                                                ).then_inc(s_hl, 1)

                with pool.Fori(0, E // 2) as j:
                    for u in range(2):
                        lows(j, u, FC * (2 * j + u))

            @block.scalar
            def _(act):
                for kc in range(KC):
                    act_attT(act, kc, f"o_a{kc}")
                for kc in range(KC):
                    wide_hi(act, U[f"m_x{kc}"], xTh[:, kc, :])
                act.wait_ge(s_lg, 1)
                nc.scalar.activation(sc[:, :, :], lg[:, :, :], ACT.Exp).then_inc(s_ex, 1)

                def highs(e, q, nw1, nw2):
                    for f in range(FC):
                        act.wait_ge(s_r, FC * e + f + 1)
                        nc.scalar.activation(hTh[q][:, f, :], rr[f % 3][:, :], ACT.Copy).then_inc(s_hh, 1)
                        if f == 3 and nw1:
                            act_w1(act, e + 1, 1 - q)
                        if f == 6 and nw2:
                            act_w2(act, e, q)

                highs(0, 0, False, False)
                with act.Fori(0, E // 2 - 1) as j:
                    for u in range(2):
                        highs(2 * j + u + 1, 1 - u, True, True)
                highs(E - 1, 1, False, True)

            @block.tensor
            def _(pe):
                for kc in range(KC):
                    pe_attT(pe, kc, f"o_a{kc}")
                pe.wait_ge(s_wf, U["o_a1"] + 1)
                pe_out_proj(pe, 1, ("o_p0", "o_p1"))
                pe.wait_ge(s_xn, 4 * NTILE)
                for kc in range(KC):
                    pe_free(pe, f"m_x{kc}")
                    transpose_rows(pe, U[f"m_x{kc}"], kc)
                pe.wait_ge(s_wf, U["m_x1"] + 1)
                pe_free(pe, "rt")
                for t, (t0, tn) in enumerate(TT):
                    for kc in range(KC):
                        last = split3(pe, W("rt")[0:tn, t * E:(t + 1) * E], xTh[:, kc, t0:t0 + tn],
                                      xTl[:, kc, t0:t0 + tn], gwh[:, kc, :], gwl[:, kc, :], kc == 0, kc == KC - 1)
                last.then_inc(s_wd, 1)
                pe.wait_ge(s_cb, 1)
                pe_free(pe, "ct")
                for t, (t0, tn) in enumerate(TT):
                    last = nc.tensor.transpose(W("ct")[0:E, t0:t0 + tn], rk[0:tn, t, :], ident[0:tn, 0:tn])
                last.then_inc(s_wd, 1)
                pe.wait_ge(s_wf, U["ct"] + 1)
                for t, (t0, tn) in enumerate(TT):
                    if t % 4 == 0:
                        pe_free(pe, f"b{t // 4}")
                    last = nc.tensor.matmul(W(f"b{t // 4}")[0:tn, (t % 4) * D:(t % 4 + 1) * D], cT[:, t0:t0 + tn],
                                            b2r[:, :], start=True, stop=True)
                    if t in (3, FULL):
                        last.then_inc(s_wd, 1)
                pe.wait_ge(s_wf, U["b1"] + 1)

                def hidden(e, q):
                    pe.wait_ge(s_w1l, e + 1)
                    for f in range(FC):
                        n = FC * e + f
                        if not (isinstance(n, int) and n < 2):
                            pe.wait_ge(s_r, n - 1)
                        for kc in range(KC):
                            for lh, rhs in ((w1h[q], xTh), (w1h[q], xTl), (w1l[q], xTh)):
                                for t0, t1 in ((0, WIDE0), (WIDE0, NT)):
                                    last = nc.tensor.matmul(
                                        wide[f % 2][:, t0:t1], lh[:, kc, f, :], rhs[:, kc, t0:t1],
                                        start=(kc == 0 and lh is w1h[q] and rhs is xTh),
                                        stop=(kc == KC - 1 and lh is w1l[q]))
                        last.then_inc(s_hd, 1)

                def outcome(e, q):
                    pe.wait_ge(s_hl, FC * (e + 1))
                    pe.wait_ge(s_w2l, e + 1)
                    for t, (t0, tn) in enumerate(TT):
                        n = NTILE * e + t
                        pe.wait_ge(s_ya, n - (YR if t >= YR else NTILE - YR) + 1 + YB)
                        bank = PS[0:tn, 4 + t % YR, 0:D]
                        for f in range(FC):
                            last = split3(pe, bank, hTh[q][:, f, t0:t0 + tn], hTl[q][:, f, t0:t0 + tn],
                                          w2h[q][:, f, :], w2l[q][:, f, :], f == 0, f == FC - 1)
                        last.then_inc(s_yd, 1)

                hidden(0, 0)
                with pe.Fori(0, E // 2 - 1) as j:
                    for u in range(2):
                        hidden(2 * j + u + 1, 1 - u)
                        outcome(2 * j + u, u)
                hidden(E - 1, 1)
                outcome(E - 2, 0)
                outcome(E - 1, 1)

            @block.vector
            def _(dve):
                def link(ins):
                    ins.then_inc(s_dve, 1)
                    step[0] += 1
                    dve.wait_ge(s_dve, step[0])

                dve_bias_in(dve, 1)
                for kc in range(KC):
                    dve_attT(dve, kc, f"o_a{kc}")
                dve_residual(dve, ("o_p0", "o_p1"), tgs[:, 1:2])
                layernorm_stats(dve)
                layernorm_rows(dve, 3)
                for kc in range(KC):
                    wide_lo(dve, U[f"m_x{kc}"], xTh[:, kc, :], xTl[:, kc, :], None, UH[f"m_x{kc}"])
                link(nc.vector.memset(lg[:, :, :], 0.0))
                dve.wait_ge(s_wd, U["rt"] + 1)
                for rows, t0, t1 in ((P, 0, FULL), (LAST, FULL, NTILE)):
                    ins = nc.vector.scalar_tensor_tensor(
                        out=lg[0:rows, t0:t1, :], in0=W("rt")[0:rows, t0 * E:t1 * E].rearrange("p (t e) -> p t e", e=E),
                        scalar=1.0 / WS, in1=gbr[0:rows, :].unsqueeze(1).to_broadcast([rows, t1 - t0, E]),
                        op0=ALU.mult, op1=ALU.add)
                ins.then_inc(s_wf, 1)
                dve.wait_ge(s_wf, U["rt"] + 1)
                bc = [P, NTILE, E]
                link(nc.vector.tensor_reduce(red[:, :], lg[:, :, :], X, ALU.max))
                nc.vector.tensor_tensor(lg[:, :, :], lg[:, :, :], red[:, :].unsqueeze(2).to_broadcast(bc),
                                        ALU.subtract).then_inc(s_lg, 1)
                dve.wait_ge(s_ex, 1)
                link(nc.vector.tensor_reduce(red[:, :], sc[:, :, :], X, ALU.add))
                link(nc.vector.reciprocal(red[:, :], red[:, :]))
                link(nc.vector.tensor_tensor(sc[:, :, :], sc[:, :, :], red[:, :].unsqueeze(2).to_broadcast(bc), ALU.mult))
                b4 = [P, NTILE, E, E]
                other, own = sc[:, :, :].unsqueeze(2).to_broadcast(b4), sc[:, :, :].unsqueeze(3).to_broadcast(b4)
                nc.vector.tensor_tensor(cmp_[:, :, :, :], other, own, ALU.is_gt)
                link(nc.vector.tensor_tensor(eqq[:, :, :, :], other, own, ALU.is_equal))
                dve.wait_ge(s_low, 2)
                link(nc.vector.tensor_tensor(eqq[:, :, :, :], eqq[:, :, :, :],
                                             low[:, :, :].unsqueeze(1).to_broadcast(b4), ALU.mult))
                link(nc.vector.tensor_tensor(cmp_[:, :, :, :], cmp_[:, :, :, :], eqq[:, :, :, :], ALU.add))
                link(nc.vector.tensor_reduce(rk[:, :, :], cmp_[:, :, :, :], X, ALU.add))
                link(nc.vector.tensor_scalar(rk[:, :, :], rk[:, :, :], 2.0, None, ALU.is_lt))
                link(nc.vector.tensor_tensor(rk[:, :, :], rk[:, :, :], sc[:, :, :], ALU.mult))
                nc.vector.tensor_scalar(rk[:, :, :], rk[:, :, :], tg[:, 3:4], None, ALU.mult).then_inc(s_cb, 1)
                dve.wait_ge(s_cb, 1)
                nc.vector.tensor_scalar(cs[:, :, :], rk[:, :, :], 1.0 / (WS * WS), None, ALU.mult)
                dve.wait_ge(s_wd, U["ct"] + 1)
                nc.vector.tensor_copy(cT[:, :], W("ct")[0:E, 0:NT]).then_inc(s_wf, 1)
                dve.wait_ge(s_wf, U["ct"] + 1)
                dve_residual(dve, ("b0", "b1"), ones[:, 0:1])
                nc.vector.tensor_copy(small[:, 0:1], small[:, 1:2]).then_inc(s_ya, YB)

                def relus(e, q, nw1, nw2):
                    for f in range(FC):
                        n = FC * e + f
                        dve.wait_ge(s_hd, n + 1)
                        if not (isinstance(n, int) and n < 3):
                            dve.wait_ge(s_hl, n - 1 if f < 2 else n - 2)
                        nc.vector.tensor_scalar(rr[f % 3][:, :], wide[f % 2][:, 0:NT], b1c[:, bass.ds(e, 1), f], 0.0,
                                                ALU.add, ALU.max).then_inc(s_r, 1)
                        if f == 3 and nw1:
                            dve_w1(dve, e + 1, 1 - q)
                        if f == 6 and nw2:
                            dve_w2(dve, e, q)

                def adds(e):
                    for t, (t0, tn) in enumerate(TT):
                        n = NTILE * e + t
                        dve.wait_ge(s_yd, n + 1)
                        nc.vector.scalar_tensor_tensor(out=xr[0:tn, t, :], in0=PS[0:tn, 4 + t % YR, 0:D],
                                                       scalar=cs[0:tn, t, bass.ds(e, 1)], in1=xr[0:tn, t, :],
                                                       op0=ALU.mult, op1=ALU.add).then_inc(s_ya, 1)

                relus(0, 0, False, False)
                with dve.Fori(0, E // 2 - 1) as j:
                    for u in range(2):
                        relus(2 * j + u + 1, 1 - u, True, True)
                        adds(2 * j + u)
                relus(E - 1, 1, False, True)
                adds(E - 2)
                adds(E - 1)


_INS = ['x', 'ctx_1024', 'g_xattn', 'g_ffn', 'L0_xattn_w_ref', 'L0_xattn_b_ref', 'L0_xattn_w_attn',
        'L0_xattn_b_attn', 'L0_xattn_w_proj', 'L0_xattn_b_proj', 'L0_ffn_clip_x', 'L0_ffn_clip_down',
        'L0_ffn_w_gate', 'L0_ffn_w_up', 'L0_ffn_w_down', 'L1_xattn_w_q', 'L1_xattn_b_q', 'L1_xattn_w_k',
        'L1_xattn_b_k', 'L1_xattn_w_v', 'L1_xattn_b_v', 'L1_xattn_w_o', 'L1_xattn_b_o', 'L1_ffn_gate_w',
        'L1_ffn_gate_b', 'L1_ffn_w1', 'L1_ffn_b1', 'L1_ffn_w2', 'L1_ffn_b2']


def kernel(**inputs):
    import numpy as _np
    import concourse.bacc as _bacc
    from concourse import mybir as _mybir
    from concourse.bass_utils import run_bass_kernel_spmd as _run

    nc = _bacc.Bacc("TRN2", target_bir_lowering=False, num_devices=1)
    arrays, args = {}, []
    for name in _INS:
        a = _np.ascontiguousarray(inputs[name])
        arrays[f"in_{name}_dram"] = a
        args.append(nc.dram_tensor(f"in_{name}_dram", a.shape, _mybir.dt.from_np(a.dtype), kind="ExternalInput").ap())
    dt = _mybir.dt.from_np(_np.dtype("float32"))
    args.append(nc.dram_tensor("out_0_dram", inputs["x"].shape, dt, kind="ExternalOutput").ap())
    flamingo(nc, *args)
    r = _run(nc, [arrays], core_ids=[0])
    return r.results[0]["out_0_dram"]
```

```python
from contextlib import ExitStack

import concourse.bass as bass
from concourse import mybir

ALU = mybir.AluOpType
ACT = mybir.ActivationFunctionType
F32 = mybir.dt.float32
F16 = mybir.dt.float16
X = mybir.AxisListType.X
XY = mybir.AxisListType.XY

P = 128
WS = 16.0
MAGIC = 12582912.0
EPS = 1e-5
QMAX = 127.0
BIG = 32768.0


def flamingo(nc, x, ctx_seq, g_xattn, g_ffn,
             w_ref, b_ref, w_attn, b_attn, w_proj, b_proj,
             clip_x, clip_down, w_gate, w_up, w_down,
             w_q, b_q, w_k, b_k, w_v, b_v, w_o, b_o,
             gate_w, gate_b, w1, b1, w2, b2, out):
    B, T, D = x.shape
    TC = ctx_seq.shape[1]
    NT = B * T
    H = 16
    DH = D // H
    KC = D // P
    NTILE = -(-NT // P)
    LAST = NT - (NTILE - 1) * P
    FULL = NTILE - 1
    S0 = T + TC
    NI = w_gate.shape[0]
    NIB = -(-NI // P)
    LASTI = NI - (NIB - 1) * P
    E = w1.shape[0]
    DF = w1.shape[2]
    FC = DF // P
    CH = -(-TC // 3)
    CSZ = [CH, (TC - CH) // 2, (TC - CH) // 2]
    COFF = [0, CSZ[0], CSZ[0] + CSZ[1]]
    KROWS = 4 * DH
    SCALE = DH ** -0.5 / (WS * WS)
    CTX_BIAS = -2.0
    VW = DH + 1
    HM = H // 2
    HG = 4
    GW = HG * VW
    VS = GW + VW
    WIDE0 = 512
    TT = [(t * P, P if t < FULL else LAST) for t in range(NTILE)]
    xf = x.rearrange("b t d -> (b t) d")
    of = out.rearrange("b t d -> (b t) d")

    q_dram = nc.dram_tensor("q_scratch", (H, DH, 4, NT), F16, kind="Internal").ap()
    sk_dram = nc.dram_tensor("own_key_scratch", (H, DH, 4, NT), F16, kind="Internal").ap()
    k_dram = [nc.dram_tensor(f"k{l}_scratch", (B, H, DH, 4, TC), F16, kind="Internal").ap() for l in range(2)]
    v1_dram = nc.dram_tensor("v1_scratch", (B, CH, 3 * H * VW), F32, kind="Internal").ap()

    top = ExitStack()
    with top:
        def sb(name, shape, dt=F32, es=top):
            return es.enter_context(nc.sbuf_tensor(name, shape, dt))

        def sem(name):
            return top.enter_context(nc.semaphore(name))

        PS = top.enter_context(nc.psum_tensor("PS", [P, 8, 512], F32))
        wide = [PS[:, 2 * w:2 * w + 2, :].rearrange("p a n -> p (a n)") for w in range(4)]
        sm_bank = [PS[:, 0, :], PS[:, 1, :]]
        st_bank = [PS[:, 2, :], PS[:, 3, :]]
        pv_bank = [PS[:, 4, :], PS[:, 5, :]]
        misc = [PS[:, 5, :], PS[:, 6, :], PS[:, 7, :]]

        xr = sb("xr", [P, NTILE, D])
        xn = sb("xn", [P, NTILE, D])
        xTh = sb("xTh", [P, KC, NT], F16)
        xTl = sb("xTl", [P, KC, NT], F16)
        ident = sb("ident", [P, P])
        ones = sb("ones", [P, P])
        stats = sb("stats", [P, NTILE, 6])
        mv = sb("mv", [P, NTILE, 2])
        veps = sb("veps", [P, NTILE])
        rstd = sb("rstd", [P, NTILE])
        mhalf = sb("mhalf", [P, NTILE])
        gts = sb("gts", [P, 4])
        tg = sb("tg", [P, 4])
        tgs = sb("tgs", [P, 4])
        clips = sb("clips", [P, 2])
        clipt = sb("clipt", [P, 2])
        bcol = sb("bcol", [P, 5, 2])
        brow = sb("brow", [P, 3, D])
        bpr = sb("bpr", [P, 2, D])
        gbr = sb("gbr", [P, E])
        b1c = sb("b1c", [P, E, FC])
        b2r = sb("b2r", [E, D])
        gwr = sb("gwr", [P, KC, E])
        gwh = sb("gwh", [P, KC, E], F16)
        gwl = sb("gwl", [P, KC, E], F16)
        wph = sb("wph", [P, 2, KC, D], F16)
        wpl = sb("wpl", [P, 2, KC, D], F16)
        w1kh = sb("w1kh", [P, 2, KC, D], F16)
        w1kl = sb("w1kl", [P, 2, KC, D], F16)
        aTh = sb("aTh", [P, KC, NT], F16)
        aTl = sb("aTl", [P, KC, NT], F16)
        magic = sb("magic", [P, 2])
        small = sb("small", [P, 8])
        row1 = sb("row1", [1, 1])

        s_x = sem("x_loaded")
        s_pad = sem("padding_cleared")
        s_bias = sem("biases_loaded")
        s_small = sem("small_inputs_loaded")
        s_biasp = sem("biases_scaled")
        s_wr = [sem(f"raw_weights_loaded{k}") for k in range(4)]
        s_const = sem("constants_made")
        s_zero = sem("values_padding_cleared")
        s_tanh = sem("gates_through_tanh")
        s_dve = sem("vector_step")
        s_var = sem("variances_taken")
        s_rstd = sem("rstd_made")
        s_xn = sem("rows_normalised")
        s_wh8 = sem("raw_weights_high_half")
        s_split = sem("weights_split")
        s_wd = sem("wide_product_done")
        s_wh = sem("wide_high_half_done")
        s_wf = sem("wide_tile_freed")
        s_ctx = [sem(f"context_loaded{p}") for p in range(2)]
        s_md = sem("misc_product_done")
        s_mh = sem("misc_high_half_done")
        s_mf = sem("misc_bank_freed")
        s_smd = sem("score_rows_done")
        s_smf = sem("score_max_taken")
        s_std = sem("score_columns_done")
        s_exp = sem("exponentials_done")
        s_msk = sem("masks_done")
        s_mb = sem("masks_begun")
        s_pvd = sem("head_values_done")
        s_ev = sem("outcome_copied")
        s_tvd = sem("outcome_turned")
        s_rd = sem("denominators_inverted")
        s_nrm = sem("heads_normalised")
        s_ks = [[sem(f"stack_loaded{p}{m}") for m in range(2)] for p in range(2)]
        s_nm = [sem(f"max_row_loaded{p}") for p in range(2)]
        s_kw = [[sem(f"k{l}_written{p}") for p in range(2)] for l in range(2)]
        s_qw = sem("queries_written")
        s_kr = sem("stacks_rows_laid")
        s_v1w = [sem(f"v1_written{p}") for p in range(2)]
        s_vc = [sem(f"v1_loaded{p}") for p in range(2)]
        s_out = sem("output_written")

        def split3(pe, out_ap, lh, ll, rh, rl, first, last):
            nc.tensor.matmul(out_ap, lh, rh, start=first, stop=False)
            nc.tensor.matmul(out_ap, lh, rl, start=False, stop=False)
            return nc.tensor.matmul(out_ap, ll, rh, start=False, stop=last)

        def layernorm_stats(dve):
            for t in range(NTILE):
                nc.vector.bn_stats(stats[:, t, :], xr[:, t, :]).then_inc(s_dve, 1)
            step[0] += NTILE
            dve.wait_ge(s_dve, step[0])
            for t in range(NTILE):
                nc.vector.bn_aggr(mv[:, t, :], stats[:, t, :]).then_inc(s_dve, 1)
            step[0] += NTILE
            dve.wait_ge(s_dve, step[0])
            nc.vector.tensor_scalar(veps[:, :], mv[:, :, 1], EPS, None, ALU.add).then_inc(s_var, 1)

        def layernorm_rows(dve, k):
            dve.wait_ge(s_rstd, k + 1)
            for t in range(NTILE):
                nc.vector.tensor_scalar(xn[:, t, :], xr[:, t, :], mv[:, t, 0:1], rstd[:, t:t + 1],
                                        ALU.subtract, ALU.mult).then_inc(s_xn, 1)

        def pool_rstd(pool, k):
            pool.wait_ge(s_var, k + 1)
            nc.gpsimd.tensor_tensor(rstd[:, :], veps[:, :], mhalf[:, :], ALU.pow).then_inc(s_rstd, 1)

        def transpose_rows(pe, n, kc, k=None):
            for t, (t0, tn) in enumerate(TT):
                if k is not None:
                    pe.wait_ge(s_xn, k * NTILE + t + 1)
                last = nc.tensor.transpose(wide[n % 4][:, t0:t0 + tn], xn[0:tn, t, kc * P:(kc + 1) * P],
                                           ident[0:tn, 0:tn])
            last.then_inc(s_wd, 1)

        def project_T(pe, n, wh, wl, mb):
            for t0, t1 in ((0, WIDE0), (WIDE0, NT)):
                for kc in range(KC):
                    last = split3(pe, wide[n % 4][:, t0:t1], wh[:, kc, mb * P:(mb + 1) * P],
                                  wl[:, kc, mb * P:(mb + 1) * P], xTh[:, kc, t0:t1], xTl[:, kc, t0:t1],
                                  kc == 0, kc == KC - 1)
            last.then_inc(s_wd, 1)

        def wide_hi(act, n, dst, bias=None):
            act.wait_ge(s_wd, n + 1)
            src = wide[n % 4][:, 0:NT]
            if bias is None:
                nc.scalar.activation(dst, src, ACT.Copy).then_inc(s_wh, 1)
            else:
                nc.scalar.activation(dst, src, ACT.Identity, bias=bias).then_inc(s_wh, 1)

        def wide_lo(dve, n, hi, dst, bias=None, nh=None):
            dve.wait_ge(s_wh, (n if nh is None else nh) + 1)
            src = wide[n % 4][:, 0:NT]
            if bias is None:
                nc.vector.tensor_tensor(dst, src, hi, ALU.subtract).then_inc(s_wf, 1)
            else:
                nc.vector.scalar_tensor_tensor(out=dst, in0=src, scalar=bias, in1=hi, op0=ALU.add,
                                               op1=ALU.subtract).then_inc(s_wf, 1)

        step = [0]

        def dve_bias_in(dve, l):
            nc.vector.tensor_scalar(bpr[:, l, :], bpr[:, l, :], tg[:, l:l + 1], None, ALU.mult).then_inc(s_dve, 1)
            step[0] += 1
            dve.wait_ge(s_dve, step[0])
            nc.vector.tensor_tensor(xr[:, :, :], xr[:, :, :], bpr[:, l:l + 1, :].to_broadcast([P, NTILE, D]),
                                    ALU.add).then_inc(s_dve, 1)
            step[0] += 1
            dve.wait_ge(s_dve, step[0])

        es_att = top.enter_context(ExitStack())
        bigid = sb("bigid", [T, T], F16, es_att)
        maskv = sb("maskv", [T, 2 * T], F16, es_att)
        KSa = sb("KS", [P, 2, H, S0], F16, es_att)
        KS = [KSa[0:KROWS + 1, p] for p in range(2)]
        QS = [sb(f"QS{p}", [KROWS + 1, H, T], F16, es_att) for p in range(2)]
        PT = sb("PT", [P, 4, H, T], F32, es_att)
        qh = sb("qh", [P, KC, NT], F16, es_att)
        ql = sb("ql", [P, KC, NT], F16, es_att)
        aallw = sb("aall", [P, B, D], F32, es_att)
        aall = aallw[0:T]
        mx = [sb(f"mx{p}", [T, H], F32, es_att) for p in range(2)]
        nm = [sb(f"nm{p}", [H, T], F16, es_att) for p in range(2)]
        rdens = [sb(f"rden{p}", [T, H], F32, es_att) for p in range(2)]
        pvs = sb("pvs", [GW, H // HG * T], F32, es_att)
        Vc = [sb(f"Vc{p}", [CH, 3, H, VS], F32, es_att) for p in range(2)]

        RD = max(NI, 2 * TC)
        share = sb("share", [P, 2 * NIB * D + KC * RD], F32, es_att)
        rg, ru = (share[:, m * NIB * D:(m + 1) * NIB * D].rearrange("p (i d) -> p i d", i=NIB) for m in range(2))
        rd_ = share[:, 2 * NIB * D:].rearrange("p (k n) -> p k n", k=KC)
        cn = [rg[0:CH, 3 * p:3 * p + 3, :] for p in range(2)]
        kc_ = [[r[:, :, :].rearrange("p a d -> p (a d)")[:, p * 2 * TC:(p + 1) * 2 * TC].bitcast(F16).rearrange(
            "p (s k t) -> p s k t", s=2, k=KC) for p in range(2)] for r in (ru, rd_)]
        kfree = KSa[:, 0, :, :].rearrange("p h s -> p (h s)")
        wgT, wuT = (kfree[:, m * KC * NI:(m + 1) * KC * NI].rearrange("p (k i) -> p k i", k=KC) for m in range(2))
        wdT = kfree[:, 2 * KC * NI:2 * KC * NI + NIB * D].rearrange("p (i d) -> p i d", i=NIB)
        wm = sb("wm", [P, 2 * NIB + KC], F32, es_att)
        winv = sb("winv", [P, 2 * NIB + KC], F32, es_att)
        WPIECES = ([(m, kc, ibs) for m in range(2) for kc in range(KC) for ibs in ((0, 1, 2, 3), (4, 5))]
                   + [(2, 0, ibs) for ibs in ((0, 1), (2, 3), (4, 5))])
        s_fw = sem("block_weights_loaded")
        s_fm = sem("block_weight_maxima_taken")
        s_fs = sem("block_weight_scales_made")
        s_fq = sem("block_weights_rounded")
        s_ft = sem("block_weights_turned")
        s_fc = sem("block_weights_in_fp16")

        es_a = es_att.enter_context(ExitStack())
        cTh = [sb(f"cTh{p}", [P, KC, TC], F16, es_a) for p in range(2)]
        cTl = [sb(f"cTl{p}", [P, KC, TC], F16, es_a) for p in range(2)]
        V1s = [xn[0:CH, :, :].rearrange("p t d -> p (t d)")[:, p * 3 * H * VW:(p + 1) * 3 * H * VW].rearrange(
            "p (c h v) -> p c h v", c=3, h=H) for p in range(2)]
        skh, skl = aTh, aTl
        Vs = sb("Vs", [T, B, H, VW], F32, es_a)
        wah = sb("wah", [P, KC, 3 * D], F16, es_a)
        wal = sb("wal", [P, KC, 3 * D], F16, es_a)
        wrh = sb("wrh", [P, KC, D], F16, es_a)
        wrl = sb("wrl", [P, KC, D], F16, es_a)
        wvh = sb("wvh", [P, KC, 2, D], F16, es_a)
        wvl = sb("wvl", [P, KC, 2, D], F16, es_a)
        PTf = PT[:, :, :, :].rearrange("p c h t -> p c (h t)")
        r_attn = PTf[:, 0, 0:KC * 3 * D].rearrange("p (k n) -> p k n", k=KC)
        r_ref = PTf[:, 1, 0:KC * 2 * D].rearrange("p (k n) -> p k n", k=KC)
        r_proj = PTf[:, 1, KC * 2 * D:KC * 3 * D].rearrange("p (k n) -> p k n", k=KC)
        r_l1 = [PTf[:, 2, m * KC * D:(m + 1) * KC * D].rearrange("p (k n) -> p k n", k=KC) for m in range(3)]
        r_l1.append(PTf[:, 3, 0:KC * D].rearrange("p (k n) -> p k n", k=KC))
        krow = PTf[0:H, 3, KC * D:KC * D + S0 // 2 + 1].bitcast(F16)[:, 0:S0]

        MBANK = [2, 0, 1, 2, 0, 1, 2, 0, 1, 0]
        UT, UK, UN, UV = 0, 2, 6, 7
        SMH = [2, 1, 2, 1, 2, 1, 2, 1, 2, 1, 1, 0, 0, 0, 0, 0]
        TKS = {0: 0, 1: 1, 3: 2, 4: 3, 6: 4, 7: 5}
        NSTEP = 12

        def pe_T(pe, j, o, kc, n):
            p = o % 2
            if kc == 0:
                pe.wait_ge(s_ctx[p], 32 * (j + o // 2 + 1))
            if not (isinstance(n, int) and n < 2):
                pe.wait_ge(s_mf, n - 1)
            bank = misc[MBANK[UT + kc]]
            for c in range(3):
                last = nc.tensor.transpose(bank[:, COFF[c]:COFF[c] + CSZ[c]],
                                           cn[p][0:CSZ[c], c, kc * P:(kc + 1) * P], ident[0:CSZ[c], 0:CSZ[c]])
            last.then_inc(s_md, 1)

        def pe_K(pe, j, o, k, n, nT):
            p, l, mb = o % 2, k // 2, k % 2
            pe.wait_ge(s_mf, nT + 1)
            wh, wl = (wrh, wrl) if l == 0 else (w1kh[:, 0], w1kl[:, 0])
            bank = misc[MBANK[UK + k]][:, 0:TC]
            if k > 1:
                pe.wait_ge(s_mf, n - 1)
            for kc in range(KC):
                last = split3(pe, bank, wh[:, kc, mb * P:(mb + 1) * P], wl[:, kc, mb * P:(mb + 1) * P],
                              cTh[p][:, kc, :], cTl[p][:, kc, :], kc == 0, kc == KC - 1)
            last.then_inc(s_md, 1)

        def pe_V(pe, j, o, c, n):
            p = o % 2
            pe.wait_ge(s_mf, n - 1)
            bank = misc[MBANK[UV + c]][0:CSZ[c], :]
            sl = slice(COFF[c], COFF[c] + CSZ[c])
            for kc in range(KC):
                last = split3(pe, bank, cTh[p][:, kc, sl], cTl[p][:, kc, sl],
                              wvh[:, kc, :, :].rearrange("p l n -> p (l n)"),
                              wvl[:, kc, :, :].rearrange("p l n -> p (l n)"), kc == 0, kc == KC - 1)
            last.then_inc(s_md, 1)

        def pe_SM(pe, j, o, h, layer, smn):
            p = o % 2
            if h % HM == 0:
                nd = NDS[layer]
                pe.wait_ge(s_ks[p][h // HM], 16 * nd * (j + o // 2 + 1) + KSB[layer])
            idx = 2 * H * j + H * o + h + smn
            if not (isinstance(idx, int) and idx < 2):
                pe.wait_ge(s_smf, idx - 1)
            bank = sm_bank[h % 2]
            if layer == 0:
                nc.tensor.matmul(bank[0:T, 0:S0], QS[p][0:KROWS, h, :], KS[p][0:KROWS, h, :],
                                 start=True, stop=False)
                nc.tensor.matmul(bank[0:T, 0:2 * T], bigid[:, :], maskv[:, :], start=False, stop=True
                                 ).then_inc(s_smd, 1)
            else:
                nc.tensor.matmul(bank[0:T, 0:TC], QS[p][0:KROWS, h, :], KS[p][0:KROWS, h, 0:TC],
                                 start=True, stop=True).then_inc(s_smd, 1)

        def pe_N(pe, j, o, smn, n, freed):
            p = o % 2
            pe.wait_ge(s_smf, 2 * H * j + H * (o + 1) + smn)
            pe.wait_ge(s_mf, freed)
            nc.tensor.transpose(misc[MBANK[UN]][0:H, 0:T], mx[p][:, :], ident[0:T, 0:T]).then_inc(s_md, 1)

        def pe_ST(pe, j, o, t, layer, stn, nmc):
            p = o % 2
            nch = 4 - layer
            g, c = t // nch, t % nch
            if t == 0:
                pe.wait_ge(s_nm[p], 16 * (j + o // 2 + 1) + nmc)
            if t >= 2 or layer == 1:
                pe.wait_ge(s_exp, 2 * (H // HG) * nch * j + (H // HG) * nch * o + t + stn - 1)
            bank = st_bank[t % 2]
            if layer == 0:
                k0, kn = (0, T) if c == 0 else (T + COFF[c - 1], CSZ[c - 1])
            else:
                k0, kn = COFF[c], CSZ[c]
            for i in range(HG):
                h = g * HG + i
                last = nc.tensor.matmul(bank[0:kn, i * T:(i + 1) * T], KS[p][:, h, k0:k0 + kn],
                                        QS[p][:, h, :], start=True, stop=True)
            last.then_inc(s_std, 1)

        def pe_PV(pe, j, o, h, layer, stn, mkn, nrn):
            p = o % 2
            nch = 4 - layer
            g = h // HG
            if h % HG == 0:
                per = (H // HG) * nch
                pe.wait_ge(s_exp, 2 * per * j + per * o + nch * (g + 1) + stn)
                if layer == 0:
                    pe.wait_ge(s_msk, 2 * (H // HG) * j + (H // HG) * o + g + 1)
                else:
                    if g == 0:
                        pe.wait_ge(s_vc[p], 16 * (j + o // 2 + 1))
            if h == 0 and layer == 1:
                pe.wait_ge(s_nrm, 2 * j + o + nrn - 1)
            elif h == 0 and isinstance(j, int) and 2 * j + o > 0:
                pe.wait_ge(s_nrm, 2 * j + o + nrn)
            i = h % HG
            dst = pv_bank[p * layer][0:GW, g * T:(g + 1) * T]
            for c in range(nch):
                if layer == 0:
                    kn = T if c == 0 else CSZ[c - 1]
                    v = VSB[p][:, :, :] if c == 0 else Vc[p][0:kn, c - 1, :, :]
                else:
                    kn = CSZ[c]
                    v = Vc[p][0:kn, c, :, :]
                w0 = g * HG * VS + i * GW
                last = nc.tensor.matmul(dst, v.rearrange("p h v -> p (h v)")[:, w0:w0 + GW], PT[0:kn, c, h, :],
                                        start=(i == 0 and c == 0), stop=(i == HG - 1 and c == nch - 1))
            last.then_inc(s_pvd, 1)

        def pe_turn(pe, j, o, bsum):
            bank = pv_bank[o % 2 if bsum else 0]
            pe.wait_ge(s_ev, 2 * j + o + 1 + bsum)
            for g in range(H // HG):
                last = nc.tensor.transpose(bank[0:T, g * GW:(g + 1) * GW], pvs[:, g * T:(g + 1) * T],
                                           ident[0:GW, 0:GW])
            last.then_inc(s_tvd, 1)

        def act_hi_T(act, j, o, kc, n):
            act.wait_ge(s_md, n + 1)
            nc.scalar.activation(cTh[o % 2][:, kc, :], misc[MBANK[UT + kc]][:, 0:TC], ACT.Copy).then_inc(s_mh, 1)

        def act_hi_K(act, j, o, k, n):
            p, l, mb = o % 2, k // 2, k % 2
            if o >= 2 and mb == 0:
                act.wait_ge(s_kw[l][p], KW * (j + o // 2))
            act.wait_ge(s_md, n + 1)
            nc.scalar.activation(kc_[l][p][:, 0, mb, :], misc[MBANK[UK + k]][:, 0:TC], ACT.Identity,
                                 bias=bcol[:, 2 + l, mb:mb + 1]).then_inc(s_mh, 1)

        def act_exp(act, j, o, t, layer, stn):
            nch = 4 - layer
            g, c = t // nch, t % nch
            idx = 2 * (H // HG) * nch * j + (H // HG) * nch * o + t + stn
            act.wait_ge(s_std, idx + 1)
            if layer == 0:
                kn, bias = (T, 0.0) if c == 0 else (CSZ[c - 1], ctxb[0:CSZ[c - 1], 0:1])
            else:
                kn, bias = CSZ[c], 0.0
            nc.scalar.activation(PT[0:kn, c, g * HG:(g + 1) * HG, :].rearrange("p h t -> p (h t)"),
                                 st_bank[t % 2][0:kn, 0:HG * T], ACT.Exp, scale=SCALE, bias=bias
                                 ).then_inc(s_exp, 1)

        def act_evac(act, j, o, bsum):
            act.wait_ge(s_pvd, H * (2 * j + o + 1 + bsum))
            bank = pv_bank[o % 2 if bsum else 0]
            nc.scalar.activation(pvs[:, :], bank[0:GW, 0:H // HG * T], ACT.Copy).then_inc(s_ev, 1)

        def dve_lo_T(dve, j, o, kc, n, nh):
            p = o % 2
            dve.wait_ge(s_mh, nh + 1)
            nc.vector.tensor_tensor(cTl[p][:, kc, :], misc[MBANK[UT + kc]][:, 0:TC], cTh[p][:, kc, :],
                                    ALU.subtract).then_inc(s_mf, 1)

        def dve_lo_K(dve, j, o, k, n, nh):
            p, l, mb = o % 2, k // 2, k % 2
            dve.wait_ge(s_mh, nh + 1)
            nc.vector.scalar_tensor_tensor(out=kc_[l][p][:, 1, mb, :], in0=misc[MBANK[UK + k]][:, 0:TC],
                                           scalar=bcol[:, 2 + l, mb:mb + 1], in1=kc_[l][p][:, 0, mb, :],
                                           op0=ALU.add, op1=ALU.subtract).then_inc(s_mf, 1)

        def dve_V(dve, j, o, c, n):
            p = o % 2
            dve.wait_ge(s_md, n + 1)
            kn = CSZ[c]
            bank = misc[MBANK[UV + c]][0:kn, :].rearrange("p (l h d) -> p l h d", l=2, h=H)
            row = brow[0:kn, 1:3, :].rearrange("p l (h d) -> p l h d", h=H)
            nc.vector.tensor_tensor(Vc[p][0:kn, c, :, 0:DH], bank[:, 0], row[:, 0], ALU.add)
            nc.vector.tensor_tensor(V1s[p][0:kn, c, :, 0:DH], bank[:, 1], row[:, 1], ALU.add).then_inc(s_mf, 1)

        def dve_max(dve, j, o, h, layer, smn):
            p = o % 2
            dve.wait_ge(s_smd, 2 * H * j + H * o + h + smn + 1)
            nc.vector.tensor_reduce(mx[p][:, h:h + 1], sm_bank[h % 2][0:T, 0:(S0 if layer == 0 else TC)], X,
                                    ALU.max).then_inc(s_smf, 1)

        def dve_N(dve, j, o, n):
            p = o % 2
            dve.wait_ge(s_md, n + 1)
            nc.vector.tensor_scalar(nm[p][:, :], misc[MBANK[UN]][0:H, 0:T], -1.0 / (WS * WS), None,
                                    ALU.mult).then_inc(s_mf, 1)

        def dve_norm(dve, j, o, bsum):
            dve.wait_ge(s_tvd, 2 * j + o + 1 + bsum)
            pv = pv_bank[o % 2 if bsum else 0][0:T, 0:H * VW].rearrange("p (h v) -> p h v", h=H)
            rden = rdens[o % 2]
            nc.vector.reciprocal(rden[:, :], pv[:, :, DH]).then_inc(s_rd, 1)
            dve.wait_ge(s_rd, 2 * j + o + 1 + bsum)
            nc.vector.tensor_tensor(aall[:, bass.ds(2 * j + o, 1), :].rearrange("p a (h d) -> p (a h) d", h=H),
                                    pv[:, :, 0:DH], rden[:, :].unsqueeze(2).to_broadcast([T, H, DH]),
                                    ALU.mult).then_inc(s_nrm, 1)
            
        NDS = [3, 2]
        KSB = [0, 16 * 3 * (B // 2)]
        QSLOTS, KSLOTS = ((0, 2, 1), (2, 4, 1)), ((0, 3, 2), (1, 4, 2))
        VSB = [sb(f"VSB{p}", [T, H, VS], F32, es_a) for p in range(2)]
        ctxb = sb("ctxb", [P, 1], F32, es_a)
        s_vsb = [sem(f"own_values_staged{p}") for p in range(2)]
        KW = 16 * 2 * KC

        def sp_ctx(sp, j, o):
            p = o % 2
            b = 2 * j + o
            src = ctx_seq[bass.ds(b, 1), :, :].rearrange("a t d -> (a t) d")
            sp.dma_start(cn[p][:, 0, :], src[0:CH, :]).then_inc(s_ctx[p], 16)
            sp.dma_start(cn[p][0:CSZ[1], 1:3, :], src[CH:TC, :].rearrange("(c t) d -> t c d", c=2)
                         ).then_inc(s_ctx[p], 16)

        def sp_halves_out(sp, dram, halves, mb, slots, sem_):
            for src, (s0, s1, step_) in zip(halves, slots):
                sp.dma_start(dram[mb * HM:(mb + 1) * HM, :, s0:s1:step_, :].rearrange("h d s t -> (h d) s t"),
                             src[:, mb:mb + 1, :].to_broadcast([P, 2, NT])).then_inc(sem_, 16)

        def sp_keys_out(sp, j, o, l):
            p = o % 2
            for mb in range(KC):
                for s in (0, 2):
                    sp.dma_start(k_dram[l][bass.ds(2 * j + o, 1), mb * HM:(mb + 1) * HM, :, s:s + 2, :].rearrange(
                        "b h d s t -> (b h d) s t"), kc_[l][p][:, :, mb, :]).then_inc(s_kw[l][p], 16)

        def sp_stack_in(sp, j, o, mb, dst, dram, own):
            p = o % 2
            hs = slice(mb * HM, (mb + 1) * HM)
            b = 2 * j + o
            if own:
                src = dram[hs, :, :, bass.ds(b * T, T)].rearrange("h d s t -> (d s) h t")
            else:
                src = dram[bass.ds(b, 1), hs].rearrange("b h d s t -> (d s) (b h) t")
            sp.dma_start(dst, src).then_inc(s_ks[p][mb], 16)

        def sp_stack0(sp, j, o, mb):
            p, hs = o % 2, slice(mb * HM, (mb + 1) * HM)
            sp_stack_in(sp, j, o, mb, QS[p][0:KROWS, hs, :], q_dram, True)
            sp_stack_in(sp, j, o, mb, KS[p][0:KROWS, hs, 0:T], sk_dram, True)
            sp_stack_in(sp, j, o, mb, KS[p][0:KROWS, hs, T:S0], k_dram[0], False)

        def sp_stack1(sp, j, o, mb, keys=True, queries=True):
            p, hs = o % 2, slice(mb * HM, (mb + 1) * HM)
            if keys:
                sp_stack_in(sp, j, o, mb, KS[p][0:KROWS, hs, 0:TC], k_dram[1], False)
            if queries:
                sp_stack_in(sp, j, o, mb, QS[p][0:KROWS, hs, :], q_dram, True)

        with nc.Block() as block:

            @block.sync
            def _(sp):
                sp.dma_start(xr[:, 0:FULL, :], xf[0:FULL * P, :].rearrange("(t p) d -> p t d", p=P)).then_inc(s_x, 16)
                sp.wait_ge(s_pad, 1)
                sp.dma_start(xr[0:LAST, FULL, :], xf[FULL * P:NT, :]).then_inc(s_x, 16)
                sp.dma_start(r_attn, w_attn.rearrange("(k p) n -> p k n", p=P)).then_inc(s_wr[0], 16)
                sp_ctx(sp, 0, 0)
                sp.dma_start(r_ref, w_ref.rearrange("(k p) n -> p k n", p=P)).then_inc(s_wr[1], 16)
                sp.dma_start(r_proj, w_proj.rearrange("(k p) n -> p k n", p=P)).then_inc(s_wr[1], 16)
                for m, w in enumerate((w_k, w_v, w_q, w_o)):
                    sp.dma_start(r_l1[m], w.rearrange("(k p) n -> p k n", p=P)).then_inc(s_wr[2], 16)
                sp_ctx(sp, 0, 1)
                for p in range(2):
                    if p == 0:
                        sp.wait_ge(s_const, 1)
                    sp.dma_start(KS[p][KROWS:KROWS + 1, :, :], krow[:, :]).then_inc(s_kr, 16)

                for mb in range(KC):
                    sp.wait_ge(s_wf, 3 + mb)
                    sp_halves_out(sp, q_dram, (qh, ql), mb, QSLOTS, s_qw)
                for mb in range(KC):
                    sp.wait_ge(s_wf, 5 + mb)
                    sp_halves_out(sp, sk_dram, (skh, skl), mb, KSLOTS, s_qw)
                sp.wait_ge(s_mf, 2)
                sp_ctx(sp, 0, 2)
                sp.wait_ge(s_mf, 4)
                sp_keys_out(sp, 0, 0, 0)
                sp.wait_ge(s_qw, 16 * 8)
                sp.wait_ge(s_kw[0][0], KW)
                for mb in range(KC):
                    sp_stack0(sp, 0, 0, mb)
                sp.wait_ge(s_mf, 10)
                sp_keys_out(sp, 0, 1, 0)
                sp.wait_ge(s_zero, 1)
                sp.dma_start(VSB[0][:, :, 0:VW], Vs[:, 0, :, :]).then_inc(s_vsb[0], 16)
                sp.wait_ge(s_kw[0][1], KW)
                sp_stack0(sp, 0, 1, 0)
                sp.wait_ge(s_mf, 16)
                sp.dma_start(QS[0][KROWS:KROWS + 1, :, :], nm[0][:, :]).then_inc(s_nm[0], 16)
                sp_stack0(sp, 0, 1, 1)
                sp_ctx(sp, 0, 3)
                for o in range(2):
                    sp_keys_out(sp, 0, o, 1)
                sp.dma_start(v1_dram[0], V1s[0][:, :, :, :].rearrange("p c h v -> p (c h v)")).then_inc(s_v1w[0], 16)

                def round0(j, u, ctx, keys, nxt):
                    n0 = 16 + 10 * (2 * j + u)
                    p = u % 2
                    n1 = n0 + (UN if keys else 0)
                    if nxt:
                        sp.wait_ge(s_std, 16 * (2 * j + u) + 8)
                        sp.dma_start(VSB[1 - p][:, :, 0:VW], Vs[:, bass.ds(2 * j + u + 1, 1), :, :].rearrange(
                            "p a h v -> p (a h) v")).then_inc(s_vsb[1 - p], 16)
                    if ctx:
                        sp.wait_ge(s_mf, n0 + 2)
                        sp_ctx(sp, j, u + 4)
                    if keys:
                        sp.wait_ge(s_mf, n0 + 4)
                        sp_keys_out(sp, j, u + 2, 0)
                        sp.wait_ge(s_mf, n0 + 6)
                        sp_keys_out(sp, j, u + 2, 1)
                        sp.wait_ge(s_kw[0][p], KW * (j + 2))
                        sp_stack0(sp, j, u + 2, 0)
                    if nxt:
                        sp.wait_ge(s_mf, n1 + 1)
                        sp.dma_start(QS[1 - p][KROWS:KROWS + 1, :, :], nm[1 - p][:, :]).then_inc(s_nm[1 - p], 16)
                    if keys:
                        sp.wait_ge(s_std, 16 * (2 * j + u + 1))
                        sp_stack0(sp, j, u + 2, 1)
                    if nxt:
                        sp.wait_ge(s_mf, n1 + 4)
                        sp.dma_start(v1_dram[bass.ds(2 * j + u + 1, 1)].rearrange("b p n -> (b p) n"),
                                     V1s[1 - p][:, :, :, :].rearrange("p c h v -> p (c h v)")).then_inc(s_v1w[1 - p], 16)

                with sp.Fori(0, B // 2 - 2) as j:
                    for u in range(2):
                        round0(j, u, True, True, True)
                for u in range(2):
                    round0(B // 2 - 2, u, False, True, True)
                for p in range(2):
                    for l in range(2):
                        sp.wait_ge(s_kw[l][p], KW * B // 2)
                FI = (NIB - 1) * P
                for dst, src in ((rg, w_gate), (ru, w_up)):
                    sp.dma_start(dst[:, 0:NIB - 1, :], src[0:FI, :].rearrange("(i p) d -> p i d", p=P)).then_inc(s_fw, 16)
                    sp.dma_start(dst[0:LASTI, NIB - 1, :], src[FI:NI, :]).then_inc(s_fw, 16)
                sp.dma_start(rd_[:, :, 0:NI], w_down.rearrange("(k p) n -> p k n", p=P)).then_inc(s_fw, 16)
                round0(B // 2 - 1, 0, False, False, True)
                for p in range(2):
                    sp.wait_ge(s_v1w[p], 16 * B // 2)

            @block.gpsimd
            def _(pool):
                nc.gpsimd.memset(xr[:, FULL, :], 0.0).then_inc(s_pad, 1)
                nc.gpsimd.memset(ident[:, :], 0.0)
                nc.gpsimd.memset(krow[:, :], WS * WS)
                nc.gpsimd.memset(bigid[:, :], 0.0)
                nc.gpsimd.memset(maskv[:, :], 0.0)
                nc.gpsimd.memset(mhalf[:, :], -0.5)
                nc.gpsimd.memset(ones[:, :], 1.0)
                nc.gpsimd.memset(ctxb[:, :], CTX_BIAS)
                nc.gpsimd.memset(magic[:, 0:1], MAGIC)
                nc.gpsimd.memset(magic[:, 1:2], -MAGIC).then_inc(s_const, 1)
                pool.wait_ge(s_const, 1)
                nc.gpsimd.affine_select(out=ident[:, :], in_=ident[:, :], compare_op=ALU.not_equal, fill=1.0,
                                        base=0, pattern=[[-1, P]], channel_multiplier=1).then_inc(s_const, 1)
                nc.gpsimd.affine_select(out=bigid[:, :], in_=bigid[:, :], compare_op=ALU.not_equal, fill=BIG,
                                        base=0, pattern=[[-1, T]], channel_multiplier=1).then_inc(s_const, 1)
                nc.gpsimd.affine_select(out=maskv[:, 0:T], in_=maskv[:, 0:T], compare_op=ALU.is_ge, fill=-BIG,
                                        base=0, pattern=[[-1, T]], channel_multiplier=1).then_inc(s_const, 1)
                nc.gpsimd.affine_select(out=maskv[:, T:2 * T], in_=maskv[:, T:2 * T], compare_op=ALU.not_equal,
                                        fill=-BIG, base=0, pattern=[[-1, T]], channel_multiplier=1
                                        ).then_inc(s_const, 1)
                pool_rstd(pool, 0)
                for p in range(2):
                    nc.gpsimd.memset(Vc[p][:, :, :, :], 0.0)
                    last = nc.gpsimd.memset(VSB[p][:, :, :], 0.0)
                last.then_inc(s_zero, 1)

                def masks(j, u):
                    for g in range(H // HG):
                        hs = slice(g * HG, (g + 1) * HG)
                        pool.wait_ge(s_exp, 16 * (2 * j + u) + 4 * g + 2)
                        pool.sem_inc(s_mb, 1)
                        nc.gpsimd.affine_select(out=PT[0:T, 0, hs, :], in_=PT[0:T, 0, hs, :], compare_op=ALU.is_ge,
                                                fill=0.0, base=0, pattern=[[0, HG], [1, T]], channel_multiplier=-1)
                        nc.gpsimd.affine_select(out=PT[0:T, 1, hs, :], in_=PT[0:T, 1, hs, :],
                                                compare_op=ALU.not_equal, fill=0.0, base=0,
                                                pattern=[[0, HG], [-1, T]], channel_multiplier=1).then_inc(s_msk, 1)

                with pool.Fori(0, B // 2 - 1) as j:
                    for u in range(2):
                        masks(j, u)
                masks(B // 2 - 1, 0)
                masks(B // 2 - 1, 1)

            @block.scalar
            def _(act):
                for k, (dst, src) in enumerate((
                        (bcol[:, 0, :], b_attn[0:D].rearrange("(k p) -> p k", p=P)),
                        (bcol[:, 1, :], b_attn[D:2 * D].rearrange("(k p) -> p k", p=P)),
                        (bcol[:, 2, :], b_ref[0:D].rearrange("(k p) -> p k", p=P)),
                        (bcol[:, 3, :], b_k.rearrange("(k p) -> p k", p=P)),
                        (bcol[:, 4, :], b_q.rearrange("(k p) -> p k", p=P)),
                        (brow[:, 0, :], b_attn[2 * D:3 * D].partition_broadcast(P)),
                        (brow[:, 1, :], b_ref[D:2 * D].partition_broadcast(P)),
                        (brow[:, 2, :], b_v.partition_broadcast(P)))):
                    act.dma_start(dst, src, allow_slow_non_contiguous=k <= 4).then_inc(s_bias, 16)
                act.wait_ge(s_wr[0], 16)
                nc.scalar.activation(wah[:, :, :], r_attn, ACT.Copy, scale=WS).then_inc(s_wh8, 1)
                for kc in range(KC):
                    wide_hi(act, kc, xTh[:, kc, :])
                for dst, src in (
                        (gts[:, 0:2], g_xattn.partition_broadcast(P)), (gts[:, 2:4], g_ffn.partition_broadcast(P)),
                        (clips[:, 0:1], clip_x.partition_broadcast(P)), (clips[:, 1:2], clip_down.partition_broadcast(P)),
                        (bpr[:, 0, :], b_proj.partition_broadcast(P)), (bpr[:, 1, :], b_o.partition_broadcast(P)),
                        (gbr[:, :], gate_b.partition_broadcast(P)),
                        (b1c[:, :, :], b1.rearrange("e (p f) -> p e f", p=P)), (b2r[:, :], b2),
                        (gwr[:, :, :], gate_w.rearrange("(k p) e -> p k e", p=P))):
                    act.dma_start(dst, src).then_inc(s_small, 16)
                act.wait_ge(s_biasp, 1)
                for mb in range(KC):
                    wide_hi(act, 2 + mb, qh[:, mb, :], bcol[:, 0, mb:mb + 1])
                for mb in range(KC):
                    wide_hi(act, 4 + mb, skh[:, mb, :], bcol[:, 1, mb:mb + 1])
                act.wait_ge(s_wr[1], 32)
                act.wait_ge(s_small, 16 * 10)
                nc.scalar.activation(wrh[:, :, :], r_ref[:, :, 0:D], ACT.Copy, scale=WS)
                nc.scalar.activation(wvh[:, :, 0, :], r_ref[:, :, D:2 * D], ACT.Copy, scale=WS)
                nc.scalar.activation(wph[:, 0, :, :], r_proj, ACT.Copy, scale=WS)
                nc.scalar.activation(gwh[:, :, :], gwr[:, :, :], ACT.Copy, scale=WS).then_inc(s_wh8, 1)
                nc.scalar.activation(tg[:, :], gts[:, :], ACT.Tanh)
                nc.scalar.activation(clipt[:, :], clips[:, :], ACT.Tanh, scale=0.5).then_inc(s_tanh, 1)
                for n, dsts in ((8, (w1kh[:, 0], wvh[:, :, 1])), (9, (w1kh[:, 1], wph[:, 1]))):
                    act.wait_ge(s_wd, n + 1)
                    for i, dst in enumerate(dsts):
                        last = nc.scalar.activation(dst, wide[n % 4][:, 512 * i:512 * i + 512].rearrange(
                            "p (k n) -> p k n", k=KC), ACT.Copy, scale=WS)
                    last.then_inc(s_wh, 1)

                for o in range(2):
                    for kc in range(KC):
                        act_hi_T(act, 0, o, kc, 6 * o + kc)
                    for k in range(4):
                        act_hi_K(act, 0, o, k, 6 * o + 2 + k)

                act.wait_ge(s_wf, 10)
                act.wait_ge(s_split, 2)

                def rounding(k):
                    if k == 0:
                        act.wait_ge(s_fs, 1)
                    if k < 2 * NIB:
                        r, ib = (rg, ru)[k // NIB], k % NIB
                        n = P if ib < NIB - 1 else LASTI
                        piece = r[0:n, ib, :]
                    else:
                        n, piece = P, rd_[:, k - 2 * NIB, 0:NI]
                    nc.scalar.activation(piece, piece, ACT.Identity, bias=magic[0:n, 0:1],
                                         scale=winv[0:n, k:k + 1]).then_inc(s_fq, 1)

                def round0(j, u, keys, weights=False):
                    n0 = 16 + 10 * (2 * j + u)
                    for t in range(16):
                        act_exp(act, j, u, t, 0, 0)
                        if weights and 4 <= t < 4 + NIB + KC // 2:
                            rounding(2 * (t - 4))
                            rounding(2 * (t - 4) + 1)
                        if keys and t in TKS:
                            k = TKS[t]
                            if k < 2:
                                act_hi_T(act, j, u + 2, k, n0 + k)
                            else:
                                act_hi_K(act, j, u + 2, k - 2, n0 + k)
                    act_evac(act, j, u, 0)

                with act.Fori(0, B // 2 - 1) as j:
                    for u in range(2):
                        round0(j, u, True)
                for u in range(2):
                    round0(B // 2 - 1, u, False, u == 1)

            @block.tensor
            def _(pe):
                pe.wait_ge(s_const, 5)
                for kc in range(KC):
                    transpose_rows(pe, kc, kc, 0)
                pe.wait_ge(s_split, 1)
                pe.wait_ge(s_wf, 2)
                for mb in range(KC):
                    project_T(pe, 2 + mb, wah, wal, mb)
                for mb in range(KC):
                    pe.wait_ge(s_wf, 4 + mb - 3)
                    project_T(pe, 4 + mb, wah, wal, KC + mb)
                for n in range(2):
                    pe.wait_ge(s_wf, 6 + n - 3)
                    for i in range(4):
                        b = 4 * n + i
                        for kc in range(KC):
                            last = split3(pe, wide[(6 + n) % 4][0:T, i * D:(i + 1) * D],
                                          xTh[:, kc, b * T:(b + 1) * T], xTl[:, kc, b * T:(b + 1) * T],
                                          wah[:, kc, 2 * D:3 * D], wal[:, kc, 2 * D:3 * D], kc == 0, kc == KC - 1)
                    last.then_inc(s_wd, 1)
                pe.wait_ge(s_wr[2], 64)
                for n in range(2):
                    pe.wait_ge(s_wf, 8 + n - 3)
                    for i in range(2):
                        for kc in range(KC):
                            for ob in range(KC):
                                o0 = 512 * i + kc * D + ob * P
                                last = nc.tensor.transpose(wide[(8 + n) % 4][:, o0:o0 + P],
                                                           r_l1[2 * n + i][:, ob, kc * P:(kc + 1) * P], ident[:, :])
                    last.then_inc(s_wd, 1)
                pe.wait_ge(s_split, 2)
                pe.wait_ge(s_wf, 10)
                for o in range(2):
                    n0 = 6 * o
                    for kc in range(KC):
                        pe_T(pe, 0, o, kc, n0 + kc)
                    for k in range(4):
                        pe_K(pe, 0, o, k, n0 + 2 + k, n0 + 1)
                for c in range(3):
                    pe_V(pe, 0, 0, c, 12 + c)
                for h in range(H):
                    pe_SM(pe, 0, 0, h, 0, 0)
                pe_N(pe, 0, 0, 0, 15, 15)
                pe.wait_ge(s_kr, 32)
                pe.wait_ge(s_mf, 16)

                def turning(k):
                    m, kc, ibs = WPIECES[k]
                    if k >= 3:
                        pe.wait_ge(s_fc, k - 2)
                    pe.wait_ge(s_fq, min((m + 1) * NIB, 2 * NIB) if m < 2 else 2 * NIB + KC)
                    for i, ib in enumerate(ibs):
                        n = P if ib < NIB - 1 else LASTI
                        if m < 2:
                            last = nc.tensor.transpose(misc[k % 3][:, i * P:i * P + n],
                                                       (rg, ru)[m][0:n, ib, kc * P:(kc + 1) * P], ident[0:n, 0:n])
                        else:
                            for q in range(KC):
                                last = nc.tensor.transpose(misc[k % 3][0:n, i * D + q * P:i * D + (q + 1) * P],
                                                           rd_[:, q, ib * P:ib * P + n], ident[:, :])
                    last.then_inc(s_ft, 1)

                def round0(j, u, keys, nxt, weights=False):
                    n0 = 16 + 10 * (2 * j + u)
                    h = 0
                    for t in range(16):
                        if t == 4:
                            pe.wait_ge(s_vsb[u], 16 * (j + 1))
                        pe_ST(pe, j, u, t, 0, 0, 0)
                        if keys and t in TKS:
                            k = TKS[t]
                            if k < 2:
                                pe_T(pe, j, u + 2, k, n0 + k)
                            else:
                                pe_K(pe, j, u + 2, k - 2, n0 + k, n0 + 1)
                        if nxt:
                            for _ in range(SMH[t]):
                                pe_SM(pe, j, u + 1, h, 0, 0)
                                h += 1
                        if t >= 4:
                            pe_PV(pe, j, u, t - 4, 0, 0, 0, 0)
                        if weights and t >= 9:
                            turning(t - 9)
                        if nxt and t == NSTEP:
                            n1 = n0 + (UN if keys else 0)
                            pe_N(pe, j, u + 1, 0, n1, n1 - 1)
                    for i in range(4):
                        pe_PV(pe, j, u, 12 + i, 0, 0, 0, 0)
                        if nxt and i == 0:
                            pe_V(pe, j, u + 1, 0, n1 + 1)
                    if nxt:
                        for c in (1, 2):
                            pe_V(pe, j, u + 1, c, n1 + 1 + c)
                    if weights:
                        for k in range(7, len(WPIECES)):
                            turning(k)
                    pe_turn(pe, j, u, 0)

                with pe.Fori(0, B // 2 - 1) as j:
                    for u in range(2):
                        round0(j, u, True, True)
                round0(B // 2 - 1, 0, False, True)
                round0(B // 2 - 1, 1, False, False, True)

            @block.vector
            def _(dve):
                dve.wait_ge(s_x, 32)
                layernorm_stats(dve)
                layernorm_rows(dve, 0)
                dve.wait_ge(s_bias, 16 * 8)
                nc.vector.tensor_scalar(brow[:, :, :], brow[:, :, :], WS, None, ALU.mult)
                nc.vector.tensor_scalar(bcol[:, :, :], bcol[:, :, :], WS, None, ALU.mult).then_inc(s_biasp, 1)
                dve.wait_ge(s_wh8, 1)
                nc.vector.scalar_tensor_tensor(out=wal[:, :, :], in0=r_attn, scalar=WS, in1=wah[:, :, :],
                                               op0=ALU.mult, op1=ALU.subtract).then_inc(s_split, 1)
                for kc in range(KC):
                    wide_lo(dve, kc, xTh[:, kc, :], xTl[:, kc, :])
                dve.wait_ge(s_biasp, 1)
                for mb in range(KC):
                    wide_lo(dve, 2 + mb, qh[:, mb, :], ql[:, mb, :], bcol[:, 0, mb:mb + 1])
                for mb in range(KC):
                    wide_lo(dve, 4 + mb, skh[:, mb, :], skl[:, mb, :], bcol[:, 1, mb:mb + 1])
                for p in range(2):
                    nc.vector.memset(V1s[p][:, :, :, DH:VW], WS)
                nc.vector.memset(Vs[:, :, :, DH:VW], WS)
                dve.wait_ge(s_wh8, 2)
                for dst, src, hi in ((wrl[:, :, :], r_ref[:, :, 0:D], wrh[:, :, :]),
                                     (wvl[:, :, 0, :], r_ref[:, :, D:2 * D], wvh[:, :, 0, :]),
                                     (wpl[:, 0, :, :], r_proj, wph[:, 0, :, :]),
                                     (gwl[:, :, :], gwr[:, :, :], gwh[:, :, :])):
                    last = nc.vector.scalar_tensor_tensor(out=dst, in0=src, scalar=WS, in1=hi, op0=ALU.mult,
                                                          op1=ALU.subtract)
                last.then_inc(s_split, 1)
                for n in range(2):
                    dve.wait_ge(s_wd, 6 + n + 1)
                    for i in range(4):
                        last = nc.vector.tensor_tensor(
                            Vs[:, 4 * n + i, :, 0:DH],
                            wide[(6 + n) % 4][0:T, i * D:(i + 1) * D].rearrange("p (h d) -> p h d", h=H),
                            brow[0:T, 0, :].rearrange("p (h d) -> p h d", h=H), ALU.add)
                    last.then_inc(s_wf, 1)
                for n, dsts in ((8, ((w1kh[:, 0], w1kl[:, 0]), (wvh[:, :, 1], wvl[:, :, 1]))),
                                (9, ((w1kh[:, 1], w1kl[:, 1]), (wph[:, 1], wpl[:, 1])))):
                    dve.wait_ge(s_wh, n + 1 - 2)
                    for i, (hi, lo) in enumerate(dsts):
                        last = nc.vector.scalar_tensor_tensor(
                            out=lo, in0=wide[n % 4][:, 512 * i:512 * i + 512].rearrange("p (k n) -> p k n", k=KC),
                            scalar=WS, in1=hi, op0=ALU.mult, op1=ALU.subtract)
                    last.then_inc(s_wf, 1)
                dve.wait_ge(s_zero, 1)
                for p in range(2):
                    nc.vector.memset(Vc[p][:, :, :, DH:VW], WS)
                dve.wait_ge(s_tanh, 1)
                nc.vector.tensor_scalar(tgs[:, :], tg[:, :], 1.0 / WS, None, ALU.mult)
                nc.vector.tensor_scalar(clipt[:, :], clipt[:, :], 1.0, 0.5 / QMAX, ALU.add, ALU.mult)
                nc.vector.tensor_scalar(b1c[:, :, :], b1c[:, :, :], WS, None, ALU.mult)
                for o in range(2):
                    for kc in range(KC):
                        dve_lo_T(dve, 0, o, kc, 6 * o + kc, 6 * o + kc)
                    for k in range(4):
                        dve_lo_K(dve, 0, o, k, 6 * o + 2 + k, 6 * o + 2 + k)
                for c in range(3):
                    dve_V(dve, 0, 0, c, 12 + c)
                for h in range(H):
                    dve_max(dve, 0, 0, h, 0, 0)
                dve_N(dve, 0, 0, 15)

                def round0(j, u, keys, nxt):
                    i = 2 * j + u
                    n0 = 16 + 10 * i
                    nh0 = 12 + 6 * i
                    h = 0
                    for t in range(16):
                        if keys and t in TKS:
                            k = TKS[t]
                            if k == 2 and not (isinstance(j, int) and i < 2):
                                pass
                            if k < 2:
                                dve_lo_T(dve, j, u + 2, k, n0 + k, nh0 + k)
                            else:
                                dve_lo_K(dve, j, u + 2, k - 2, n0 + k, nh0 + k)
                        if nxt:
                            for _ in range(SMH[t]):
                                dve_max(dve, j, u + 1, h, 0, 0)
                                h += 1
                        if nxt and t == NSTEP:
                            n1 = n0 + (UN if keys else 0)
                            dve_N(dve, j, u + 1, n1)
                    if nxt:
                        for c in range(3):
                            dve_V(dve, j, u + 1, c, n1 + 1 + c)
                    dve_norm(dve, j, u, 0)

                with dve.Fori(0, B // 2 - 1) as j:
                    for u in range(2):
                        round0(j, u, True, True)
                round0(B // 2 - 1, 0, False, True)
                nc.vector.memset(wm[:, :], 1.0).then_inc(s_fm, 1)
                dve.wait_ge(s_fm, 1)
                dve.wait_ge(s_fw, 16 * 5)
                for r, base in ((rg, 0), (ru, NIB)):
                    nc.vector.tensor_reduce(wm[:, base:base + NIB - 1], r[:, 0:NIB - 1, :], X, ALU.max,
                                            apply_absolute_value=True)
                    nc.vector.tensor_reduce(wm[0:LASTI, base + NIB - 1:base + NIB], r[0:LASTI, NIB - 1:NIB, :], X,
                                            ALU.max, apply_absolute_value=True)
                nc.vector.tensor_reduce(wm[:, 2 * NIB:], rd_[:, :, 0:NI], X, ALU.max,
                                        apply_absolute_value=True).then_inc(s_fm, 1)
                dve.wait_ge(s_fm, 2)
                nc.vector.tensor_scalar(wm[:, :], wm[:, :], 1.0 / QMAX, None, ALU.mult).then_inc(s_fm, 1)
                dve.wait_ge(s_fm, 3)
                nc.vector.reciprocal(winv[:, :], wm[:, :]).then_inc(s_fs, 1)
                dve_bias_in(dve, 0)
                for k, (m, kc, ibs) in enumerate(WPIECES):
                    dve.wait_ge(s_ft, k + 1)
                    if m < 2:
                        c0, c1 = ibs[0] * P, min(NI, (ibs[-1] + 1) * P)
                        last = nc.vector.tensor_scalar((wgT, wuT)[m][:, kc, c0:c1], misc[k % 3][:, 0:c1 - c0], -MAGIC,
                                                       None, ALU.add)
                    elif ibs[-1] < NIB - 1:
                        last = nc.vector.tensor_scalar(wdT[:, ibs[0]:ibs[-1] + 1, :].rearrange("p i d -> p (i d)"),
                                                       misc[k % 3][:, 0:2 * D], -MAGIC, None, ALU.add)
                    else:
                        nc.vector.tensor_scalar(wdT[:, ibs[0], :], misc[k % 3][:, 0:D], -MAGIC, None, ALU.add)
                        last = nc.vector.tensor_scalar(wdT[0:LASTI, ibs[1], :], misc[k % 3][0:LASTI, D:2 * D], -MAGIC,
                                                       None, ALU.add)
                    last.then_inc(s_fc, 1)
                round0(B // 2 - 1, 1, False, False)

        PLAN = (["a0", "a1", "p0", "p1", "sd", "xm", "xb", "x0", "x1"]
                + [f"{m}{ib}" for ib in range(NIB) for m in ("gate", "up")]
                + ["hm", "hb", "y0", "y1", "q_x0", "q_x1", "q0", "q1",
                   "o_a0", "o_a1", "o_p0", "o_p1", "m_x0", "m_x1", "rt", "ct", "b0", "b1"])
        U = {name: 10 + k for k, name in enumerate(PLAN)}
        HALVES = ["a0", "a1", "q_x0", "q_x1", "q0", "q1", "o_a0", "o_a1", "m_x0", "m_x1"]
        UH = {name: 8 + k for k, name in enumerate(HALVES)}

        def W(name):
            return wide[U[name] % 4]

        def pe_free(pe, name):
            pe.wait_ge(s_wf, U[name] - 3)

        def pe_attT(pe, kc, name):
            pe_free(pe, name)
            for b in range(B):
                o0 = 512 * (b // 4) + (b % 4) * T
                last = nc.tensor.transpose(W(name)[:, o0:o0 + T], aall[:, b, kc * P:(kc + 1) * P], ident[0:T, 0:T])
            last.then_inc(s_wd, 1)

        def act_attT(act, kc, name):
            act.wait_ge(s_wd, U[name] + 1)
            src = W(name).rearrange("p (a n) -> p a n", a=2)[:, :, 0:4 * T]
            nc.scalar.activation(aTh[:, kc, :].rearrange("p (a n) -> p a n", a=2), src, ACT.Copy).then_inc(s_wh, 1)

        def dve_attT(dve, kc, name):
            dve.wait_ge(s_wh, UH[name] + 1)
            src = W(name).rearrange("p (a n) -> p a n", a=2)[:, :, 0:4 * T]
            nc.vector.tensor_tensor(aTl[:, kc, :].rearrange("p (a n) -> p a n", a=2), src,
                                    aTh[:, kc, :].rearrange("p (a n) -> p a n", a=2), ALU.subtract).then_inc(s_wf, 1)

        def pe_out_proj(pe, l, names):
            for t, (t0, tn) in enumerate(TT):
                if t % 4 == 0:
                    pe_free(pe, names[t // 4])
                o0 = (t % 4) * D
                for kc in range(KC):
                    last = split3(pe, W(names[t // 4])[0:tn, o0:o0 + D], aTh[:, kc, t0:t0 + tn],
                                  aTl[:, kc, t0:t0 + tn], wph[:, l, kc, :], wpl[:, l, kc, :], kc == 0, kc == KC - 1)
                if t % 4 == 3 or t == FULL:
                    last.then_inc(s_wd, 1)

        def tile_groups(name0, name1):
            return [(name0, P, 0, 4), (name1, P, 4, FULL), (name1, LAST, FULL, NTILE)]

        def dve_residual(dve, names, scalar):
            for name, rows, t0, t1 in tile_groups(*names):
                dve.wait_ge(s_wd, U[name] + 1)
                o0 = (t0 % 4) * D
                ins = nc.vector.scalar_tensor_tensor(
                    out=xr[0:rows, t0:t1, :], in0=W(name)[0:rows, o0:o0 + (t1 - t0) * D].rearrange(
                        "p (t d) -> p t d", d=D), scalar=scalar[0:rows, :], in1=xr[0:rows, t0:t1, :],
                    op0=ALU.mult, op1=ALU.add)
                if t1 in (4, NTILE):
                    ins.then_inc(s_wf, 1)
                    dve.wait_ge(s_wf, U[name] + 1)
                else:
                    ins.then_inc(s_dve, 1)
                    step[0] += 1
                    dve.wait_ge(s_dve, step[0])

        def pe_max_bcast(pe, nm_, nb_, k):
            pe.wait_ge(s_am, k)
            pe_free(pe, nm_)
            nc.tensor.transpose(W(nm_)[0:1, 0:P], small[:, 2:3], ident[:, :]).then_inc(s_wd, 1)
            pe.wait_ge(s_wf, U[nm_] + 1)
            nc.tensor.matmul(W(nb_)[:, 0:1], ones[0:1, :], row1[:, :], start=True, stop=True).then_inc(s_wd, 1)

        def dve_max_bcast(dve, nm_, nb_, clip, col):
            dve.wait_ge(s_wd, U[nm_] + 1)
            nc.vector.tensor_reduce(row1[:, :], W(nm_)[0:1, 0:P], X, ALU.max).then_inc(s_wf, 1)
            dve.wait_ge(s_wd, U[nb_] + 1)
            nc.vector.tensor_scalar(small[:, col:col + 1], W(nb_)[:, 0:1], clip, None, ALU.mult).then_inc(s_wf, 1)
            dve.wait_ge(s_wf, U[nb_] + 1)
            nc.vector.reciprocal(small[:, col + 1:col + 2], small[:, col:col + 1]).then_inc(s_dve, 1)
            step[0] += 1
            dve.wait_ge(s_dve, step[0])


        es_a.close()
        es_f = es_att.enter_context(ExitStack())
        dgd = sb("dgd", [P, KC, P], F32, es_f)
        sdb = sb("sdb", [P, D], F32, es_f)
        th = [sb(f"th{k}", [P, NT], F32, es_f) for k in range(2)]
        hid = PTf[:, 0:3, :].rearrange("p c n -> p (c n)")[:, 0:NIB * NT].rearrange("p (i n) -> p i n", i=NIB)
        hq = sb("hq", [P, NIB, NT], F16, es_f)
        fac = sb("fac", [P, 4, NIB], F32, es_f)
        hmx = sb("hmx", [P, NIB], F32, es_f)
        s_am = sem("row_maxima_taken")
        s_sc = sem("scale_made")
        s_th = sem("tanh_made")
        s_hq = sem("hidden_rounded")
        s_hz = sem("hidden_in_fp16")
        s_xq = sem("rows_rounded")

        with nc.Block() as block:

            @block.gpsimd
            def _(pool):
                pool_rstd(pool, 1)

            @block.scalar
            def _(act):
                for kc in range(KC):
                    act_attT(act, kc, f"a{kc}")
                act.wait_ge(s_sc, 1)
                for ib in range(NIB):
                    n = P if ib < NIB - 1 else LASTI
                    act.wait_ge(s_wd, U[f"gate{ib}"] + 1)
                    if ib >= 2:
                        act.wait_ge(s_wf, U[f"up{ib - 2}"] + 1)
                    nc.scalar.activation(th[ib % 2][0:n, :], W(f"gate{ib}")[0:n, 0:NT], ACT.Tanh,
                                         scale=fac[0:n, 0, ib:ib + 1]).then_inc(s_th, 1)
                for ib in range(NIB):
                    n = P if ib < NIB - 1 else LASTI
                    act.wait_ge(s_hq, ib + 1)
                    nc.scalar.activation(hq[0:n, ib, :], hid[0:n, ib, :], ACT.Identity, bias=magic[0:n, 1:2]
                                         ).then_inc(s_hz, 1)

            @block.tensor
            def _(pe):
                for kc in range(KC):
                    pe_attT(pe, kc, f"a{kc}")
                pe.wait_ge(s_wf, U["a1"] + 1)
                pe_out_proj(pe, 0, ("p0", "p1"))
                pe.wait_ge(s_fm, 4)
                pe_free(pe, "sd")
                for k in range(KC):
                    last = nc.tensor.matmul(W("sd")[:, k * P:(k + 1) * P], ones[:, :], dgd[:, k, :],
                                            start=True, stop=True)
                last.then_inc(s_wd, 1)
                pe_max_bcast(pe, "xm", "xb", 1)
                pe.wait_ge(s_xq, 1)
                for kc in range(KC):
                    pe_free(pe, f"x{kc}")
                    transpose_rows(pe, U[f"x{kc}"], kc)
                pe.wait_ge(s_wf, U["x1"] + 1)
                for ib in range(NIB):
                    n = P if ib < NIB - 1 else LASTI
                    for m, wt in (("gate", wgT), ("up", wuT)):
                        name = f"{m}{ib}"
                        pe_free(pe, name)
                        for t0, t1 in ((0, WIDE0), (WIDE0, NT)):
                            for kc in range(KC):
                                last = nc.tensor.matmul(W(name)[0:n, t0:t1], wt[:, kc, ib * P:ib * P + n],
                                                        xTh[:, kc, t0:t1], start=(kc == 0), stop=(kc == KC - 1))
                        last.then_inc(s_wd, 1)
                pe_max_bcast(pe, "hm", "hb", 2)
                pe_free(pe, "y1")
                for ib in range(NIB):
                    n = P if ib < NIB - 1 else LASTI
                    pe.wait_ge(s_hz, ib + 1)
                    for t, (t0, tn) in enumerate(TT):
                        last = nc.tensor.matmul(W(f"y{t // 4}")[0:tn, (t % 4) * D:(t % 4 + 1) * D],
                                                hq[0:n, ib, t0:t0 + tn], wdT[0:n, ib, :],
                                                start=(ib == 0 and t % 2 == 0), stop=(ib == NIB - 1),
                                                skip_group_check=True)
                        if ib == NIB - 1 and t in (3, FULL):
                            last.then_inc(s_wd, 1)

            @block.vector
            def _(dve):
                def link(ins):
                    ins.then_inc(s_dve, 1)
                    step[0] += 1
                    dve.wait_ge(s_dve, step[0])

                link(nc.vector.memset(small[:, :], 0.0))
                for kc in range(KC):
                    dve_attT(dve, kc, f"a{kc}")
                for k in range(KC):
                    last = nc.vector.tensor_scalar(dgd[:, k, :], ident[:, :], wm[:, 2 * NIB + k:2 * NIB + k + 1], None,
                                                   ALU.mult)
                last.then_inc(s_fm, 1)
                dve_residual(dve, ("p0", "p1"), tgs[:, 0:1])
                layernorm_stats(dve)
                layernorm_rows(dve, 1)
                dve.wait_ge(s_xn, 2 * NTILE)
                nc.vector.tensor_reduce(small[:, 2:3], xn[:, :, :], XY, ALU.max, apply_absolute_value=True
                                        ).then_inc(s_am, 1)
                dve.wait_ge(s_wd, U["sd"] + 1)
                nc.vector.tensor_copy(sdb[:, :], W("sd")[:, 0:D]).then_inc(s_wf, 1)
                dve_max_bcast(dve, "xm", "xb", clipt[:, 0:1], 4)
                link(nc.vector.tensor_scalar(xn[:, :, :], xn[:, :, :], small[:, 5:6], MAGIC, ALU.mult, ALU.add))
                nc.vector.tensor_scalar(xn[:, :, :], xn[:, :, :], MAGIC + QMAX, MAGIC - QMAX - 1.0, ALU.min, ALU.max
                                        ).then_inc(s_xq, 1)
                link(nc.vector.tensor_scalar(fac[:, 0, :], wm[:, 0:NIB], small[:, 4:5], 0.5, ALU.mult, ALU.mult))
                nc.vector.tensor_scalar(fac[:, 1, :], wm[:, NIB:2 * NIB], small[:, 4:5], None, ALU.mult).then_inc(s_sc, 1)
                dve.wait_ge(s_sc, 1)
                link(nc.vector.tensor_tensor(fac[:, 2, :], fac[:, 0, :], fac[:, 1, :], ALU.mult))
                for kc in range(KC):
                    dve.wait_ge(s_wd, U[f"x{kc}"] + 1)
                    nc.vector.tensor_scalar(xTh[:, kc, :], W(f"x{kc}")[:, 0:NT], -MAGIC, None, ALU.add).then_inc(s_wf, 1)
                link(nc.vector.memset(hmx[:, :], 0.0))
                for ib in range(NIB):
                    n = P if ib < NIB - 1 else LASTI
                    dve.wait_ge(s_th, ib + 1)
                    nc.vector.scalar_tensor_tensor(out=hid[0:n, ib, :], in0=th[ib % 2][0:n, :], scalar=1.0,
                                                   in1=W(f"gate{ib}")[0:n, 0:NT], op0=ALU.add, op1=ALU.mult
                                                   ).then_inc(s_wf, 1)
                    dve.wait_ge(s_wf, U[f"gate{ib}"] + 1)
                    dve.wait_ge(s_wd, U[f"up{ib}"] + 1)
                    nc.vector.scalar_tensor_tensor(out=hid[0:n, ib, :], in0=hid[0:n, ib, :],
                                                   scalar=fac[0:n, 2, ib:ib + 1], in1=W(f"up{ib}")[0:n, 0:NT],
                                                   op0=ALU.mult, op1=ALU.mult).then_inc(s_wf, 1)
                    dve.wait_ge(s_wf, U[f"up{ib}"] + 1)
                    link(nc.vector.tensor_reduce(hmx[0:n, ib:ib + 1], hid[0:n, ib, :], X, ALU.max,
                                                 apply_absolute_value=True))
                nc.vector.tensor_reduce(small[:, 2:3], hmx[:, :], X, ALU.max).then_inc(s_am, 1)
                dve_max_bcast(dve, "hm", "hb", clipt[:, 1:2], 6)
                for ib in range(NIB):
                    n = P if ib < NIB - 1 else LASTI
                    link(nc.vector.tensor_scalar(hid[0:n, ib, :], hid[0:n, ib, :], small[0:n, 7:8], MAGIC,
                                                 ALU.mult, ALU.add))
                    nc.vector.tensor_scalar(hid[0:n, ib, :], hid[0:n, ib, :], MAGIC + QMAX, MAGIC - QMAX - 1.0,
                                            ALU.min, ALU.max).then_inc(s_hq, 1)
                link(nc.vector.tensor_scalar(sdb[:, :], sdb[:, :], small[:, 6:7], tg[:, 2:3], ALU.mult, ALU.mult))
                for name, rows, t0, t1 in tile_groups("y0", "y1"):
                    dve.wait_ge(s_wd, U[name] + 1)
                    o0 = (t0 % 4) * D
                    ins = nc.vector.tensor_tensor(
                        xn[0:rows, t0:t1, :], W(name)[0:rows, o0:o0 + (t1 - t0) * D].rearrange("p (t d) -> p t d", d=D),
                        sdb[0:rows, :].unsqueeze(1).to_broadcast([rows, t1 - t0, D]), ALU.mult)
                    if t1 in (4, NTILE):
                        ins.then_inc(s_wf, 1)
                        dve.wait_ge(s_wf, U[name] + 1)
                    else:
                        link(ins)
                    link(nc.vector.tensor_tensor(xr[0:rows, t0:t1, :], xr[0:rows, t0:t1, :], xn[0:rows, t0:t1, :],
                                                 ALU.add))

        es_f.close()
        es_m = es_att.enter_context(ExitStack())
        w1r = share[:, 0:KC * DF].rearrange("p (k n) -> p k n", k=KC)
        w2r = share[:, KC * DF:KC * DF + FC * D].rearrange("p (f n) -> p f n", f=FC)
        w1h = [sb(f"w1h{p}", [P, KC, FC, P], F16, es_m) for p in range(2)]
        w1l = [sb(f"w1l{p}", [P, KC, FC, P], F16, es_m) for p in range(2)]
        w2h = [sb(f"w2h{p}", [P, FC, D], F16, es_m) for p in range(2)]
        w2l = [sb(f"w2l{p}", [P, FC, D], F16, es_m) for p in range(2)]
        s_w1 = sem("expert_w1_loaded")
        s_w2 = sem("expert_w2_loaded")
        s_w1h = sem("expert_w1_high_half")
        s_w2h = sem("expert_w2_high_half")
        s_w1l = sem("expert_w1_split")
        s_w2l = sem("expert_w2_split")
        SMN, STN, NBN = H * B, 16 * B, B
        MN = 80
        SMH1 = [2, 2, 2, 2, 2, 2, 2, 2, 0, 0, 0, 0]
        NSTEP1 = 8
        PVL1 = [2, 1, 1, 0, 0, 0, 0, 0, 0, 0, 0, 0]
        PVH1 = [0, 0, 0, 1, 2, 1, 1, 2, 1, 1, 2, 1]
        NTURN1 = 4
        NST1 = 12
        QB = 16 * 8

        def sp_w1(sp, e):
            sp.dma_start(w1r[:, :, :], w1[bass.ds(e, 1)].rearrange("e (k p) n -> p (e k) n", p=P)).then_inc(s_w1, 16)

        def sp_w2(sp, e):
            sp.dma_start(w2r[:, :, :], w2[bass.ds(e, 1)].rearrange("e (p f) n -> p (e f) n", f=FC)).then_inc(s_w2, 16)

        def act_w1(act, e, p):
            act.wait_ge(s_w1, 16 * (e + 1))
            nc.scalar.activation(w1h[p][:, :, :, :], w1r[:, :, :].rearrange("p k (m c) -> p k c m", c=FC), ACT.Copy,
                                 scale=WS).then_inc(s_w1h, 1)

        def act_w2(act, e, p):
            act.wait_ge(s_w2, 16 * (e + 1))
            nc.scalar.activation(w2h[p][:, :, :].rearrange("p c n -> p (c n)"), w2r[:, :, :].rearrange("p c n -> p (c n)"),
                                 ACT.Copy, scale=WS).then_inc(s_w2h, 1)

        def dve_w1(dve, e, p):
            dve.wait_ge(s_w1h, e + 1)
            for k in range(KC):
                last = nc.vector.scalar_tensor_tensor(
                    out=w1l[p][:, k, :, :], in0=w1r[:, k, :].rearrange("p (m c) -> p c m", c=FC), scalar=WS,
                    in1=w1h[p][:, k, :, :], op0=ALU.mult, op1=ALU.subtract)
            last.then_inc(s_w1l, 1)

        def dve_w2(dve, e, p):
            dve.wait_ge(s_w2h, e + 1)
            nc.vector.scalar_tensor_tensor(out=w2l[p][:, :, :].rearrange("p c n -> p (c n)"),
                                           in0=w2r[:, :, :].rearrange("p c n -> p (c n)"), scalar=WS,
                                           in1=w2h[p][:, :, :].rearrange("p c n -> p (c n)"), op0=ALU.mult,
                                           op1=ALU.subtract).then_inc(s_w2l, 1)

        with nc.Block() as block:

            @block.sync
            def _(sp):
                for o in range(2):
                    for mb in range(KC):
                        sp_stack1(sp, 0, o, mb, queries=False)
                sp_w1(sp, 0)
                sp_w2(sp, 0)
                sp.dma_start(Vc[0][:, :, :, 0:VW].rearrange("p c h v -> p (c h) v"),
                             v1_dram[0].rearrange("p (n v) -> p n v", v=VW)).then_inc(s_vc[0], 16)
                for mb in range(KC):
                    sp.wait_ge(s_wf, U[f"q{mb}"] + 1)
                    sp_halves_out(sp, q_dram, (qh, ql), mb, QSLOTS, s_qw)
                sp.wait_ge(s_qw, QB + 16 * 4)
                for o in range(2):
                    for mb in range(KC):
                        sp_stack1(sp, 0, o, mb, keys=False)
                sp.wait_ge(s_mf, MN + 1)
                sp.dma_start(QS[0][KROWS:KROWS + 1, :, :], nm[0][:, :]).then_inc(s_nm[0], 16)
                sp.wait_ge(s_w1l, 1)
                sp_w1(sp, 1)

                def round1(j, u, keys, nxt):
                    p = u % 2
                    i = 2 * j + u
                    if nxt:
                        sp.wait_ge(s_std, STN + NST1 * i + 6)
                        sp.dma_start(Vc[1 - p][:, :, :, 0:VW].rearrange("p c h v -> p (c h) v"),
                                     v1_dram[bass.ds(i + 1, 1)].rearrange("b p (n v) -> (b p) n v", v=VW)
                                     ).then_inc(s_vc[1 - p], 16)
                    if keys:
                        sp_stack1(sp, j, u + 2, 0)
                    if nxt:
                        sp.wait_ge(s_mf, MN + i + 2)
                        sp.dma_start(QS[1 - p][KROWS:KROWS + 1, :, :], nm[1 - p][:, :]).then_inc(s_nm[1 - p], 16)
                    if keys:
                        sp.wait_ge(s_std, STN + NST1 * (i + 1))
                        sp_stack1(sp, j, u + 2, 1)

                with sp.Fori(0, B // 2 - 1) as j:
                    for u in range(2):
                        round1(j, u, True, True)
                round1(B // 2 - 1, 0, False, True)

            @block.gpsimd
            def _(pool):
                pool_rstd(pool, 2)

            @block.scalar
            def _(act):
                for kc in range(KC):
                    wide_hi(act, U[f"q_x{kc}"], xTh[:, kc, :])
                for mb in range(KC):
                    wide_hi(act, U[f"q{mb}"], qh[:, mb, :], bcol[:, 4, mb:mb + 1])
                act_w1(act, 0, 0)
                act_w2(act, 0, 0)

                def round1(j, o, first):
                    for t in range(NST1):
                        act_exp(act, j, o, t, 1, STN)
                        if t == NTURN1 - 1 and not first:
                            act_evac(act, j, o - 1, NBN)

                round1(0, 0, True)
                with act.Fori(0, B // 2 - 1) as j:
                    for o in (1, 2):
                        round1(j, o, False)
                round1(B // 2 - 1, 1, False)
                act_evac(act, B // 2 - 1, 1, NBN)
                act_w1(act, 1, 1)

            @block.tensor
            def _(pe):
                for kc in range(KC):
                    pe_free(pe, f"q_x{kc}")
                    transpose_rows(pe, U[f"q_x{kc}"], kc, 2)
                pe.wait_ge(s_wf, U["q_x1"] + 1)
                for mb in range(KC):
                    pe_free(pe, f"q{mb}")
                    project_T(pe, U[f"q{mb}"], w1kh[:, 1], w1kl[:, 1], mb)
                pe.wait_ge(s_wf, U["q1"] + 1)
                for h in range(H):
                    pe_SM(pe, 0, 0, h, 1, SMN)
                pe_N(pe, 0, 0, SMN, MN, MN)

                def round1(j, o, first, nxt):
                    i = 2 * j + o
                    h = hv = 0
                    hl = sum(PVH1)
                    for t in range(NST1):
                        pe_ST(pe, j, o, t, 1, STN, 16 * (B // 2))
                        if not first:
                            for _ in range(PVL1[t]):
                                pe_PV(pe, j, o - 1, hl, 1, STN, 0, NBN)
                                hl += 1
                            if t == NTURN1:
                                pe_turn(pe, j, o - 1, NBN)
                        if nxt:
                            for _ in range(SMH1[t]):
                                pe_SM(pe, j, o + 1, h, 1, SMN)
                                h += 1
                            if t == NSTEP1:
                                pe_N(pe, j, o + 1, SMN, MN + i + 1, MN + i + 1)
                        for _ in range(PVH1[t]):
                            pe_PV(pe, j, o, hv, 1, STN, 0, NBN)
                            hv += 1

                round1(0, 0, True, True)
                with pe.Fori(0, B // 2 - 1) as j:
                    for o in (1, 2):
                        round1(j, o, False, True)
                round1(B // 2 - 1, 1, False, False)
                for h in range(sum(PVH1), H):
                    pe_PV(pe, B // 2 - 1, 1, h, 1, STN, 0, NBN)
                pe_turn(pe, B // 2 - 1, 1, NBN)

            @block.vector
            def _(dve):
                layernorm_stats(dve)
                layernorm_rows(dve, 2)
                for kc in range(KC):
                    wide_lo(dve, U[f"q_x{kc}"], xTh[:, kc, :], xTl[:, kc, :], None, UH[f"q_x{kc}"])
                for mb in range(KC):
                    wide_lo(dve, U[f"q{mb}"], qh[:, mb, :], ql[:, mb, :], bcol[:, 4, mb:mb + 1], UH[f"q{mb}"])
                nc.vector.memset(KS[0][KROWS:KROWS + 1, :, 0:TC], WS * WS)
                for h in range(H):
                    dve_max(dve, 0, 0, h, 1, SMN)
                dve_N(dve, 0, 0, MN)
                dve_w1(dve, 0, 0)
                dve_w2(dve, 0, 0)

                def round1(j, o, first, nxt):
                    i = 2 * j + o
                    for h in range(H):
                        if nxt:
                            dve_max(dve, j, o + 1, h, 1, SMN)
                        if h == 7 and not first:
                            dve_norm(dve, j, o - 1, NBN)
                    if nxt:
                        dve_N(dve, j, o + 1, MN + i + 1)

                round1(0, 0, True, True)
                with dve.Fori(0, B // 2 - 1) as j:
                    for o in (1, 2):
                        round1(j, o, False, True)
                round1(B // 2 - 1, 1, False, False)
                dve_norm(dve, B // 2 - 1, 1, NBN)
                dve_w1(dve, 1, 1)

        lg = sb("lg", [P, NTILE, E])
        sc = sb("sc", [P, NTILE, E])
        rk = sb("rk", [P, NTILE, E])
        red = sb("red", [P, NTILE])
        cmp_ = sb("cmp", [P, NTILE, E, E])
        eqq = sb("eqq", [P, NTILE, E, E])
        low = sb("low", [P, E, E])
        cs = sb("cs", [P, NTILE, E])
        cT = xn[0:E, :, :].rearrange("p t d -> p (t d)")[:, 0:NT]
        hA = PTf.rearrange("p c n -> p (c n)").bitcast(F16)
        hB = KSa[:, :, :, :].rearrange("p a h s -> p (a h s)")
        hTh, hTl = ([h_[:, k * FC * NT:(k + 1) * FC * NT].rearrange("p (f n) -> p f n", f=FC) for h_ in (hA, hB)]
                    for k in range(2))
        af = aallw[:, :, :].rearrange("p b d -> p (b d)")
        rr = [af[:, 0:NT], af[:, NT:2 * NT], qh[:, :, :].rearrange("p k n -> p (k n)").bitcast(F32)]
        YR = 4
        YB = 3
        s_ex = sem("logits_through_exp")
        s_lg = sem("logits_ready")
        s_low = sem("order_mask_made")
        s_cb = sem("router_done")
        s_hd = sem("hidden_product_done")
        s_r = sem("hidden_through_relu")
        s_hh = sem("hidden_high_half")
        s_hl = sem("hidden_split")
        s_yd = sem("expert_product_done")
        s_ya = sem("expert_product_added")
        s_acc = sem("residual_ready")

        with nc.Block() as block:

            @block.sync
            def _(sp):
                def round_w(e, first, second):
                    if first:
                        sp.wait_ge(s_w1l, e + 2)
                        sp_w1(sp, e + 2)
                    if second:
                        sp.wait_ge(s_w2l, e + 1)
                        sp_w2(sp, e + 1)

                with sp.Fori(0, E // 2 - 1) as j:
                    for u in range(2):
                        round_w(2 * j + u, True, True)
                round_w(E - 2, False, True)
                for t, (t0, tn) in enumerate(TT):
                    sp.wait_ge(s_ya, YB + NTILE * (E - 1) + t + 1)
                    sp.dma_start(of[t0:t0 + tn, :], xr[0:tn, t, :]).then_inc(s_out, 16)
                sp.wait_ge(s_out, 16 * NTILE)

            @block.gpsimd
            def _(pool):
                nc.gpsimd.memset(low[:, :, :], 1.0).then_inc(s_low, 1)
                pool.wait_ge(s_low, 1)
                nc.gpsimd.affine_select(out=low[:, :, :], in_=low[:, :, :], compare_op=ALU.is_gt, fill=0.0, base=0,
                                        pattern=[[1, E], [-1, E]], channel_multiplier=0).then_inc(s_low, 1)
                pool_rstd(pool, 3)

                def lows(j, u, n0):
                    for f in range(FC):
                        n = n0 + f
                        pool.wait_ge(s_hh, n + 1)
                        nc.gpsimd.tensor_tensor(hTl[u][:, f, :], rr[f % 3][:, :], hTh[u][:, f, :], ALU.subtract
                                                ).then_inc(s_hl, 1)

                with pool.Fori(0, E // 2) as j:
                    for u in range(2):
                        lows(j, u, FC * (2 * j + u))

            @block.scalar
            def _(act):
                for kc in range(KC):
                    act_attT(act, kc, f"o_a{kc}")
                for kc in range(KC):
                    wide_hi(act, U[f"m_x{kc}"], xTh[:, kc, :])
                act.wait_ge(s_lg, 1)
                nc.scalar.activation(sc[:, :, :], lg[:, :, :], ACT.Exp).then_inc(s_ex, 1)

                def highs(e, q):
                    for f in range(FC):
                        act.wait_ge(s_r, FC * e + f + 1)
                        nc.scalar.activation(hTh[q][:, f, :], rr[f % 3][:, :], ACT.Copy).then_inc(s_hh, 1)

                highs(0, 0)
                with act.Fori(0, E // 2 - 1) as j:
                    for u in range(2):
                        highs(2 * j + u + 1, 1 - u)
                        act_w1(act, 2 * j + u + 2, u)
                        act_w2(act, 2 * j + u + 1, 1 - u)
                highs(E - 1, 1)
                act_w2(act, E - 1, 1)

            @block.tensor
            def _(pe):
                for kc in range(KC):
                    pe_attT(pe, kc, f"o_a{kc}")
                pe.wait_ge(s_wf, U["o_a1"] + 1)
                pe_out_proj(pe, 1, ("o_p0", "o_p1"))
                for kc in range(KC):
                    pe_free(pe, f"m_x{kc}")
                    transpose_rows(pe, U[f"m_x{kc}"], kc, 3)
                pe.wait_ge(s_wf, U["m_x1"] + 1)
                pe_free(pe, "rt")
                for t, (t0, tn) in enumerate(TT):
                    for kc in range(KC):
                        last = split3(pe, W("rt")[0:tn, t * E:(t + 1) * E], xTh[:, kc, t0:t0 + tn],
                                      xTl[:, kc, t0:t0 + tn], gwh[:, kc, :], gwl[:, kc, :], kc == 0, kc == KC - 1)
                last.then_inc(s_wd, 1)
                pe.wait_ge(s_cb, 1)
                pe_free(pe, "ct")
                for t, (t0, tn) in enumerate(TT):
                    last = nc.tensor.transpose(W("ct")[0:E, t0:t0 + tn], rk[0:tn, t, :], ident[0:tn, 0:tn])
                last.then_inc(s_wd, 1)
                pe.wait_ge(s_wf, U["ct"] + 1)
                for t, (t0, tn) in enumerate(TT):
                    if t % 4 == 0:
                        pe_free(pe, f"b{t // 4}")
                    last = nc.tensor.matmul(W(f"b{t // 4}")[0:tn, (t % 4) * D:(t % 4 + 1) * D], cT[:, t0:t0 + tn],
                                            b2r[:, :], start=True, stop=True)
                    if t in (3, FULL):
                        last.then_inc(s_wd, 1)
                pe.wait_ge(s_wf, U["b1"] + 1)

                def hidden(e, q):
                    pe.wait_ge(s_w1l, e + 1)
                    for f in range(FC):
                        n = FC * e + f
                        if not (isinstance(n, int) and n < 2):
                            pe.wait_ge(s_r, n - 1)
                        for kc in range(KC):
                            for lh, rhs in ((w1h[q], xTh), (w1h[q], xTl), (w1l[q], xTh)):
                                for t0, t1 in ((0, WIDE0), (WIDE0, NT)):
                                    last = nc.tensor.matmul(
                                        wide[f % 2][:, t0:t1], lh[:, kc, f, :], rhs[:, kc, t0:t1],
                                        start=(kc == 0 and lh is w1h[q] and rhs is xTh),
                                        stop=(kc == KC - 1 and lh is w1l[q]))
                        last.then_inc(s_hd, 1)

                def outcome(e, q):
                    pe.wait_ge(s_hl, FC * (e + 1))
                    pe.wait_ge(s_w2l, e + 1)
                    for t, (t0, tn) in enumerate(TT):
                        n = NTILE * e + t
                        pe.wait_ge(s_ya, n - (YR if t >= YR else NTILE - YR) + 1 + YB)
                        bank = PS[0:tn, 4 + t % YR, 0:D]
                        for f in range(FC):
                            last = split3(pe, bank, hTh[q][:, f, t0:t0 + tn], hTl[q][:, f, t0:t0 + tn],
                                          w2h[q][:, f, :], w2l[q][:, f, :], f == 0, f == FC - 1)
                        last.then_inc(s_yd, 1)

                hidden(0, 0)
                with pe.Fori(0, E // 2 - 1) as j:
                    for u in range(2):
                        hidden(2 * j + u + 1, 1 - u)
                        outcome(2 * j + u, u)
                hidden(E - 1, 1)
                outcome(E - 2, 0)
                outcome(E - 1, 1)

            @block.vector
            def _(dve):
                def link(ins):
                    ins.then_inc(s_dve, 1)
                    step[0] += 1
                    dve.wait_ge(s_dve, step[0])

                dve_bias_in(dve, 1)
                for kc in range(KC):
                    dve_attT(dve, kc, f"o_a{kc}")
                dve_residual(dve, ("o_p0", "o_p1"), tgs[:, 1:2])
                layernorm_stats(dve)
                layernorm_rows(dve, 3)
                for kc in range(KC):
                    wide_lo(dve, U[f"m_x{kc}"], xTh[:, kc, :], xTl[:, kc, :], None, UH[f"m_x{kc}"])
                link(nc.vector.memset(lg[:, :, :], 0.0))
                dve.wait_ge(s_wd, U["rt"] + 1)
                for rows, t0, t1 in ((P, 0, FULL), (LAST, FULL, NTILE)):
                    ins = nc.vector.scalar_tensor_tensor(
                        out=lg[0:rows, t0:t1, :], in0=W("rt")[0:rows, t0 * E:t1 * E].rearrange("p (t e) -> p t e", e=E),
                        scalar=1.0 / WS, in1=gbr[0:rows, :].unsqueeze(1).to_broadcast([rows, t1 - t0, E]),
                        op0=ALU.mult, op1=ALU.add)
                ins.then_inc(s_wf, 1)
                dve.wait_ge(s_wf, U["rt"] + 1)
                bc = [P, NTILE, E]
                link(nc.vector.tensor_reduce(red[:, :], lg[:, :, :], X, ALU.max))
                nc.vector.tensor_tensor(lg[:, :, :], lg[:, :, :], red[:, :].unsqueeze(2).to_broadcast(bc),
                                        ALU.subtract).then_inc(s_lg, 1)
                dve.wait_ge(s_ex, 1)
                link(nc.vector.tensor_reduce(red[:, :], sc[:, :, :], X, ALU.add))
                link(nc.vector.reciprocal(red[:, :], red[:, :]))
                link(nc.vector.tensor_tensor(sc[:, :, :], sc[:, :, :], red[:, :].unsqueeze(2).to_broadcast(bc), ALU.mult))
                b4 = [P, NTILE, E, E]
                other, own = sc[:, :, :].unsqueeze(2).to_broadcast(b4), sc[:, :, :].unsqueeze(3).to_broadcast(b4)
                nc.vector.tensor_tensor(cmp_[:, :, :, :], other, own, ALU.is_gt)
                link(nc.vector.tensor_tensor(eqq[:, :, :, :], other, own, ALU.is_equal))
                dve.wait_ge(s_low, 2)
                link(nc.vector.tensor_tensor(eqq[:, :, :, :], eqq[:, :, :, :],
                                             low[:, :, :].unsqueeze(1).to_broadcast(b4), ALU.mult))
                link(nc.vector.tensor_tensor(cmp_[:, :, :, :], cmp_[:, :, :, :], eqq[:, :, :, :], ALU.add))
                link(nc.vector.tensor_reduce(rk[:, :, :], cmp_[:, :, :, :], X, ALU.add))
                link(nc.vector.tensor_scalar(rk[:, :, :], rk[:, :, :], 2.0, None, ALU.is_lt))
                link(nc.vector.tensor_tensor(rk[:, :, :], rk[:, :, :], sc[:, :, :], ALU.mult))
                nc.vector.tensor_scalar(rk[:, :, :], rk[:, :, :], tg[:, 3:4], None, ALU.mult).then_inc(s_cb, 1)
                dve.wait_ge(s_cb, 1)
                nc.vector.tensor_scalar(cs[:, :, :], rk[:, :, :], 1.0 / (WS * WS), None, ALU.mult)
                dve.wait_ge(s_wd, U["ct"] + 1)
                nc.vector.tensor_copy(cT[:, :], W("ct")[0:E, 0:NT]).then_inc(s_wf, 1)
                dve.wait_ge(s_wf, U["ct"] + 1)
                dve_residual(dve, ("b0", "b1"), ones[:, 0:1])
                nc.vector.tensor_copy(small[:, 0:1], small[:, 1:2]).then_inc(s_ya, YB)

                def relus(e, q):
                    for f in range(FC):
                        n = FC * e + f
                        dve.wait_ge(s_hd, n + 1)
                        if not (isinstance(n, int) and n < 3):
                            dve.wait_ge(s_hl, n - 1 if f < 2 else n - 2)
                        nc.vector.tensor_scalar(rr[f % 3][:, :], wide[f % 2][:, 0:NT], b1c[:, bass.ds(e, 1), f], 0.0,
                                                ALU.add, ALU.max).then_inc(s_r, 1)

                def adds(e, q, nw1, nw2):
                    for t, (t0, tn) in enumerate(TT):
                        n = NTILE * e + t
                        if t == 1 and nw1:
                            dve_w1(dve, e + 2, q)
                        if t == 4 and nw2:
                            dve_w2(dve, e + 1, 1 - q)
                        dve.wait_ge(s_yd, n + 1)
                        nc.vector.scalar_tensor_tensor(out=xr[0:tn, t, :], in0=PS[0:tn, 4 + t % YR, 0:D],
                                                       scalar=cs[0:tn, t, bass.ds(e, 1)], in1=xr[0:tn, t, :],
                                                       op0=ALU.mult, op1=ALU.add).then_inc(s_ya, 1)

                relus(0, 0)
                with dve.Fori(0, E // 2 - 1) as j:
                    for u in range(2):
                        relus(2 * j + u + 1, 1 - u)
                        adds(2 * j + u, u, True, True)
                relus(E - 1, 1)
                adds(E - 2, 0, False, True)
                adds(E - 1, 1, False, False)


_INS = ['x', 'ctx_1024', 'g_xattn', 'g_ffn', 'L0_xattn_w_ref', 'L0_xattn_b_ref', 'L0_xattn_w_attn',
        'L0_xattn_b_attn', 'L0_xattn_w_proj', 'L0_xattn_b_proj', 'L0_ffn_clip_x', 'L0_ffn_clip_down',
        'L0_ffn_w_gate', 'L0_ffn_w_up', 'L0_ffn_w_down', 'L1_xattn_w_q', 'L1_xattn_b_q', 'L1_xattn_w_k',
        'L1_xattn_b_k', 'L1_xattn_w_v', 'L1_xattn_b_v', 'L1_xattn_w_o', 'L1_xattn_b_o', 'L1_ffn_gate_w',
        'L1_ffn_gate_b', 'L1_ffn_w1', 'L1_ffn_b1', 'L1_ffn_w2', 'L1_ffn_b2']


def kernel(**inputs):
    import numpy as _np
    import concourse.bacc as _bacc
    from concourse import mybir as _mybir
    from concourse.bass_utils import run_bass_kernel_spmd as _run

    nc = _bacc.Bacc("TRN2", target_bir_lowering=False, num_devices=1)
    arrays, args = {}, []
    for name in _INS:
        a = _np.ascontiguousarray(inputs[name])
        arrays[f"in_{name}_dram"] = a
        args.append(nc.dram_tensor(f"in_{name}_dram", a.shape, _mybir.dt.from_np(a.dtype), kind="ExternalInput").ap())
    dt = _mybir.dt.from_np(_np.dtype("float32"))
    args.append(nc.dram_tensor("out_0_dram", inputs["x"].shape, dt, kind="ExternalOutput").ap())
    flamingo(nc, *args)
    r = _run(nc, [arrays], core_ids=[0])
    return r.results[0]["out_0_dram"]
```

```python
from contextlib import ExitStack

import concourse.bass as bass
from concourse import mybir

ALU = mybir.AluOpType
ACT = mybir.ActivationFunctionType
F32 = mybir.dt.float32
F16 = mybir.dt.float16
X = mybir.AxisListType.X
XY = mybir.AxisListType.XY

P = 128
WS = 16.0
MAGIC = 12582912.0
EPS = 1e-5
QMAX = 127.0
BIG = 1e30


def flamingo(nc, x, ctx_seq, g_xattn, g_ffn,
             w_ref, b_ref, w_attn, b_attn, w_proj, b_proj,
             clip_x, clip_down, w_gate, w_up, w_down,
             w_q, b_q, w_k, b_k, w_v, b_v, w_o, b_o,
             gate_w, gate_b, w1, b1, w2, b2, out):
    B, T, D = x.shape
    TC = ctx_seq.shape[1]
    NT = B * T
    H = 16
    DH = D // H
    KC = D // P
    NTILE = -(-NT // P)
    LAST = NT - (NTILE - 1) * P
    FULL = NTILE - 1
    S0 = T + TC
    NI = w_gate.shape[0]
    NIB = -(-NI // P)
    LASTI = NI - (NIB - 1) * P
    E = w1.shape[0]
    DF = w1.shape[2]
    FC = DF // P
    CH = -(-TC // 3)
    CSZ = [CH, (TC - CH) // 2, (TC - CH) // 2]
    COFF = [0, CSZ[0], CSZ[0] + CSZ[1]]
    KROWS = 4 * DH
    SCALE = DH ** -0.5 / (WS * WS)
    CTX_BIAS = -2.0
    VW = DH + 1
    HM = H // 2
    HG = 4
    GW = HG * VW
    VS = GW + VW
    WIDE0 = 512
    TT = [(t * P, P if t < FULL else LAST) for t in range(NTILE)]
    xf = x.rearrange("b t d -> (b t) d")
    of = out.rearrange("b t d -> (b t) d")

    q_dram = nc.dram_tensor("q_scratch", (H, DH, 4, NT), F16, kind="Internal").ap()
    sk_dram = nc.dram_tensor("own_key_scratch", (H, DH, 4, NT), F16, kind="Internal").ap()
    k_dram = [nc.dram_tensor(f"k{l}_scratch", (B, H, DH, 4, TC), F16, kind="Internal").ap() for l in range(2)]
    g_dram = nc.dram_tensor("shares_scratch", (E, NT), F32, kind="Internal").ap()
    v1_dram = nc.dram_tensor("v1_scratch", (B, CH, 3 * H * VW), F32, kind="Internal").ap()

    top = ExitStack()
    with top:
        def sb(name, shape, dt=F32, es=top):
            return es.enter_context(nc.sbuf_tensor(name, shape, dt))

        def sem(name):
            return top.enter_context(nc.semaphore(name))

        PS = top.enter_context(nc.psum_tensor("PS", [P, 8, 512], F32))
        wide = [PS[:, 2 * w:2 * w + 2, :].rearrange("p a n -> p (a n)") for w in range(4)]
        sm_bank = [PS[:, 0, :], PS[:, 1, :]]
        st_bank = [PS[:, 2, :], PS[:, 3, :]]
        pv_bank = [PS[:, 4, :], PS[:, 5, :]]
        misc = [PS[:, 5, :], PS[:, 6, :], PS[:, 7, :]]

        xr = sb("xr", [P, NTILE, D])
        xn = sb("xn", [P, NTILE, D])
        xTh = sb("xTh", [P, KC, NT], F16)
        xTl = sb("xTl", [P, KC, NT], F16)
        ident = sb("ident", [P, P])
        ones = sb("ones", [P, P])
        stats = sb("stats", [P, NTILE, 6])
        mv = sb("mv", [P, NTILE, 2])
        veps = sb("veps", [P, NTILE])
        rstd = sb("rstd", [P, NTILE])
        mhalf = sb("mhalf", [P, NTILE])
        gts = sb("gts", [P, 4])
        tg = sb("tg", [P, 4])
        tgs = sb("tgs", [P, 4])
        clips = sb("clips", [P, 2])
        clipt = sb("clipt", [P, 2])
        bcol = sb("bcol", [P, 5, 2])
        brow = sb("brow", [P, 3, D])
        bpr = sb("bpr", [P, 2, D])
        gbr = sb("gbr", [P, E])
        b1c = sb("b1c", [P, E, FC])
        b2r = sb("b2r", [E, D])
        gwr = sb("gwr", [P, KC, E])
        gwh = sb("gwh", [P, KC, E], F16)
        gwl = sb("gwl", [P, KC, E], F16)
        wph = sb("wph", [P, 2, KC, D], F16)
        wpl = sb("wpl", [P, 2, KC, D], F16)
        w1kh = sb("w1kh", [P, 2, KC, D], F16)
        w1kl = sb("w1kl", [P, 2, KC, D], F16)
        aTh = sb("aTh", [P, KC, NT], F16)
        aTl = sb("aTl", [P, KC, NT], F16)
        magic = sb("magic", [P, 2])
        small = sb("small", [P, 8])
        row1 = sb("row1", [1, 1])

        s_x = sem("x_loaded")
        s_pad = sem("padding_cleared")
        s_bias = sem("biases_loaded")
        s_small = sem("small_inputs_loaded")
        s_biasp = sem("biases_scaled")
        s_wr = [sem(f"raw_weights_loaded{k}") for k in range(4)]
        s_const = sem("constants_made")
        s_zero = sem("values_padding_cleared")
        s_tanh = sem("gates_through_tanh")
        s_dve = sem("vector_step")
        s_var = sem("variances_taken")
        s_rstd = sem("rstd_made")
        s_xn = sem("rows_normalised")
        s_wh8 = sem("raw_weights_high_half")
        s_split = sem("weights_split")
        s_wd = sem("wide_product_done")
        s_wh = sem("wide_high_half_done")
        s_wf = sem("wide_tile_freed")
        s_ctx = [sem(f"context_loaded{p}") for p in range(2)]
        s_md = sem("misc_product_done")
        s_mh = sem("misc_high_half_done")
        s_mf = sem("misc_bank_freed")
        s_smd = sem("score_rows_done")
        s_smf = sem("score_max_taken")
        s_rb = sem("score_rows_met")
        s_std = sem("score_columns_done")
        s_exp = sem("exponentials_done")
        s_msk = sem("masks_done")
        s_mb = sem("masks_begun")
        s_pvd = sem("head_values_done")
        s_ev = sem("outcome_copied")
        s_tvd = sem("outcome_turned")
        s_rd = sem("denominators_inverted")
        s_nrm = sem("heads_normalised")
        s_ks = [[sem(f"stack_loaded{p}{m}") for m in range(2)] for p in range(2)]
        s_nm = [sem(f"max_row_loaded{p}") for p in range(2)]
        s_kw = [[sem(f"k{l}_written{p}") for p in range(2)] for l in range(2)]
        s_qw = sem("queries_written")
        s_kr = sem("stacks_rows_laid")
        s_v1w = [sem(f"v1_written{p}") for p in range(2)]
        s_vc = [sem(f"v1_loaded{p}") for p in range(2)]
        s_out = sem("output_written")

        def split3(pe, out_ap, lh, ll, rh, rl, first, last):
            nc.tensor.matmul(out_ap, lh, rh, start=first, stop=False)
            nc.tensor.matmul(out_ap, lh, rl, start=False, stop=False)
            return nc.tensor.matmul(out_ap, ll, rh, start=False, stop=last)

        def layernorm_stats(dve):
            for t in range(NTILE):
                nc.vector.bn_stats(stats[:, t, :], xr[:, t, :]).then_inc(s_dve, 1)
            step[0] += NTILE
            dve.wait_ge(s_dve, step[0])
            for t in range(NTILE):
                nc.vector.bn_aggr(mv[:, t, :], stats[:, t, :]).then_inc(s_dve, 1)
            step[0] += NTILE
            dve.wait_ge(s_dve, step[0])
            nc.vector.tensor_scalar(veps[:, :], mv[:, :, 1], EPS, None, ALU.add).then_inc(s_var, 1)

        def layernorm_rows(dve, k):
            dve.wait_ge(s_rstd, k + 1)
            for t in range(NTILE):
                nc.vector.tensor_scalar(xn[:, t, :], xr[:, t, :], mv[:, t, 0:1], rstd[:, t:t + 1],
                                        ALU.subtract, ALU.mult).then_inc(s_xn, 1)

        def pool_rstd(pool, k):
            pool.wait_ge(s_var, k + 1)
            nc.gpsimd.tensor_tensor(rstd[:, :], veps[:, :], mhalf[:, :], ALU.pow).then_inc(s_rstd, 1)

        def transpose_rows(pe, n, kc, k=None):
            for t, (t0, tn) in enumerate(TT):
                if k is not None:
                    pe.wait_ge(s_xn, k * NTILE + t + 1)
                last = nc.tensor.transpose(wide[n % 4][:, t0:t0 + tn], xn[0:tn, t, kc * P:(kc + 1) * P],
                                           ident[0:tn, 0:tn])
            last.then_inc(s_wd, 1)

        def project_T(pe, n, wh, wl, mb):
            for t0, t1 in ((0, WIDE0), (WIDE0, NT)):
                for kc in range(KC):
                    last = split3(pe, wide[n % 4][:, t0:t1], wh[:, kc, mb * P:(mb + 1) * P],
                                  wl[:, kc, mb * P:(mb + 1) * P], xTh[:, kc, t0:t1], xTl[:, kc, t0:t1],
                                  kc == 0, kc == KC - 1)
            last.then_inc(s_wd, 1)

        def wide_hi(act, n, dst, bias=None):
            act.wait_ge(s_wd, n + 1)
            src = wide[n % 4][:, 0:NT]
            if bias is None:
                nc.scalar.activation(dst, src, ACT.Copy).then_inc(s_wh, 1)
            else:
                nc.scalar.activation(dst, src, ACT.Identity, bias=bias).then_inc(s_wh, 1)

        def wide_lo(dve, n, hi, dst, bias=None, nh=None):
            dve.wait_ge(s_wh, (n if nh is None else nh) + 1)
            src = wide[n % 4][:, 0:NT]
            if bias is None:
                nc.vector.tensor_tensor(dst, src, hi, ALU.subtract).then_inc(s_wf, 1)
            else:
                nc.vector.scalar_tensor_tensor(out=dst, in0=src, scalar=bias, in1=hi, op0=ALU.add,
                                               op1=ALU.subtract).then_inc(s_wf, 1)

        step = [0]

        def dve_bias_in(dve, l):
            nc.vector.tensor_scalar(bpr[:, l, :], bpr[:, l, :], tg[:, l:l + 1], None, ALU.mult).then_inc(s_dve, 1)
            step[0] += 1
            dve.wait_ge(s_dve, step[0])
            nc.vector.tensor_tensor(xr[:, :, :], xr[:, :, :], bpr[:, l:l + 1, :].to_broadcast([P, NTILE, D]),
                                    ALU.add).then_inc(s_dve, 1)
            step[0] += 1
            dve.wait_ge(s_dve, step[0])

        es_att = top.enter_context(ExitStack())
        maskv = sb("maskv", [T, S0], F32, es_att)
        KSa = sb("KS", [P, 2, H, S0], F16, es_att)
        KS = [KSa[0:KROWS + 1, p] for p in range(2)]
        QS = [sb(f"QS{p}", [KROWS + 1, H, T], F16, es_att) for p in range(2)]
        PT = sb("PT", [P, 4, H, T], F32, es_att)
        qh = sb("qh", [P, KC, NT], F16, es_att)
        ql = sb("ql", [P, KC, NT], F16, es_att)
        aallw = sb("aall", [P, B, D], F32, es_att)
        aall = aallw[0:T]
        mx = [sb(f"mx{p}", [T, H], F32, es_att) for p in range(2)]
        nm = [sb(f"nm{p}", [H, T], F16, es_att) for p in range(2)]
        rdens = [sb(f"rden{p}", [T, H], F32, es_att) for p in range(2)]
        pvs = sb("pvs", [GW, H // HG * T], F32, es_att)
        Vc = [sb(f"Vc{p}", [CH, 3, H, VS], F32, es_att) for p in range(2)]

        RD = max(NI, 2 * TC)
        share = sb("share", [P, 2 * NIB * D + KC * RD], F32, es_att)
        rg, ru = (share[:, m * NIB * D:(m + 1) * NIB * D].rearrange("p (i d) -> p i d", i=NIB) for m in range(2))
        rd_ = share[:, 2 * NIB * D:].rearrange("p (k n) -> p k n", k=KC)
        cn = [rg[0:CH, 3 * p:3 * p + 3, :] for p in range(2)]
        kc_ = [[r[:, :, :].rearrange("p a d -> p (a d)")[:, p * 2 * TC:(p + 1) * 2 * TC].bitcast(F16).rearrange(
            "p (s k t) -> p s k t", s=2, k=KC) for p in range(2)] for r in (ru, rd_)]
        kfree = KSa[:, 0, :, :].rearrange("p h s -> p (h s)")
        wgT, wuT = (kfree[:, m * KC * NI:(m + 1) * KC * NI].rearrange("p (k i) -> p k i", k=KC) for m in range(2))
        wdT = kfree[:, 2 * KC * NI:2 * KC * NI + NIB * D].rearrange("p (i d) -> p i d", i=NIB)
        wm = sb("wm", [P, 2 * NIB + KC], F32, es_att)
        winv = sb("winv", [P, 2 * NIB + KC], F32, es_att)
        WPIECES = ([(m, kc, ibs) for m in range(2) for kc in range(KC) for ibs in ((0, 1, 2, 3), (4, 5))]
                   + [(2, 0, ibs) for ibs in ((0, 1), (2, 3), (4, 5))])
        s_fw = sem("block_weights_loaded")
        s_fm = sem("block_weight_maxima_taken")
        s_fs = sem("block_weight_scales_made")
        s_fq = sem("block_weights_rounded")
        s_ft = sem("block_weights_turned")
        s_fc = sem("block_weights_in_fp16")

        es_a = es_att.enter_context(ExitStack())
        cTh = [sb(f"cTh{p}", [P, KC, TC], F16, es_a) for p in range(2)]
        cTl = [sb(f"cTl{p}", [P, KC, TC], F16, es_a) for p in range(2)]
        V1s = [xn[0:CH, :, :].rearrange("p t d -> p (t d)")[:, p * 3 * H * VW:(p + 1) * 3 * H * VW].rearrange(
            "p (c h v) -> p c h v", c=3, h=H) for p in range(2)]
        skh, skl = aTh, aTl
        Vs = sb("Vs", [T, B, H, VW], F32, es_a)
        wah = sb("wah", [P, KC, 3 * D], F16, es_a)
        wal = sb("wal", [P, KC, 3 * D], F16, es_a)
        wrh = sb("wrh", [P, KC, D], F16, es_a)
        wrl = sb("wrl", [P, KC, D], F16, es_a)
        wvh = sb("wvh", [P, KC, 2, D], F16, es_a)
        wvl = sb("wvl", [P, KC, 2, D], F16, es_a)
        PTf = PT[:, :, :, :].rearrange("p c h t -> p c (h t)")
        r_attn = PTf[:, 0, 0:KC * 3 * D].rearrange("p (k n) -> p k n", k=KC)
        r_ref = PTf[:, 1, 0:KC * 2 * D].rearrange("p (k n) -> p k n", k=KC)
        r_proj = PTf[:, 1, KC * 2 * D:KC * 3 * D].rearrange("p (k n) -> p k n", k=KC)
        r_l1 = [PTf[:, 2, m * KC * D:(m + 1) * KC * D].rearrange("p (k n) -> p k n", k=KC) for m in range(3)]
        r_l1.append(PTf[:, 3, 0:KC * D].rearrange("p (k n) -> p k n", k=KC))
        krow = PTf[0:H, 3, KC * D:KC * D + S0 // 2 + 1].bitcast(F16)[:, 0:S0]

        TB, VB, KB, NB = (0, 2), (0, 1, 1), (0, 2, 0, 1), 2
        NV0, NK0, NN0 = 2, 4, 8
        SMH = [1, 1, 2, 1, 2, 1, 2, 1, 2, 1, 2, 0, 0, 0, 0, 0]
        TVK = {0: "T0", 1: "T1", 2: "V0", 3: "V1", 4: "K0", 5: "K1", 7: "K2", 8: "K3"}
        SM0 = (0, 5, 10, 16)
        LAG = 5
        NSTEP = 12

        def pe_T(pe, j, o, kc, n):
            p = o % 2
            if kc == 0:
                pe.wait_ge(s_ctx[p], 32 * (j + o // 2 + 1))
            if not (isinstance(n, int) and n < 2):
                pe.wait_ge(s_mf, n - 1)
            bank = misc[TB[kc]]
            for c in range(3):
                last = nc.tensor.transpose(bank[:, COFF[c]:COFF[c] + CSZ[c]],
                                           cn[p][0:CSZ[c], c, kc * P:(kc + 1) * P], ident[0:CSZ[c], 0:CSZ[c]])
            last.then_inc(s_md, 1)

        def pe_K(pe, j, o, k, n, nT, late=False):
            p, l, mb = o % 2, k // 2, k % 2
            pe.wait_ge(s_mf, nT + 1)
            wh, wl = (wrh, wrl) if l == 0 else (w1kh[:, 0], w1kl[:, 0])
            bank = misc[KB[k]][:, 0:TC]
            if k > 1 or late:
                pe.wait_ge(s_mf, n - 1)
            for kc in range(KC):
                last = split3(pe, bank, wh[:, kc, mb * P:(mb + 1) * P], wl[:, kc, mb * P:(mb + 1) * P],
                              cTh[p][:, kc, :], cTl[p][:, kc, :], kc == 0, kc == KC - 1)
            last.then_inc(s_md, 1)

        def pe_V(pe, j, o, c, n, freed=None):
            p = o % 2
            pe.wait_ge(s_mf, n - 1 if freed is None else freed)
            bank = misc[VB[c]][0:CSZ[c], :]
            sl = slice(COFF[c], COFF[c] + CSZ[c])
            for kc in range(KC):
                last = split3(pe, bank, cTh[p][:, kc, sl], cTl[p][:, kc, sl],
                              wvh[:, kc, :, :].rearrange("p l n -> p (l n)"),
                              wvl[:, kc, :, :].rearrange("p l n -> p (l n)"), kc == 0, kc == KC - 1)
            last.then_inc(s_md, 1)

        def pe_SM(pe, j, o, h, layer, smn):
            p = o % 2
            if h % HM == 0:
                nd = NDS[layer]
                pe.wait_ge(s_ks[p][h // HM], 16 * nd * (j + o // 2 + 1) + KSB[layer])
            idx = 2 * H * j + H * o + h + smn
            if not (isinstance(idx, int) and idx < 2):
                pe.wait_ge(s_smf, idx - 1)
            bank = sm_bank[h % 2]
            if layer == 0:
                nc.tensor.matmul(bank[0:T, 0:S0], QS[p][0:KROWS, h, :], KS[p][0:KROWS, h, :],
                                 start=True, stop=True).then_inc(s_smd, 1)
            else:
                nc.tensor.matmul(bank[0:T, 0:TC], QS[p][0:KROWS, h, :], KS[p][0:KROWS, h, 0:TC],
                                 start=True, stop=True).then_inc(s_smd, 1)

        def pe_N(pe, j, o, smn, n, freed):
            p = o % 2
            pe.wait_ge(s_smf, 2 * H * j + H * (o + 1) + smn)
            pe.wait_ge(s_mf, freed)
            nc.tensor.transpose(misc[NB][0:H, 0:T], mx[p][:, :], ident[0:T, 0:T]).then_inc(s_md, 1)

        def pe_ST(pe, j, o, t, layer, stn, nmc):
            p = o % 2
            nch = 4 - layer
            g, c = t // nch, t % nch
            if t == 0:
                pe.wait_ge(s_nm[p], 16 * (j + o // 2 + 1) + nmc)
            if t >= 2 or layer == 1:
                pe.wait_ge(s_exp, 2 * (H // HG) * nch * j + (H // HG) * nch * o + t + stn - 1)
            bank = st_bank[t % 2]
            if layer == 0:
                k0, kn = (0, T) if c == 0 else (T + COFF[c - 1], CSZ[c - 1])
            else:
                k0, kn = COFF[c], CSZ[c]
            for i in range(HG):
                h = g * HG + i
                last = nc.tensor.matmul(bank[0:kn, i * T:(i + 1) * T], KS[p][:, h, k0:k0 + kn],
                                        QS[p][:, h, :], start=True, stop=True)
            last.then_inc(s_std, 1)

        def pe_PV(pe, j, o, h, layer, stn, nrn):
            p = o % 2
            nch = 4 - layer
            g = h // HG
            if h % HG == 0:
                per = (H // HG) * nch
                pe.wait_ge(s_exp, 2 * per * j + per * o + nch * (g + 1) + stn)
                if layer == 0:
                    pe.wait_ge(s_msk, 2 * (H // HG) * j + (H // HG) * o + g + 1)
                else:
                    if g == 0:
                        pe.wait_ge(s_vc[p], 16 * (j + o // 2 + 1))
            if h == 0 and layer == 1:
                pe.wait_ge(s_nrm, 2 * j + o + nrn - 1)
            elif h == 0 and isinstance(j, int) and 2 * j + o > 0:
                pe.wait_ge(s_nrm, 2 * j + o + nrn)
            i = h % HG
            dst = pv_bank[p * layer][0:GW, g * T:(g + 1) * T]
            for c in range(nch):
                if layer == 0:
                    kn = T if c == 0 else CSZ[c - 1]
                    v = VSB[p][:, :, :] if c == 0 else Vc[p][0:kn, c - 1, :, :]
                else:
                    kn = CSZ[c]
                    v = Vc[p][0:kn, c, :, :]
                w0 = g * HG * VS + i * GW
                last = nc.tensor.matmul(dst, v.rearrange("p h v -> p (h v)")[:, w0:w0 + GW], PT[0:kn, c, h, :],
                                        start=(i == 0 and c == 0), stop=(i == HG - 1 and c == nch - 1))
            last.then_inc(s_pvd, 1)

        def pe_turn(pe, j, o, bsum):
            bank = pv_bank[o % 2 if bsum else 0]
            pe.wait_ge(s_ev, 2 * j + o + 1 + bsum)
            for g in range(H // HG):
                last = nc.tensor.transpose(bank[0:T, g * GW:(g + 1) * GW], pvs[:, g * T:(g + 1) * T],
                                           ident[0:GW, 0:GW])
            last.then_inc(s_tvd, 1)

        def act_hi_T(act, j, o, kc, n):
            act.wait_ge(s_md, n + 1)
            nc.scalar.activation(cTh[o % 2][:, kc, :], misc[TB[kc]][:, 0:TC], ACT.Copy).then_inc(s_mh, 1)

        def act_hi_K(act, j, o, k, n):
            p, l, mb = o % 2, k // 2, k % 2
            if o >= 2 and mb == 0:
                act.wait_ge(s_kw[l][p], KW * (j + o // 2))
            act.wait_ge(s_md, n + 1)
            nc.scalar.activation(kc_[l][p][:, 0, mb, :], misc[KB[k]][:, 0:TC], ACT.Identity,
                                 bias=bcol[:, 2 + l, mb:mb + 1]).then_inc(s_mh, 1)

        def act_exp(act, j, o, t, layer, stn):
            nch = 4 - layer
            g, c = t // nch, t % nch
            idx = 2 * (H // HG) * nch * j + (H // HG) * nch * o + t + stn
            act.wait_ge(s_std, idx + 1)
            if layer == 0:
                kn, bias = (T, 0.0) if c == 0 else (CSZ[c - 1], ctxb[0:CSZ[c - 1], 0:1])
            else:
                kn, bias = CSZ[c], 0.0
            nc.scalar.activation(PT[0:kn, c, g * HG:(g + 1) * HG, :].rearrange("p h t -> p (h t)"),
                                 st_bank[t % 2][0:kn, 0:HG * T], ACT.Exp, scale=SCALE, bias=bias
                                 ).then_inc(s_exp, 1)

        def act_evac(act, j, o, bsum):
            act.wait_ge(s_pvd, H * (2 * j + o + 1 + bsum))
            bank = pv_bank[o % 2 if bsum else 0]
            nc.scalar.activation(pvs[:, :], bank[0:GW, 0:H // HG * T], ACT.Copy).then_inc(s_ev, 1)

        def dve_lo_T(dve, j, o, kc, n, nh):
            p = o % 2
            dve.wait_ge(s_mh, nh + 1)
            nc.vector.tensor_tensor(cTl[p][:, kc, :], misc[TB[kc]][:, 0:TC], cTh[p][:, kc, :],
                                    ALU.subtract).then_inc(s_mf, 1)

        def dve_lo_K(dve, j, o, k, n, nh):
            p, l, mb = o % 2, k // 2, k % 2
            dve.wait_ge(s_mh, nh + 1)
            nc.vector.scalar_tensor_tensor(out=kc_[l][p][:, 1, mb, :], in0=misc[KB[k]][:, 0:TC],
                                           scalar=bcol[:, 2 + l, mb:mb + 1], in1=kc_[l][p][:, 0, mb, :],
                                           op0=ALU.add, op1=ALU.subtract).then_inc(s_mf, 1)

        def dve_V(dve, j, o, c, n):
            p = o % 2
            dve.wait_ge(s_md, n + 1)
            kn = CSZ[c]
            bank = misc[VB[c]][0:kn, :].rearrange("p (l h d) -> p l h d", l=2, h=H)
            row = brow[0:kn, 1:3, :].rearrange("p l (h d) -> p l h d", h=H)
            nc.vector.tensor_tensor(Vc[p][0:kn, c, :, 0:DH], bank[:, 0], row[:, 0], ALU.add)
            nc.vector.tensor_tensor(V1s[p][0:kn, c, :, 0:DH], bank[:, 1], row[:, 1], ALU.add).then_inc(s_mf, 1)

        def dve_max(dve, j, o, h, layer, smn):
            p = o % 2
            dve.wait_ge(s_smd, 2 * H * j + H * o + h + smn + 1)
            if layer == 0:
                dve.sem_inc(s_rb, 1)
                rows = sm_bank[h % 2][0:T, 0:S0]
                nc.vector.tensor_tensor_reduce(rows, rows, maskv[:, :], 1.0, -BIG,
                                               ALU.add, ALU.max, mx[p][:, h:h + 1]).then_inc(s_smf, 1)
            else:
                nc.vector.tensor_reduce(mx[p][:, h:h + 1], sm_bank[h % 2][0:T, 0:TC], X, ALU.max).then_inc(s_smf, 1)

        def dve_N(dve, j, o, n):
            p = o % 2
            dve.wait_ge(s_md, n + 1)
            nc.vector.tensor_scalar(nm[p][:, :], misc[NB][0:H, 0:T], -1.0 / (WS * WS), None,
                                    ALU.mult).then_inc(s_mf, 1)

        def dve_norm(dve, j, o, bsum):
            dve.wait_ge(s_tvd, 2 * j + o + 1 + bsum)
            pv = pv_bank[o % 2 if bsum else 0][0:T, 0:H * VW].rearrange("p (h v) -> p h v", h=H)
            rden = rdens[o % 2]
            nc.vector.reciprocal(rden[:, :], pv[:, :, DH]).then_inc(s_rd, 1)
            dve.wait_ge(s_rd, 2 * j + o + 1 + bsum)
            nc.vector.tensor_tensor(aall[:, bass.ds(2 * j + o, 1), :].rearrange("p a (h d) -> p (a h) d", h=H),
                                    pv[:, :, 0:DH], rden[:, :].unsqueeze(2).to_broadcast([T, H, DH]),
                                    ALU.mult).then_inc(s_nrm, 1)
            
        NDS = [3, 2]
        KSB = [0, 16 * 3 * (B // 2)]
        QSLOTS, KSLOTS = ((0, 2, 1), (2, 4, 1)), ((0, 3, 2), (1, 4, 2))
        VSB = [sb(f"VSB{p}", [T, H, VS], F32, es_a) for p in range(2)]
        ctxb = sb("ctxb", [P, 1], F32, es_a)
        s_vsb = [sem(f"own_values_staged{p}") for p in range(2)]
        KW = 16 * 2 * KC

        def sp_ctx(sp, j, o):
            p = o % 2
            b = 2 * j + o
            src = ctx_seq[bass.ds(b, 1), :, :].rearrange("a t d -> (a t) d")
            sp.dma_start(cn[p][:, 0, :], src[0:CH, :]).then_inc(s_ctx[p], 16)
            sp.dma_start(cn[p][0:CSZ[1], 1:3, :], src[CH:TC, :].rearrange("(c t) d -> t c d", c=2)
                         ).then_inc(s_ctx[p], 16)

        def sp_halves_out(sp, dram, halves, mb, slots):
            for src, (s0, s1, step_) in zip(halves, slots):
                sp.dma_start(dram[mb * HM:(mb + 1) * HM, :, s0:s1:step_, :].rearrange("h d s t -> (h d) s t"),
                             src[:, mb:mb + 1, :].to_broadcast([P, 2, NT])).then_inc(s_qw, 16)

        def sp_keys_out(sp, j, o, l):
            p = o % 2
            for mb in range(KC):
                for s in (0, 2):
                    sp.dma_start(k_dram[l][bass.ds(2 * j + o, 1), mb * HM:(mb + 1) * HM, :, s:s + 2, :].rearrange(
                        "b h d s t -> (b h d) s t"), kc_[l][p][:, :, mb, :]).then_inc(s_kw[l][p], 16)

        def sp_stack_in(sp, j, o, mb, dst, dram, own):
            p = o % 2
            hs = slice(mb * HM, (mb + 1) * HM)
            b = 2 * j + o
            if own:
                src = dram[hs, :, :, bass.ds(b * T, T)].rearrange("h d s t -> (d s) h t")
            else:
                src = dram[bass.ds(b, 1), hs].rearrange("b h d s t -> (d s) (b h) t")
            sp.dma_start(dst, src).then_inc(s_ks[p][mb], 16)

        def sp_stack0(sp, j, o, mb):
            p, hs = o % 2, slice(mb * HM, (mb + 1) * HM)
            sp_stack_in(sp, j, o, mb, QS[p][0:KROWS, hs, :], q_dram, True)
            sp_stack_in(sp, j, o, mb, KS[p][0:KROWS, hs, 0:T], sk_dram, True)
            sp_stack_in(sp, j, o, mb, KS[p][0:KROWS, hs, T:S0], k_dram[0], False)

        def sp_stack1(sp, j, o, mb, keys=True, queries=True):
            p, hs = o % 2, slice(mb * HM, (mb + 1) * HM)
            if keys:
                sp_stack_in(sp, j, o, mb, KS[p][0:KROWS, hs, 0:TC], k_dram[1], False)
            if queries:
                sp_stack_in(sp, j, o, mb, QS[p][0:KROWS, hs, :], q_dram, True)

        with nc.Block() as block:

            @block.sync
            def _(sp):
                sp.dma_start(xr[:, 0:FULL, :], xf[0:FULL * P, :].rearrange("(t p) d -> p t d", p=P)).then_inc(s_x, 16)
                sp.wait_ge(s_pad, 1)
                sp.dma_start(xr[0:LAST, FULL, :], xf[FULL * P:NT, :]).then_inc(s_x, 16)
                sp.dma_start(r_attn, w_attn.rearrange("(k p) n -> p k n", p=P)).then_inc(s_wr[0], 16)
                sp_ctx(sp, 0, 0)
                sp.dma_start(r_ref, w_ref.rearrange("(k p) n -> p k n", p=P)).then_inc(s_wr[1], 16)
                sp.dma_start(r_proj, w_proj.rearrange("(k p) n -> p k n", p=P)).then_inc(s_wr[1], 16)
                for m, w in enumerate((w_k, w_v, w_q, w_o)):
                    sp.dma_start(r_l1[m], w.rearrange("(k p) n -> p k n", p=P)).then_inc(s_wr[2], 16)
                sp_ctx(sp, 0, 1)
                for p in range(2):
                    if p == 0:
                        sp.wait_ge(s_const, 1)
                    sp.dma_start(KS[p][KROWS:KROWS + 1, :, :], krow[:, :]).then_inc(s_kr, 16)

                for mb in range(KC):
                    sp.wait_ge(s_wf, 3 + mb)
                    sp_halves_out(sp, q_dram, (qh, ql), mb, QSLOTS)
                for mb in range(KC):
                    sp.wait_ge(s_wf, 5 + mb)
                    sp_halves_out(sp, sk_dram, (skh, skl), mb, KSLOTS)
                sp.wait_ge(s_mf, 2)
                sp_ctx(sp, 0, 2)
                sp.wait_ge(s_mf, 4)
                sp_keys_out(sp, 0, 0, 0)
                sp.wait_ge(s_qw, 16 * 8)
                sp.wait_ge(s_kw[0][0], KW)
                for mb in range(KC):
                    sp_stack0(sp, 0, 0, mb)
                sp.wait_ge(s_mf, 10)
                sp_keys_out(sp, 0, 1, 0)
                sp.wait_ge(s_zero, 1)
                sp.dma_start(VSB[0][:, :, 0:VW], Vs[:, 0, :, :]).then_inc(s_vsb[0], 16)
                sp.wait_ge(s_kw[0][1], KW)
                sp_stack0(sp, 0, 1, 0)
                sp.wait_ge(s_mf, 16)
                sp.dma_start(QS[0][KROWS:KROWS + 1, :, :], nm[0][:, :]).then_inc(s_nm[0], 16)
                sp_stack0(sp, 0, 1, 1)
                sp_ctx(sp, 0, 3)
                for o in range(2):
                    sp_keys_out(sp, 0, o, 1)
                sp.dma_start(v1_dram[0], V1s[0][:, :, :, :].rearrange("p c h v -> p (c h v)")).then_inc(s_v1w[0], 16)

                def round0(j, u, ctx, keys, nxt):
                    n0 = 16 + 10 * (2 * j + u)
                    p = u % 2
                    n1 = n0 + (NN0 if keys else 2)
                    if nxt:
                        sp.wait_ge(s_std, 16 * (2 * j + u) + 8)
                        sp.dma_start(VSB[1 - p][:, :, 0:VW], Vs[:, bass.ds(2 * j + u + 1, 1), :, :].rearrange(
                            "p a h v -> p (a h) v")).then_inc(s_vsb[1 - p], 16)
                    if ctx:
                        sp.wait_ge(s_mf, n0 + 2)
                        sp_ctx(sp, j, u + 4)
                    if keys:
                        sp.wait_ge(s_mf, n0 + NK0 + 2)
                        sp_keys_out(sp, j, u + 2, 0)
                        sp.wait_ge(s_mf, n0 + NK0 + 4)
                        sp_keys_out(sp, j, u + 2, 1)
                        sp.wait_ge(s_kw[0][p], KW * (j + 2))
                        sp_stack0(sp, j, u + 2, 0)
                    if nxt:
                        sp.wait_ge(s_mf, n1 + 1)
                        sp.dma_start(QS[1 - p][KROWS:KROWS + 1, :, :], nm[1 - p][:, :]).then_inc(s_nm[1 - p], 16)
                    if keys:
                        sp.wait_ge(s_std, 16 * (2 * j + u + 1))
                        sp_stack0(sp, j, u + 2, 1)
                    if nxt:
                        sp.wait_ge(s_mf, n1 + 2)
                        sp.dma_start(v1_dram[bass.ds(2 * j + u + 1, 1)].rearrange("b p n -> (b p) n"),
                                     V1s[1 - p][:, :, :, :].rearrange("p c h v -> p (c h v)")).then_inc(s_v1w[1 - p], 16)

                with sp.Fori(0, B // 2 - 2) as j:
                    for u in range(2):
                        round0(j, u, True, True, True)
                for u in range(2):
                    round0(B // 2 - 2, u, False, True, True)
                for p in range(2):
                    for l in range(2):
                        sp.wait_ge(s_kw[l][p], KW * B // 2)
                FI = (NIB - 1) * P
                for dst, src in ((rg, w_gate), (ru, w_up)):
                    sp.dma_start(dst[:, 0:NIB - 1, :], src[0:FI, :].rearrange("(i p) d -> p i d", p=P)).then_inc(s_fw, 16)
                    sp.dma_start(dst[0:LASTI, NIB - 1, :], src[FI:NI, :]).then_inc(s_fw, 16)
                sp.dma_start(rd_[:, :, 0:NI], w_down.rearrange("(k p) n -> p k n", p=P)).then_inc(s_fw, 16)
                round0(B // 2 - 1, 0, False, False, True)
                for p in range(2):
                    sp.wait_ge(s_v1w[p], 16 * B // 2)

            @block.gpsimd
            def _(pool):
                nc.gpsimd.memset(xr[:, FULL, :], 0.0).then_inc(s_pad, 1)
                nc.gpsimd.memset(ident[:, :], 0.0)
                nc.gpsimd.memset(krow[:, :], WS * WS)
                nc.gpsimd.memset(maskv[:, :], 0.0)
                nc.gpsimd.memset(mhalf[:, :], -0.5)
                nc.gpsimd.memset(ones[:, :], 1.0)
                nc.gpsimd.memset(ctxb[:, :], CTX_BIAS)
                nc.gpsimd.memset(magic[:, 0:1], MAGIC)
                nc.gpsimd.memset(magic[:, 1:2], -MAGIC).then_inc(s_const, 1)
                pool.wait_ge(s_const, 1)
                nc.gpsimd.affine_select(out=ident[:, :], in_=ident[:, :], compare_op=ALU.not_equal, fill=1.0,
                                        base=0, pattern=[[-1, P]], channel_multiplier=1).then_inc(s_const, 1)
                nc.gpsimd.affine_select(out=maskv[:, 0:T], in_=maskv[:, 0:T], compare_op=ALU.is_ge, fill=-BIG,
                                        base=0, pattern=[[-1, T]], channel_multiplier=1).then_inc(s_const, 1)
                nc.gpsimd.affine_select(out=maskv[:, T:2 * T], in_=maskv[:, T:2 * T], compare_op=ALU.not_equal,
                                        fill=-BIG, base=0, pattern=[[-1, T]], channel_multiplier=1
                                        ).then_inc(s_const, 1)
                pool_rstd(pool, 0)
                for p in range(2):
                    nc.gpsimd.memset(Vc[p][:, :, :, :], 0.0)
                    last = nc.gpsimd.memset(VSB[p][:, :, :], 0.0)
                last.then_inc(s_zero, 1)

                def masks(j, u):
                    for g in range(H // HG):
                        hs = slice(g * HG, (g + 1) * HG)
                        pool.wait_ge(s_exp, 16 * (2 * j + u) + 4 * g + 2)
                        pool.sem_inc(s_mb, 1)
                        nc.gpsimd.affine_select(out=PT[0:T, 0, hs, :], in_=PT[0:T, 0, hs, :], compare_op=ALU.is_ge,
                                                fill=0.0, base=0, pattern=[[0, HG], [1, T]], channel_multiplier=-1)
                        nc.gpsimd.affine_select(out=PT[0:T, 1, hs, :], in_=PT[0:T, 1, hs, :],
                                                compare_op=ALU.not_equal, fill=0.0, base=0,
                                                pattern=[[0, HG], [-1, T]], channel_multiplier=1).then_inc(s_msk, 1)

                with pool.Fori(0, B // 2 - 1) as j:
                    for u in range(2):
                        masks(j, u)
                masks(B // 2 - 1, 0)
                masks(B // 2 - 1, 1)

            @block.scalar
            def _(act):
                for k, (dst, src) in enumerate((
                        (bcol[:, 0, :], b_attn[0:D].rearrange("(k p) -> p k", p=P)),
                        (bcol[:, 1, :], b_attn[D:2 * D].rearrange("(k p) -> p k", p=P)),
                        (bcol[:, 2, :], b_ref[0:D].rearrange("(k p) -> p k", p=P)),
                        (bcol[:, 3, :], b_k.rearrange("(k p) -> p k", p=P)),
                        (bcol[:, 4, :], b_q.rearrange("(k p) -> p k", p=P)),
                        (brow[:, 0, :], b_attn[2 * D:3 * D].partition_broadcast(P)),
                        (brow[:, 1, :], b_ref[D:2 * D].partition_broadcast(P)),
                        (brow[:, 2, :], b_v.partition_broadcast(P)))):
                    act.dma_start(dst, src, allow_slow_non_contiguous=k <= 4).then_inc(s_bias, 16)
                act.wait_ge(s_wr[0], 16)
                nc.scalar.activation(wah[:, :, :], r_attn, ACT.Copy, scale=WS).then_inc(s_wh8, 1)
                for kc in range(KC):
                    wide_hi(act, kc, xTh[:, kc, :])
                for dst, src in (
                        (gts[:, 0:2], g_xattn.partition_broadcast(P)), (gts[:, 2:4], g_ffn.partition_broadcast(P)),
                        (clips[:, 0:1], clip_x.partition_broadcast(P)), (clips[:, 1:2], clip_down.partition_broadcast(P)),
                        (bpr[:, 0, :], b_proj.partition_broadcast(P)), (bpr[:, 1, :], b_o.partition_broadcast(P)),
                        (gbr[:, :], gate_b.partition_broadcast(P)),
                        (b1c[:, :, :], b1.rearrange("e (p f) -> p e f", p=P)), (b2r[:, :], b2),
                        (gwr[:, :, :], gate_w.rearrange("(k p) e -> p k e", p=P))):
                    act.dma_start(dst, src).then_inc(s_small, 16)
                act.wait_ge(s_biasp, 1)
                for mb in range(KC):
                    wide_hi(act, 2 + mb, qh[:, mb, :], bcol[:, 0, mb:mb + 1])
                for mb in range(KC):
                    wide_hi(act, 4 + mb, skh[:, mb, :], bcol[:, 1, mb:mb + 1])
                act.wait_ge(s_wr[1], 32)
                act.wait_ge(s_small, 16 * 10)
                nc.scalar.activation(wrh[:, :, :], r_ref[:, :, 0:D], ACT.Copy, scale=WS)
                nc.scalar.activation(wvh[:, :, 0, :], r_ref[:, :, D:2 * D], ACT.Copy, scale=WS)
                nc.scalar.activation(wph[:, 0, :, :], r_proj, ACT.Copy, scale=WS)
                nc.scalar.activation(gwh[:, :, :], gwr[:, :, :], ACT.Copy, scale=WS).then_inc(s_wh8, 1)
                nc.scalar.activation(tg[:, :], gts[:, :], ACT.Tanh)
                nc.scalar.activation(clipt[:, :], clips[:, :], ACT.Tanh, scale=0.5).then_inc(s_tanh, 1)
                for n, dsts in ((8, (w1kh[:, 0], wvh[:, :, 1])), (9, (w1kh[:, 1], wph[:, 1]))):
                    act.wait_ge(s_wd, n + 1)
                    for i, dst in enumerate(dsts):
                        last = nc.scalar.activation(dst, wide[n % 4][:, 512 * i:512 * i + 512].rearrange(
                            "p (k n) -> p k n", k=KC), ACT.Copy, scale=WS)
                    last.then_inc(s_wh, 1)

                for o in range(2):
                    for kc in range(KC):
                        act_hi_T(act, 0, o, kc, 6 * o + kc)
                    for k in range(4):
                        act_hi_K(act, 0, o, k, 6 * o + 2 + k)

                act.wait_ge(s_wf, 10)
                act.wait_ge(s_split, 2)

                def rounding(k):
                    if k == 0:
                        act.wait_ge(s_fs, 1)
                    if k < 2 * NIB:
                        r, ib = (rg, ru)[k // NIB], k % NIB
                        n = P if ib < NIB - 1 else LASTI
                        piece = r[0:n, ib, :]
                    else:
                        n, piece = P, rd_[:, k - 2 * NIB, 0:NI]
                    nc.scalar.activation(piece, piece, ACT.Identity, bias=magic[0:n, 0:1],
                                         scale=winv[0:n, k:k + 1]).then_inc(s_fq, 1)

                def round0(j, u, keys, weights=False):
                    n0 = 16 + 10 * (2 * j + u)
                    for t in range(16):
                        act_exp(act, j, u, t, 0, 0)
                        if weights and 4 <= t < 4 + NIB + KC // 2:
                            rounding(2 * (t - 4))
                            rounding(2 * (t - 4) + 1)
                        kind = TVK.get(t, "")
                        if keys and kind[:1] == "T":
                            act_hi_T(act, j, u + 2, int(kind[1]), n0 + int(kind[1]))
                        elif keys and kind[:1] == "K":
                            act_hi_K(act, j, u + 2, int(kind[1]), n0 + NK0 + int(kind[1]))
                    act_evac(act, j, u, 0)

                with act.Fori(0, B // 2 - 1) as j:
                    for u in range(2):
                        round0(j, u, True)
                for u in range(2):
                    round0(B // 2 - 1, u, False, u == 1)

            @block.tensor
            def _(pe):
                pe.wait_ge(s_const, 4)
                for kc in range(KC):
                    transpose_rows(pe, kc, kc, 0)
                pe.wait_ge(s_split, 1)
                pe.wait_ge(s_wf, 2)
                for mb in range(KC):
                    project_T(pe, 2 + mb, wah, wal, mb)
                for mb in range(KC):
                    pe.wait_ge(s_wf, 4 + mb - 3)
                    project_T(pe, 4 + mb, wah, wal, KC + mb)
                for n in range(2):
                    pe.wait_ge(s_wf, 6 + n - 3)
                    for i in range(4):
                        b = 4 * n + i
                        for kc in range(KC):
                            last = split3(pe, wide[(6 + n) % 4][0:T, i * D:(i + 1) * D],
                                          xTh[:, kc, b * T:(b + 1) * T], xTl[:, kc, b * T:(b + 1) * T],
                                          wah[:, kc, 2 * D:3 * D], wal[:, kc, 2 * D:3 * D], kc == 0, kc == KC - 1)
                    last.then_inc(s_wd, 1)
                pe.wait_ge(s_wr[2], 64)
                for n in range(2):
                    pe.wait_ge(s_wf, 8 + n - 3)
                    for i in range(2):
                        for kc in range(KC):
                            for ob in range(KC):
                                o0 = 512 * i + kc * D + ob * P
                                last = nc.tensor.transpose(wide[(8 + n) % 4][:, o0:o0 + P],
                                                           r_l1[2 * n + i][:, ob, kc * P:(kc + 1) * P], ident[:, :])
                    last.then_inc(s_wd, 1)
                pe.wait_ge(s_split, 2)
                pe.wait_ge(s_wf, 10)
                for o in range(2):
                    n0 = 6 * o
                    for kc in range(KC):
                        pe_T(pe, 0, o, kc, n0 + kc)
                    for k in range(4):
                        pe_K(pe, 0, o, k, n0 + 2 + k, n0 + 1)
                for c in range(3):
                    pe_V(pe, 0, 0, c, 12 + c, 12 + c if c == 2 else None)
                    for h in range(SM0[c], SM0[c + 1]):
                        pe_SM(pe, 0, 0, h, 0, 0)
                pe_N(pe, 0, 0, 0, 15, 15)
                pe.wait_ge(s_kr, 32)
                pe.wait_ge(s_mf, 16)

                def turning(k):
                    m, kc, ibs = WPIECES[k]
                    if k >= 3:
                        pe.wait_ge(s_fc, k - 2)
                    pe.wait_ge(s_fq, min((m + 1) * NIB, 2 * NIB) if m < 2 else 2 * NIB + KC)
                    for i, ib in enumerate(ibs):
                        n = P if ib < NIB - 1 else LASTI
                        if m < 2:
                            last = nc.tensor.transpose(misc[k % 3][:, i * P:i * P + n],
                                                       (rg, ru)[m][0:n, ib, kc * P:(kc + 1) * P], ident[0:n, 0:n])
                        else:
                            for q in range(KC):
                                last = nc.tensor.transpose(misc[k % 3][0:n, i * D + q * P:i * D + (q + 1) * P],
                                                           rd_[:, q, ib * P:ib * P + n], ident[:, :])
                    last.then_inc(s_ft, 1)

                def round0(j, u, keys, nxt, weights=False):
                    n0 = 16 + 10 * (2 * j + u)
                    nv = n0 + (NV0 if keys else 0)
                    h = 0
                    for t in range(16):
                        if t == 4:
                            pe.wait_ge(s_vsb[u], 16 * (j + 1))
                        pe_ST(pe, j, u, t, 0, 0, 0)
                        kind = TVK.get(t, "")
                        if keys and kind[:1] == "T":
                            pe_T(pe, j, u + 2, int(kind[1]), n0 + int(kind[1]))
                        elif keys and kind[:1] == "K":
                            pe_K(pe, j, u + 2, int(kind[1]), n0 + NK0 + int(kind[1]), n0 + 1, True)
                        elif nxt and kind[:1] == "V":
                            pe_V(pe, j, u + 1, int(kind[1]), nv + int(kind[1]))
                        if nxt:
                            for _ in range(SMH[t]):
                                pe_SM(pe, j, u + 1, h, 0, 0)
                                h += 1
                        if t >= LAG:
                            pe_PV(pe, j, u, t - LAG, 0, 0, 0)
                        if weights and t >= 9:
                            turning(t - 9)
                        if nxt and t == NSTEP:
                            n1 = n0 + (NN0 if keys else 2)
                            pe_N(pe, j, u + 1, 0, n1, n1 - 1)
                    for i in range(LAG):
                        pe_PV(pe, j, u, H - LAG + i, 0, 0, 0)
                    if nxt:
                        pe_V(pe, j, u + 1, 2, n1 + 1)
                    if weights:
                        for k in range(7, len(WPIECES)):
                            turning(k)
                    pe_turn(pe, j, u, 0)

                with pe.Fori(0, B // 2 - 1) as j:
                    for u in range(2):
                        round0(j, u, True, True)
                round0(B // 2 - 1, 0, False, True)
                round0(B // 2 - 1, 1, False, False, True)

            @block.vector
            def _(dve):
                dve.wait_ge(s_x, 32)
                layernorm_stats(dve)
                layernorm_rows(dve, 0)
                dve.wait_ge(s_bias, 16 * 8)
                nc.vector.tensor_scalar(brow[:, :, :], brow[:, :, :], WS, None, ALU.mult)
                nc.vector.tensor_scalar(bcol[:, :, :], bcol[:, :, :], WS, None, ALU.mult).then_inc(s_biasp, 1)
                dve.wait_ge(s_wh8, 1)
                nc.vector.scalar_tensor_tensor(out=wal[:, :, :], in0=r_attn, scalar=WS, in1=wah[:, :, :],
                                               op0=ALU.mult, op1=ALU.subtract).then_inc(s_split, 1)
                for kc in range(KC):
                    wide_lo(dve, kc, xTh[:, kc, :], xTl[:, kc, :])
                dve.wait_ge(s_biasp, 1)
                for mb in range(KC):
                    wide_lo(dve, 2 + mb, qh[:, mb, :], ql[:, mb, :], bcol[:, 0, mb:mb + 1])
                for mb in range(KC):
                    wide_lo(dve, 4 + mb, skh[:, mb, :], skl[:, mb, :], bcol[:, 1, mb:mb + 1])
                for p in range(2):
                    nc.vector.memset(V1s[p][:, :, :, DH:VW], WS)
                nc.vector.memset(Vs[:, :, :, DH:VW], WS)
                dve.wait_ge(s_wh8, 2)
                for dst, src, hi in ((wrl[:, :, :], r_ref[:, :, 0:D], wrh[:, :, :]),
                                     (wvl[:, :, 0, :], r_ref[:, :, D:2 * D], wvh[:, :, 0, :]),
                                     (wpl[:, 0, :, :], r_proj, wph[:, 0, :, :]),
                                     (gwl[:, :, :], gwr[:, :, :], gwh[:, :, :])):
                    last = nc.vector.scalar_tensor_tensor(out=dst, in0=src, scalar=WS, in1=hi, op0=ALU.mult,
                                                          op1=ALU.subtract)
                last.then_inc(s_split, 1)
                for n in range(2):
                    dve.wait_ge(s_wd, 6 + n + 1)
                    for i in range(4):
                        last = nc.vector.tensor_tensor(
                            Vs[:, 4 * n + i, :, 0:DH],
                            wide[(6 + n) % 4][0:T, i * D:(i + 1) * D].rearrange("p (h d) -> p h d", h=H),
                            brow[0:T, 0, :].rearrange("p (h d) -> p h d", h=H), ALU.add)
                    last.then_inc(s_wf, 1)
                for n, dsts in ((8, ((w1kh[:, 0], w1kl[:, 0]), (wvh[:, :, 1], wvl[:, :, 1]))),
                                (9, ((w1kh[:, 1], w1kl[:, 1]), (wph[:, 1], wpl[:, 1])))):
                    dve.wait_ge(s_wh, n + 1 - 2)
                    for i, (hi, lo) in enumerate(dsts):
                        last = nc.vector.scalar_tensor_tensor(
                            out=lo, in0=wide[n % 4][:, 512 * i:512 * i + 512].rearrange("p (k n) -> p k n", k=KC),
                            scalar=WS, in1=hi, op0=ALU.mult, op1=ALU.subtract)
                    last.then_inc(s_wf, 1)
                dve.wait_ge(s_zero, 1)
                for p in range(2):
                    nc.vector.memset(Vc[p][:, :, :, DH:VW], WS)
                dve.wait_ge(s_tanh, 1)
                nc.vector.tensor_scalar(tgs[:, :], tg[:, :], 1.0 / WS, None, ALU.mult)
                nc.vector.tensor_scalar(clipt[:, :], clipt[:, :], 1.0, 0.5 / QMAX, ALU.add, ALU.mult)
                nc.vector.tensor_scalar(b1c[:, :, :], b1c[:, :, :], WS, None, ALU.mult)
                for o in range(2):
                    for kc in range(KC):
                        dve_lo_T(dve, 0, o, kc, 6 * o + kc, 6 * o + kc)
                    for k in range(4):
                        dve_lo_K(dve, 0, o, k, 6 * o + 2 + k, 6 * o + 2 + k)
                for c in range(3):
                    dve_V(dve, 0, 0, c, 12 + c)
                    for h in range(SM0[c], SM0[c + 1]):
                        dve_max(dve, 0, 0, h, 0, 0)
                dve_N(dve, 0, 0, 15)

                def round0(j, u, keys, nxt):
                    i = 2 * j + u
                    n0 = 16 + 10 * i
                    nh0 = 12 + 6 * i
                    nv = n0 + (NV0 if keys else 0)
                    h = 0
                    for t in range(16):
                        kind = TVK.get(t, "")
                        if keys and kind[:1] == "T":
                            dve_lo_T(dve, j, u + 2, int(kind[1]), n0 + int(kind[1]), nh0 + int(kind[1]))
                        elif keys and kind[:1] == "K":
                            k = int(kind[1])
                            dve_lo_K(dve, j, u + 2, k, n0 + NK0 + k, nh0 + 2 + k)
                        elif nxt and kind[:1] == "V":
                            dve_V(dve, j, u + 1, int(kind[1]), nv + int(kind[1]))
                        if nxt:
                            for _ in range(SMH[t]):
                                dve_max(dve, j, u + 1, h, 0, 0)
                                h += 1
                        if nxt and t == NSTEP:
                            n1 = n0 + (NN0 if keys else 2)
                            dve_N(dve, j, u + 1, n1)
                    if nxt:
                        dve_V(dve, j, u + 1, 2, n1 + 1)
                    dve_norm(dve, j, u, 0)

                with dve.Fori(0, B // 2 - 1) as j:
                    for u in range(2):
                        round0(j, u, True, True)
                round0(B // 2 - 1, 0, False, True)
                nc.vector.memset(wm[:, :], 1.0).then_inc(s_fm, 1)
                dve.wait_ge(s_fm, 1)
                dve.wait_ge(s_fw, 16 * 5)
                for r, base in ((rg, 0), (ru, NIB)):
                    nc.vector.tensor_reduce(wm[:, base:base + NIB - 1], r[:, 0:NIB - 1, :], X, ALU.max,
                                            apply_absolute_value=True)
                    nc.vector.tensor_reduce(wm[0:LASTI, base + NIB - 1:base + NIB], r[0:LASTI, NIB - 1:NIB, :], X,
                                            ALU.max, apply_absolute_value=True)
                nc.vector.tensor_reduce(wm[:, 2 * NIB:], rd_[:, :, 0:NI], X, ALU.max,
                                        apply_absolute_value=True).then_inc(s_fm, 1)
                dve.wait_ge(s_fm, 2)
                nc.vector.tensor_scalar(wm[:, :], wm[:, :], 1.0 / QMAX, None, ALU.mult).then_inc(s_fm, 1)
                dve.wait_ge(s_fm, 3)
                nc.vector.reciprocal(winv[:, :], wm[:, :]).then_inc(s_fs, 1)
                dve_bias_in(dve, 0)
                for k, (m, kc, ibs) in enumerate(WPIECES):
                    dve.wait_ge(s_ft, k + 1)
                    if m < 2:
                        c0, c1 = ibs[0] * P, min(NI, (ibs[-1] + 1) * P)
                        last = nc.vector.tensor_scalar((wgT, wuT)[m][:, kc, c0:c1], misc[k % 3][:, 0:c1 - c0], -MAGIC,
                                                       None, ALU.add)
                    elif ibs[-1] < NIB - 1:
                        last = nc.vector.tensor_scalar(wdT[:, ibs[0]:ibs[-1] + 1, :].rearrange("p i d -> p (i d)"),
                                                       misc[k % 3][:, 0:2 * D], -MAGIC, None, ALU.add)
                    else:
                        nc.vector.tensor_scalar(wdT[:, ibs[0], :], misc[k % 3][:, 0:D], -MAGIC, None, ALU.add)
                        last = nc.vector.tensor_scalar(wdT[0:LASTI, ibs[1], :], misc[k % 3][0:LASTI, D:2 * D], -MAGIC,
                                                       None, ALU.add)
                    last.then_inc(s_fc, 1)
                round0(B // 2 - 1, 1, False, False)

        PLAN = (["a0", "a1", "p0", "p1", "sd", "xm", "xb", "x0", "x1"]
                + [f"{m}{ib}" for ib in range(NIB) for m in ("gate", "up")]
                + ["hm", "hb", "y0", "y1", "q_x0", "q_x1", "q0", "q1",
                   "o_a0", "o_a1", "o_p0", "o_p1", "m_x0", "m_x1", "rt", "ct", "b0", "b1"])
        U = {name: 10 + k for k, name in enumerate(PLAN)}
        HALVES = ["a0", "a1", "q_x0", "q_x1", "q0", "q1", "o_a0", "o_a1", "m_x0", "m_x1"]
        UH = {name: 8 + k for k, name in enumerate(HALVES)}

        ROUTER = {"rt": 2, "ct": 3, "b0": 2, "b1": 3}

        def W(name):
            return wide[ROUTER.get(name, U[name] % 4)]

        def pe_free(pe, name):
            pe.wait_ge(s_wf, U[name] - 3)

        def pe_attT(pe, kc, name):
            pe_free(pe, name)
            for b in range(B):
                o0 = 512 * (b // 4) + (b % 4) * T
                last = nc.tensor.transpose(W(name)[:, o0:o0 + T], aall[:, b, kc * P:(kc + 1) * P], ident[0:T, 0:T])
            last.then_inc(s_wd, 1)

        def act_attT(act, kc, name):
            act.wait_ge(s_wd, U[name] + 1)
            src = W(name).rearrange("p (a n) -> p a n", a=2)[:, :, 0:4 * T]
            nc.scalar.activation(aTh[:, kc, :].rearrange("p (a n) -> p a n", a=2), src, ACT.Copy).then_inc(s_wh, 1)

        def dve_attT(dve, kc, name):
            dve.wait_ge(s_wh, UH[name] + 1)
            src = W(name).rearrange("p (a n) -> p a n", a=2)[:, :, 0:4 * T]
            nc.vector.tensor_tensor(aTl[:, kc, :].rearrange("p (a n) -> p a n", a=2), src,
                                    aTh[:, kc, :].rearrange("p (a n) -> p a n", a=2), ALU.subtract).then_inc(s_wf, 1)

        def pe_out_proj(pe, l, names):
            for t, (t0, tn) in enumerate(TT):
                if t % 4 == 0:
                    pe_free(pe, names[t // 4])
                o0 = (t % 4) * D
                for kc in range(KC):
                    last = split3(pe, W(names[t // 4])[0:tn, o0:o0 + D], aTh[:, kc, t0:t0 + tn],
                                  aTl[:, kc, t0:t0 + tn], wph[:, l, kc, :], wpl[:, l, kc, :], kc == 0, kc == KC - 1)
                if t % 4 == 3 or t == FULL:
                    last.then_inc(s_wd, 1)

        def tile_groups(name0, name1):
            return [(name0, P, 0, 4), (name1, P, 4, FULL), (name1, LAST, FULL, NTILE)]

        def dve_residual(dve, names, scalar):
            for name, rows, t0, t1 in tile_groups(*names):
                dve.wait_ge(s_wd, U[name] + 1)
                o0 = (t0 % 4) * D
                ins = nc.vector.scalar_tensor_tensor(
                    out=xr[0:rows, t0:t1, :], in0=W(name)[0:rows, o0:o0 + (t1 - t0) * D].rearrange(
                        "p (t d) -> p t d", d=D), scalar=scalar[0:rows, :], in1=xr[0:rows, t0:t1, :],
                    op0=ALU.mult, op1=ALU.add)
                if t1 in (4, NTILE):
                    ins.then_inc(s_wf, 1)
                    dve.wait_ge(s_wf, U[name] + 1)
                else:
                    ins.then_inc(s_dve, 1)
                    step[0] += 1
                    dve.wait_ge(s_dve, step[0])

        def pe_max_bcast(pe, nm_, nb_, k):
            pe.wait_ge(s_am, k)
            pe_free(pe, nm_)
            nc.tensor.transpose(W(nm_)[0:1, 0:P], small[:, 2:3], ident[:, :]).then_inc(s_wd, 1)
            pe.wait_ge(s_wf, U[nm_] + 1)
            nc.tensor.matmul(W(nb_)[:, 0:1], ones[0:1, :], row1[:, :], start=True, stop=True).then_inc(s_wd, 1)

        def dve_max_bcast(dve, nm_, nb_, clip, col):
            dve.wait_ge(s_wd, U[nm_] + 1)
            nc.vector.tensor_reduce(row1[:, :], W(nm_)[0:1, 0:P], X, ALU.max).then_inc(s_wf, 1)
            dve.wait_ge(s_wd, U[nb_] + 1)
            nc.vector.tensor_scalar(small[:, col:col + 1], W(nb_)[:, 0:1], clip, None, ALU.mult).then_inc(s_wf, 1)
            dve.wait_ge(s_wf, U[nb_] + 1)
            nc.vector.reciprocal(small[:, col + 1:col + 2], small[:, col:col + 1]).then_inc(s_dve, 1)
            step[0] += 1
            dve.wait_ge(s_dve, step[0])


        es_a.close()
        es_f = es_att.enter_context(ExitStack())
        dgd = sb("dgd", [P, KC, P], F32, es_f)
        sdb = sb("sdb", [P, D], F32, es_f)
        th = [sb(f"th{k}", [P, NT], F32, es_f) for k in range(2)]
        hid = PTf[:, 0:3, :].rearrange("p c n -> p (c n)")[:, 0:NIB * NT].rearrange("p (i n) -> p i n", i=NIB)
        hq = sb("hq", [P, NIB, NT], F16, es_f)
        fac = sb("fac", [P, 2, NIB], F32, es_f)
        hmx = sb("hmx", [P, NIB], F32, es_f)
        s_am = sem("row_maxima_taken")
        s_sc = sem("scale_made")
        s_th = sem("silu_made")
        s_hq = sem("hidden_rounded")
        s_hz = sem("hidden_in_fp16")
        s_xq = sem("rows_rounded")

        with nc.Block() as block:

            @block.gpsimd
            def _(pool):
                pool_rstd(pool, 1)

            @block.scalar
            def _(act):
                for kc in range(KC):
                    act_attT(act, kc, f"a{kc}")
                act.wait_ge(s_sc, 1)
                for ib in range(NIB):
                    n = P if ib < NIB - 1 else LASTI
                    act.wait_ge(s_wd, U[f"gate{ib}"] + 1)
                    if ib >= 2:
                        act.wait_ge(s_wf, U[f"up{ib - 2}"] + 1)
                    nc.scalar.activation(th[ib % 2][0:n, :], W(f"gate{ib}")[0:n, 0:NT], ACT.Silu,
                                         scale=fac[0:n, 0, ib:ib + 1]).then_inc(s_th, 1)
                for ib in range(NIB):
                    n = P if ib < NIB - 1 else LASTI
                    act.wait_ge(s_hq, ib + 1)
                    nc.scalar.activation(hq[0:n, ib, :], hid[0:n, ib, :], ACT.Identity, bias=magic[0:n, 1:2]
                                         ).then_inc(s_hz, 1)

            @block.tensor
            def _(pe):
                for kc in range(KC):
                    pe_attT(pe, kc, f"a{kc}")
                pe.wait_ge(s_wf, U["a1"] + 1)
                pe_out_proj(pe, 0, ("p0", "p1"))
                pe.wait_ge(s_fm, 4)
                pe_free(pe, "sd")
                for k in range(KC):
                    last = nc.tensor.matmul(W("sd")[:, k * P:(k + 1) * P], ones[:, :], dgd[:, k, :],
                                            start=True, stop=True)
                last.then_inc(s_wd, 1)
                pe_max_bcast(pe, "xm", "xb", 1)
                pe.wait_ge(s_xq, 1)
                for kc in range(KC):
                    pe_free(pe, f"x{kc}")
                    transpose_rows(pe, U[f"x{kc}"], kc)
                pe.wait_ge(s_wf, U["x1"] + 1)
                for ib in range(NIB):
                    n = P if ib < NIB - 1 else LASTI
                    for m, wt in (("gate", wgT), ("up", wuT)):
                        name = f"{m}{ib}"
                        pe_free(pe, name)
                        for t0, t1 in ((0, WIDE0), (WIDE0, NT)):
                            for kc in range(KC):
                                last = nc.tensor.matmul(W(name)[0:n, t0:t1], wt[:, kc, ib * P:ib * P + n],
                                                        xTh[:, kc, t0:t1], start=(kc == 0), stop=(kc == KC - 1))
                        last.then_inc(s_wd, 1)
                pe_max_bcast(pe, "hm", "hb", 2)
                pe_free(pe, "y1")
                for ib in range(NIB):
                    n = P if ib < NIB - 1 else LASTI
                    pe.wait_ge(s_hz, ib + 1)
                    for t, (t0, tn) in enumerate(TT):
                        last = nc.tensor.matmul(W(f"y{t // 4}")[0:tn, (t % 4) * D:(t % 4 + 1) * D],
                                                hq[0:n, ib, t0:t0 + tn], wdT[0:n, ib, :],
                                                start=(ib == 0 and t % 2 == 0), stop=(ib == NIB - 1),
                                                skip_group_check=True)
                        if ib == NIB - 1 and t in (3, FULL):
                            last.then_inc(s_wd, 1)

            @block.vector
            def _(dve):
                def link(ins):
                    ins.then_inc(s_dve, 1)
                    step[0] += 1
                    dve.wait_ge(s_dve, step[0])

                link(nc.vector.memset(small[:, :], 0.0))
                for kc in range(KC):
                    dve_attT(dve, kc, f"a{kc}")
                for k in range(KC):
                    last = nc.vector.tensor_scalar(dgd[:, k, :], ident[:, :], wm[:, 2 * NIB + k:2 * NIB + k + 1], None,
                                                   ALU.mult)
                last.then_inc(s_fm, 1)
                dve_residual(dve, ("p0", "p1"), tgs[:, 0:1])
                layernorm_stats(dve)
                layernorm_rows(dve, 1)
                dve.wait_ge(s_xn, 2 * NTILE)
                nc.vector.tensor_reduce(small[:, 2:3], xn[:, :, :], XY, ALU.max, apply_absolute_value=True
                                        ).then_inc(s_am, 1)
                dve.wait_ge(s_wd, U["sd"] + 1)
                nc.vector.tensor_copy(sdb[:, :], W("sd")[:, 0:D]).then_inc(s_wf, 1)
                dve_max_bcast(dve, "xm", "xb", clipt[:, 0:1], 4)
                link(nc.vector.tensor_scalar(xn[:, :, :], xn[:, :, :], small[:, 5:6], MAGIC, ALU.mult, ALU.add))
                nc.vector.tensor_scalar(xn[:, :, :], xn[:, :, :], MAGIC + QMAX, MAGIC - QMAX - 1.0, ALU.min, ALU.max
                                        ).then_inc(s_xq, 1)
                nc.vector.tensor_scalar(fac[:, 0:2, :].rearrange("p m i -> p (m i)"), wm[:, 0:2 * NIB], small[:, 4:5],
                                        None, ALU.mult).then_inc(s_sc, 1)
                dve.wait_ge(s_sc, 1)
                for kc in range(KC):
                    dve.wait_ge(s_wd, U[f"x{kc}"] + 1)
                    nc.vector.tensor_scalar(xTh[:, kc, :], W(f"x{kc}")[:, 0:NT], -MAGIC, None, ALU.add).then_inc(s_wf, 1)
                link(nc.vector.memset(hmx[:, :], 0.0))
                for ib in range(NIB + 1):
                    if ib < NIB:
                        n = P if ib < NIB - 1 else LASTI
                        dve.wait_ge(s_th, ib + 1)
                        dve.wait_ge(s_wd, U[f"up{ib}"] + 1)
                        nc.vector.scalar_tensor_tensor(out=hid[0:n, ib, :], in0=W(f"up{ib}")[0:n, 0:NT],
                                                       scalar=fac[0:n, 1, ib:ib + 1], in1=th[ib % 2][0:n, :],
                                                       op0=ALU.mult, op1=ALU.mult).then_inc(s_wf, 2)
                    if ib > 0:
                        i = ib - 1
                        n = P if i < NIB - 1 else LASTI
                        dve.wait_ge(s_wf, U[f"up{i}"] + 1)
                        ins = nc.vector.tensor_reduce(hmx[0:n, i:i + 1], hid[0:n, i, :], X, ALU.max,
                                                      apply_absolute_value=True)
                link(ins)
                nc.vector.tensor_reduce(small[:, 2:3], hmx[:, :], X, ALU.max).then_inc(s_am, 1)
                dve_max_bcast(dve, "hm", "hb", clipt[:, 1:2], 6)
                for ib in range(NIB):
                    n = P if ib < NIB - 1 else LASTI
                    link(nc.vector.tensor_scalar(hid[0:n, ib, :], hid[0:n, ib, :], small[0:n, 7:8], MAGIC,
                                                 ALU.mult, ALU.add))
                    nc.vector.tensor_scalar(hid[0:n, ib, :], hid[0:n, ib, :], MAGIC + QMAX, MAGIC - QMAX - 1.0,
                                            ALU.min, ALU.max).then_inc(s_hq, 1)
                link(nc.vector.tensor_scalar(sdb[:, :], sdb[:, :], small[:, 6:7], tg[:, 2:3], ALU.mult, ALU.mult))
                for name, rows, t0, t1 in tile_groups("y0", "y1"):
                    dve.wait_ge(s_wd, U[name] + 1)
                    o0 = (t0 % 4) * D
                    ins = nc.vector.tensor_tensor(
                        xn[0:rows, t0:t1, :], W(name)[0:rows, o0:o0 + (t1 - t0) * D].rearrange("p (t d) -> p t d", d=D),
                        sdb[0:rows, :].unsqueeze(1).to_broadcast([rows, t1 - t0, D]), ALU.mult)
                    if t1 in (4, NTILE):
                        ins.then_inc(s_wf, 1)
                        dve.wait_ge(s_wf, U[name] + 1)
                    else:
                        link(ins)
                    link(nc.vector.tensor_tensor(xr[0:rows, t0:t1, :], xr[0:rows, t0:t1, :], xn[0:rows, t0:t1, :],
                                                 ALU.add))

        es_f.close()
        es_m = es_att.enter_context(ExitStack())
        w1r = share[:, 0:KC * DF].rearrange("p (k n) -> p k n", k=KC)
        w2r = share[:, KC * DF:KC * DF + FC * D].rearrange("p (f n) -> p f n", f=FC)
        w1h = [sb(f"w1h{p}", [P, KC, FC, P], F16, es_m) for p in range(2)]
        w1l = [sb(f"w1l{p}", [P, KC, FC, P], F16, es_m) for p in range(2)]
        w2h = [sb(f"w2h{p}", [P, FC, D], F16, es_m) for p in range(2)]
        w2l = [sb(f"w2l{p}", [P, FC, D], F16, es_m) for p in range(2)]
        s_w1 = sem("expert_w1_loaded")
        s_w2 = sem("expert_w2_loaded")
        s_w1h = sem("expert_w1_high_half")
        s_w2h = sem("expert_w2_high_half")
        s_w1l = sem("expert_w1_split")
        s_w2l = sem("expert_w2_split")
        SMN, STN, NBN = H * B, 16 * B, B
        MN = 80
        SMH1 = [2, 2, 2, 2, 2, 2, 2, 2, 0, 0, 0, 0]
        NSTEP1 = 8
        PVL1 = [2, 1, 1, 0, 0, 0, 0, 0, 0, 0, 0, 0]
        PVH1 = [0, 0, 0, 1, 2, 1, 1, 2, 1, 1, 2, 1]
        NTURN1 = 4
        NST1 = 12
        QB = 16 * 8

        def sp_w1(sp, e):
            sp.dma_start(w1r[:, :, :], w1[bass.ds(e, 1)].rearrange("e (k p) n -> p (e k) n", p=P)).then_inc(s_w1, 16)

        def sp_w2(sp, e):
            sp.dma_start(w2r[:, :, :], w2[bass.ds(e, 1)].rearrange("e (p f) n -> p (e f) n", f=FC)).then_inc(s_w2, 16)

        def act_w1(act, e, p):
            act.wait_ge(s_w1, 16 * (e + 1))
            nc.scalar.activation(w1h[p][:, :, :, :], w1r[:, :, :].rearrange("p k (m c) -> p k c m", c=FC), ACT.Copy,
                                 scale=WS).then_inc(s_w1h, 1)

        def act_w2(act, e, p):
            act.wait_ge(s_w2, 16 * (e + 1))
            nc.scalar.activation(w2h[p][:, :, :].rearrange("p c n -> p (c n)"), w2r[:, :, :].rearrange("p c n -> p (c n)"),
                                 ACT.Copy, scale=WS).then_inc(s_w2h, 1)

        def dve_w1(dve, e, p):
            dve.wait_ge(s_w1h, e + 1)
            for k in range(KC):
                last = nc.vector.scalar_tensor_tensor(
                    out=w1l[p][:, k, :, :], in0=w1r[:, k, :].rearrange("p (m c) -> p c m", c=FC), scalar=WS,
                    in1=w1h[p][:, k, :, :], op0=ALU.mult, op1=ALU.subtract)
            last.then_inc(s_w1l, 1)

        def dve_w2(dve, e, p):
            dve.wait_ge(s_w2h, e + 1)
            nc.vector.scalar_tensor_tensor(out=w2l[p][:, :, :].rearrange("p c n -> p (c n)"),
                                           in0=w2r[:, :, :].rearrange("p c n -> p (c n)"), scalar=WS,
                                           in1=w2h[p][:, :, :].rearrange("p c n -> p (c n)"), op0=ALU.mult,
                                           op1=ALU.subtract).then_inc(s_w2l, 1)

        with nc.Block() as block:

            @block.sync
            def _(sp):
                for o in range(2):
                    for mb in range(KC):
                        sp_stack1(sp, 0, o, mb, queries=False)
                sp_w1(sp, 0)
                sp_w2(sp, 0)
                sp.dma_start(Vc[0][:, :, :, 0:VW].rearrange("p c h v -> p (c h) v"),
                             v1_dram[0].rearrange("p (n v) -> p n v", v=VW)).then_inc(s_vc[0], 16)
                for mb in range(KC):
                    sp.wait_ge(s_wf, U[f"q{mb}"] + 1)
                    sp_halves_out(sp, q_dram, (qh, ql), mb, QSLOTS)
                sp.wait_ge(s_qw, QB + 16 * 4)
                for o in range(2):
                    for mb in range(KC):
                        sp_stack1(sp, 0, o, mb, keys=False)
                sp.wait_ge(s_mf, MN + 1)
                sp.dma_start(QS[0][KROWS:KROWS + 1, :, :], nm[0][:, :]).then_inc(s_nm[0], 16)
                sp.wait_ge(s_w1l, 1)
                sp_w1(sp, 1)

                def round1(j, u, keys, nxt):
                    p = u % 2
                    i = 2 * j + u
                    if nxt:
                        sp.wait_ge(s_std, STN + NST1 * i + 6)
                        sp.dma_start(Vc[1 - p][:, :, :, 0:VW].rearrange("p c h v -> p (c h) v"),
                                     v1_dram[bass.ds(i + 1, 1)].rearrange("b p (n v) -> (b p) n v", v=VW)
                                     ).then_inc(s_vc[1 - p], 16)
                    if keys:
                        sp_stack1(sp, j, u + 2, 0)
                    if nxt:
                        sp.wait_ge(s_mf, MN + i + 2)
                        sp.dma_start(QS[1 - p][KROWS:KROWS + 1, :, :], nm[1 - p][:, :]).then_inc(s_nm[1 - p], 16)
                    if keys:
                        sp.wait_ge(s_std, STN + NST1 * (i + 1))
                        sp_stack1(sp, j, u + 2, 1)

                with sp.Fori(0, B // 2 - 1) as j:
                    for u in range(2):
                        round1(j, u, True, True)
                round1(B // 2 - 1, 0, False, True)

            @block.gpsimd
            def _(pool):
                pool_rstd(pool, 2)

            @block.scalar
            def _(act):
                for kc in range(KC):
                    wide_hi(act, U[f"q_x{kc}"], xTh[:, kc, :])
                for mb in range(KC):
                    wide_hi(act, U[f"q{mb}"], qh[:, mb, :], bcol[:, 4, mb:mb + 1])
                act_w1(act, 0, 0)
                act_w2(act, 0, 0)

                def round1(j, o, first):
                    for t in range(NST1):
                        act_exp(act, j, o, t, 1, STN)
                        if t == NTURN1 - 1 and not first:
                            act_evac(act, j, o - 1, NBN)

                round1(0, 0, True)
                with act.Fori(0, B // 2 - 1) as j:
                    for o in (1, 2):
                        round1(j, o, False)
                round1(B // 2 - 1, 1, False)
                act_evac(act, B // 2 - 1, 1, NBN)
                act_w1(act, 1, 1)

            @block.tensor
            def _(pe):
                for kc in range(KC):
                    pe_free(pe, f"q_x{kc}")
                    transpose_rows(pe, U[f"q_x{kc}"], kc, 2)
                pe.wait_ge(s_wf, U["q_x1"] + 1)
                for mb in range(KC):
                    pe_free(pe, f"q{mb}")
                    project_T(pe, U[f"q{mb}"], w1kh[:, 1], w1kl[:, 1], mb)
                pe.wait_ge(s_wf, U["q1"] + 1)
                for h in range(H):
                    pe_SM(pe, 0, 0, h, 1, SMN)
                pe_N(pe, 0, 0, SMN, MN, MN)

                def round1(j, o, first, nxt):
                    i = 2 * j + o
                    h = hv = 0
                    hl = sum(PVH1)
                    for t in range(NST1):
                        pe_ST(pe, j, o, t, 1, STN, 16 * (B // 2))
                        if not first:
                            for _ in range(PVL1[t]):
                                pe_PV(pe, j, o - 1, hl, 1, STN, NBN)
                                hl += 1
                            if t == NTURN1:
                                pe_turn(pe, j, o - 1, NBN)
                        if nxt:
                            for _ in range(SMH1[t]):
                                pe_SM(pe, j, o + 1, h, 1, SMN)
                                h += 1
                            if t == NSTEP1:
                                pe_N(pe, j, o + 1, SMN, MN + i + 1, MN + i + 1)
                        for _ in range(PVH1[t]):
                            pe_PV(pe, j, o, hv, 1, STN, NBN)
                            hv += 1

                round1(0, 0, True, True)
                with pe.Fori(0, B // 2 - 1) as j:
                    for o in (1, 2):
                        round1(j, o, False, True)
                round1(B // 2 - 1, 1, False, False)
                for h in range(sum(PVH1), H):
                    pe_PV(pe, B // 2 - 1, 1, h, 1, STN, NBN)
                pe_turn(pe, B // 2 - 1, 1, NBN)

            @block.vector
            def _(dve):
                layernorm_stats(dve)
                layernorm_rows(dve, 2)
                for kc in range(KC):
                    wide_lo(dve, U[f"q_x{kc}"], xTh[:, kc, :], xTl[:, kc, :], None, UH[f"q_x{kc}"])
                for mb in range(KC):
                    wide_lo(dve, U[f"q{mb}"], qh[:, mb, :], ql[:, mb, :], bcol[:, 4, mb:mb + 1], UH[f"q{mb}"])
                nc.vector.memset(KS[0][KROWS:KROWS + 1, :, 0:TC], WS * WS)
                for h in range(H):
                    dve_max(dve, 0, 0, h, 1, SMN)
                dve_N(dve, 0, 0, MN)
                dve_w1(dve, 0, 0)
                dve_w2(dve, 0, 0)

                def round1(j, o, first, nxt):
                    i = 2 * j + o
                    for h in range(H):
                        if nxt:
                            dve_max(dve, j, o + 1, h, 1, SMN)
                        if h == 7 and not first:
                            dve_norm(dve, j, o - 1, NBN)
                    if nxt:
                        dve_N(dve, j, o + 1, MN + i + 1)

                round1(0, 0, True, True)
                with dve.Fori(0, B // 2 - 1) as j:
                    for o in (1, 2):
                        round1(j, o, False, True)
                round1(B // 2 - 1, 1, False, False)
                dve_norm(dve, B // 2 - 1, 1, NBN)
                dve_w1(dve, 1, 1)

        lg = sb("lg", [P, NTILE, E])
        sc = sb("sc", [P, NTILE, E])
        rk = sb("rk", [P, NTILE, E])
        red = sb("red", [P, NTILE])
        cmp_ = sb("cmp", [P, NTILE, E, E])
        eqq = sb("eqq", [P, NTILE, E, E])
        low = sb("low", [P, E, E])
        cT, cG = (Vc[p][0:E, :, :, :].rearrange("p c h v -> p (c h v)")[:, 0:NT] for p in range(2))
        G = [r[:, :, :].rearrange("p k n -> p (k n)").bitcast(F32) for r in (ql, aTl)]
        yg = aTh[:, :, :].rearrange("p k n -> p (k n)").bitcast(F32)
        acc = xn[:, :, :].rearrange("p t d -> p (t d)")[:, 0:KC * NT].rearrange("p (k n) -> p k n", k=KC)
        hA = PTf.rearrange("p c n -> p (c n)").bitcast(F16)
        hB = KSa[:, :, :, :].rearrange("p a h s -> p (a h s)")
        hTh, hTl = ([h_[:, k * FC * NT:(k + 1) * FC * NT].rearrange("p (f n) -> p f n", f=FC) for h_ in (hA, hB)]
                    for k in range(2))
        af = aallw[:, :, :].rearrange("p b d -> p (b d)")
        rr = [af[:, 0:NT], af[:, NT:2 * NT], qh[:, :, :].rearrange("p k n -> p (k n)").bitcast(F32)]
        YB = 2
        s_ex = sem("logits_through_exp")
        s_lg = sem("logits_ready")
        s_low = sem("order_mask_made")
        s_cb = sem("router_done")
        s_hd = sem("hidden_product_done")
        s_r = sem("hidden_through_relu")
        s_hh = sem("hidden_high_half")
        s_hl = sem("hidden_split")
        s_yd = sem("expert_product_done")
        s_yt = sem("expert_product_read")
        s_ya = sem("expert_product_added")
        s_gw = sem("shares_written")
        s_g = [sem(f"shares_loaded{p}") for p in range(2)]
        s_fin = sem("sum_turned")
        s_o = sem("tiles_finished")

        with nc.Block() as block:

            @block.sync
            def _(sp):
                def shares_in(e, q):
                    sp.dma_start(G[q], g_dram[bass.ds(e, 1), :].partition_broadcast(P)).then_inc(s_g[q], 16)

                def round_w(e, q, first):
                    if first:
                        sp.wait_ge(s_w1l, e + 2)
                        sp_w1(sp, e + 2)
                    sp.wait_ge(s_w2l, e + 1)
                    sp_w2(sp, e + 1)
                    sp.wait_ge(s_yt, 2 * e + YB)
                    shares_in(e + 1, 1 - q)

                sp.wait_ge(s_wf, U["ct"] + 1)
                sp.dma_start(g_dram[:, :], cG[:, :]).then_inc(s_gw, 16)
                sp.wait_ge(s_gw, 16)
                shares_in(0, 0)
                with sp.Fori(0, E // 2 - 1) as j:
                    for u in range(2):
                        round_w(2 * j + u, u, True)
                round_w(E - 2, 0, False)
                for t, (t0, tn) in enumerate(TT):
                    sp.wait_ge(s_o, t + 1)
                    sp.dma_start(of[t0:t0 + tn, :], xr[0:tn, t, :]).then_inc(s_out, 16)
                sp.wait_ge(s_out, 16 * NTILE)

            @block.gpsimd
            def _(pool):
                nc.gpsimd.memset(low[:, :, :], 1.0).then_inc(s_low, 1)
                pool.wait_ge(s_low, 1)
                nc.gpsimd.affine_select(out=low[:, :, :], in_=low[:, :, :], compare_op=ALU.is_gt, fill=0.0, base=0,
                                        pattern=[[1, E], [-1, E]], channel_multiplier=0).then_inc(s_low, 1)
                pool_rstd(pool, 3)

                def lows(j, u, n0):
                    for f in range(FC):
                        n = n0 + f
                        pool.wait_ge(s_hh, n + 1)
                        nc.gpsimd.tensor_tensor(hTl[u][:, f, :], rr[f % 3][:, :], hTh[u][:, f, :], ALU.subtract
                                                ).then_inc(s_hl, 1)

                with pool.Fori(0, E // 2) as j:
                    for u in range(2):
                        lows(j, u, FC * (2 * j + u))

            @block.scalar
            def _(act):
                for kc in range(KC):
                    act_attT(act, kc, f"o_a{kc}")
                for kc in range(KC):
                    wide_hi(act, U[f"m_x{kc}"], xTh[:, kc, :])
                act.wait_ge(s_lg, 1)
                nc.scalar.activation(sc[:, :, :], lg[:, :, :], ACT.Exp).then_inc(s_ex, 1)

                def highs(e, q):
                    for f in range(FC):
                        act.wait_ge(s_r, FC * e + f + 1)
                        nc.scalar.activation(hTh[q][:, f, :], rr[f % 3][:, :], ACT.Copy).then_inc(s_hh, 1)

                highs(0, 0)
                with act.Fori(0, E // 2 - 1) as j:
                    for u in range(2):
                        highs(2 * j + u + 1, 1 - u)
                        act_w1(act, 2 * j + u + 2, u)
                        act_w2(act, 2 * j + u + 1, 1 - u)
                highs(E - 1, 1)
                act_w2(act, E - 1, 1)

            @block.tensor
            def _(pe):
                for kc in range(KC):
                    pe_attT(pe, kc, f"o_a{kc}")
                pe.wait_ge(s_wf, U["o_a1"] + 1)
                pe_out_proj(pe, 1, ("o_p0", "o_p1"))
                for kc in range(KC):
                    pe_free(pe, f"m_x{kc}")
                    transpose_rows(pe, U[f"m_x{kc}"], kc, 3)
                pe.wait_ge(s_wf, U["m_x1"] + 1)
                for t, (t0, tn) in enumerate(TT):
                    for kc in range(KC):
                        last = split3(pe, W("rt")[0:tn, t * E:(t + 1) * E], xTh[:, kc, t0:t0 + tn],
                                      xTl[:, kc, t0:t0 + tn], gwh[:, kc, :], gwl[:, kc, :], kc == 0, kc == KC - 1)
                last.then_inc(s_wd, 1)

                def hidden(e, q):
                    pe.wait_ge(s_w1l, e + 1)
                    for f in range(FC):
                        n = FC * e + f
                        if not (isinstance(n, int) and n < 2):
                            pe.wait_ge(s_r, n - 1)
                        for kc in range(KC):
                            for lh, rhs in ((w1h[q], xTh), (w1h[q], xTl), (w1l[q], xTh)):
                                for t0, t1 in ((0, WIDE0), (WIDE0, NT)):
                                    last = nc.tensor.matmul(
                                        wide[f % 2][:, t0:t1], lh[:, kc, f, :], rhs[:, kc, t0:t1],
                                        start=(kc == 0 and lh is w1h[q] and rhs is xTh),
                                        stop=(kc == KC - 1 and lh is w1l[q]))
                        last.then_inc(s_hd, 1)
                        if isinstance(n, int) and n == FC - 2:
                            pe.wait_ge(s_cb, 1)
                            for t, (t0, tn) in enumerate(TT):
                                last = nc.tensor.transpose(W("ct")[0:E, t0:t0 + tn], rk[0:tn, t, :],
                                                           ident[0:tn, 0:tn])
                            last.then_inc(s_wd, 1)

                def turn_sum(m):
                    pe.wait_ge(s_ya, KC * (E - 1) + m + 2)
                    for t, (t0, tn) in enumerate(TT):
                        last = nc.tensor.transpose(wide[t // 4][0:tn, (t % 4) * D + m * P:(t % 4) * D + (m + 1) * P],
                                                   acc[:, m, t0:t0 + tn], ident[:, :])
                        if m == 1 and t in (3, FULL):
                            last.then_inc(s_fin, 1)

                def outcome(e, q, end=False):
                    pe.wait_ge(s_hl, FC * (e + 1))
                    pe.wait_ge(s_w2l, e + 1)
                    for m in range(KC):
                        n = KC * e + m
                        pe.wait_ge(s_yt, n - 1 + YB)
                        for f in range(FC):
                            for lh, rhs in ((w2h[q], hTh[q]), (w2h[q], hTl[q]), (w2l[q], hTh[q])):
                                for t0, t1 in ((0, WIDE0), (WIDE0, NT)):
                                    last = nc.tensor.matmul(
                                        wide[2 + m][:, t0:t1], lh[:, f, m * P:(m + 1) * P], rhs[:, f, t0:t1],
                                        start=(f == 0 and lh is w2h[q] and rhs is hTh[q]),
                                        stop=(f == FC - 1 and lh is w2l[q]))
                            if end and m == 1 and f == FC // 2:
                                turn_sum(0)
                        last.then_inc(s_yd, 1)

                hidden(0, 0)
                pe.wait_ge(s_wf, U["ct"] + 1)
                for m in range(KC):
                    for t0, t1 in ((0, WIDE0), (WIDE0, NT)):
                        last = nc.tensor.matmul(W(f"b{m}")[:, t0:t1], b2r[:, m * P:(m + 1) * P], cT[:, t0:t1],
                                                start=True, stop=True)
                    last.then_inc(s_wd, 1)
                with pe.Fori(0, E // 2 - 1) as j:
                    for u in range(2):
                        hidden(2 * j + u + 1, 1 - u)
                        outcome(2 * j + u, u)
                hidden(E - 1, 1)
                outcome(E - 2, 0)
                outcome(E - 1, 1, True)
                turn_sum(1)

            @block.vector
            def _(dve):
                def link(ins):
                    ins.then_inc(s_dve, 1)
                    step[0] += 1
                    dve.wait_ge(s_dve, step[0])

                dve_bias_in(dve, 1)
                for kc in range(KC):
                    dve_attT(dve, kc, f"o_a{kc}")
                dve_residual(dve, ("o_p0", "o_p1"), tgs[:, 1:2])
                layernorm_stats(dve)
                layernorm_rows(dve, 3)
                for kc in range(KC):
                    wide_lo(dve, U[f"m_x{kc}"], xTh[:, kc, :], xTl[:, kc, :], None, UH[f"m_x{kc}"])
                link(nc.vector.memset(lg[:, :, :], 0.0))
                dve.wait_ge(s_wd, U["rt"] + 1)
                for rows, t0, t1 in ((P, 0, FULL), (LAST, FULL, NTILE)):
                    ins = nc.vector.scalar_tensor_tensor(
                        out=lg[0:rows, t0:t1, :], in0=W("rt")[0:rows, t0 * E:t1 * E].rearrange("p (t e) -> p t e", e=E),
                        scalar=1.0 / WS, in1=gbr[0:rows, :].unsqueeze(1).to_broadcast([rows, t1 - t0, E]),
                        op0=ALU.mult, op1=ALU.add)
                ins.then_inc(s_wf, 1)
                dve.wait_ge(s_wf, U["rt"] + 1)
                bc = [P, NTILE, E]
                link(nc.vector.tensor_reduce(red[:, :], lg[:, :, :], X, ALU.max))
                nc.vector.tensor_tensor(lg[:, :, :], lg[:, :, :], red[:, :].unsqueeze(2).to_broadcast(bc),
                                        ALU.subtract).then_inc(s_lg, 1)

                def router(part):
                    b4 = [P, NTILE, E, E]
                    other, own = sc[:, :, :].unsqueeze(2).to_broadcast(b4), sc[:, :, :].unsqueeze(3).to_broadcast(b4)
                    if part == 0:
                        dve.wait_ge(s_ex, 1)
                        link(nc.vector.tensor_reduce(red[:, :], sc[:, :, :], X, ALU.add))
                        link(nc.vector.reciprocal(red[:, :], red[:, :]))
                        link(nc.vector.tensor_tensor(sc[:, :, :], sc[:, :, :], red[:, :].unsqueeze(2).to_broadcast(bc),
                                                     ALU.mult))
                    elif part == 1:
                        nc.vector.tensor_tensor(cmp_[:, :, :, :], other, own, ALU.is_gt)
                        link(nc.vector.tensor_tensor(eqq[:, :, :, :], other, own, ALU.is_equal))
                    elif part == 2:
                        dve.wait_ge(s_low, 2)
                        link(nc.vector.tensor_tensor(eqq[:, :, :, :], eqq[:, :, :, :],
                                                     low[:, :, :].unsqueeze(1).to_broadcast(b4), ALU.mult))
                        link(nc.vector.tensor_tensor(cmp_[:, :, :, :], cmp_[:, :, :, :], eqq[:, :, :, :], ALU.add))
                    elif part == 3:
                        link(nc.vector.tensor_reduce(rk[:, :, :], cmp_[:, :, :, :], X, ALU.add))
                        link(nc.vector.tensor_scalar(rk[:, :, :], rk[:, :, :], 2.0, None, ALU.is_lt))
                    elif part == 4:
                        link(nc.vector.tensor_tensor(rk[:, :, :], rk[:, :, :], sc[:, :, :], ALU.mult))
                        nc.vector.tensor_scalar(rk[:, :, :], rk[:, :, :], tg[:, 3:4], None, ALU.mult).then_inc(s_cb, 1)
                    elif part == FC - 2:
                        dve.wait_ge(s_wd, U["ct"] + 1)
                        nc.vector.tensor_copy(cT[:, :], W("ct")[0:E, 0:NT])
                        nc.vector.tensor_scalar(cG[:, :], W("ct")[0:E, 0:NT], 1.0 / (WS * WS), None, ALU.mult
                                                ).then_inc(s_wf, 1)

                def relus(e, q):
                    for f in range(FC):
                        n = FC * e + f
                        dve.wait_ge(s_hd, n + 1)
                        if not (isinstance(n, int) and n < 3):
                            dve.wait_ge(s_hl, n - 1 if f < 2 else n - 2)
                        nc.vector.tensor_scalar(rr[f % 3][:, :], wide[f % 2][:, 0:NT], b1c[:, bass.ds(e, 1), f], 0.0,
                                                ALU.add, ALU.max).then_inc(s_r, 1)
                        if isinstance(e, int) and e == 0:
                            router(f)

                def adds(e, q, nw1, nw2):
                    if nw1:
                        dve_w1(dve, e + 2, q)
                    if nw2:
                        dve_w2(dve, e + 1, 1 - q)
                    dve.wait_ge(s_g[q], 8 * (e - q) + 16)
                    for m in range(KC):
                        n = KC * e + m
                        dve.wait_ge(s_yd, n + 1)
                        dve.wait_ge(s_ya, n + 1)
                        nc.vector.tensor_tensor(yg, wide[2 + m][:, 0:NT], G[q], ALU.mult).then_inc(s_yt, 1)
                        dve.wait_ge(s_yt, n + 1 + YB)
                        nc.vector.tensor_tensor(acc[:, m, :], acc[:, m, :], yg, ALU.add).then_inc(s_ya, 1)

                relus(0, 0)
                for m in range(KC):
                    dve.wait_ge(s_wd, U[f"b{m}"] + 1)
                    last = nc.vector.tensor_copy(acc[:, m, :], W(f"b{m}")[:, 0:NT])
                    if m == 0:
                        last.then_inc(s_ya, 1)
                last.then_inc(s_yt, YB)
                dve.wait_ge(s_yt, YB)
                with dve.Fori(0, E // 2 - 1) as j:
                    for u in range(2):
                        relus(2 * j + u + 1, 1 - u)
                        adds(2 * j + u, u, True, True)
                relus(E - 1, 1)
                adds(E - 2, 0, False, True)
                adds(E - 1, 1, False, False)
                for w, rows, t0, t1 in ((0, P, 0, 4), (1, P, 4, FULL), (1, LAST, FULL, NTILE)):
                    dve.wait_ge(s_fin, w + 1)
                    o0 = (t0 % 4) * D
                    nc.vector.tensor_tensor(xr[0:rows, t0:t1, :], wide[w][0:rows, o0:o0 + (t1 - t0) * D].rearrange(
                        "p (t d) -> p t d", d=D), xr[0:rows, t0:t1, :], ALU.add).then_inc(s_o, t1 - t0)


_INS = ['x', 'ctx_1024', 'g_xattn', 'g_ffn', 'L0_xattn_w_ref', 'L0_xattn_b_ref', 'L0_xattn_w_attn',
        'L0_xattn_b_attn', 'L0_xattn_w_proj', 'L0_xattn_b_proj', 'L0_ffn_clip_x', 'L0_ffn_clip_down',
        'L0_ffn_w_gate', 'L0_ffn_w_up', 'L0_ffn_w_down', 'L1_xattn_w_q', 'L1_xattn_b_q', 'L1_xattn_w_k',
        'L1_xattn_b_k', 'L1_xattn_w_v', 'L1_xattn_b_v', 'L1_xattn_w_o', 'L1_xattn_b_o', 'L1_ffn_gate_w',
        'L1_ffn_gate_b', 'L1_ffn_w1', 'L1_ffn_b1', 'L1_ffn_w2', 'L1_ffn_b2']


def kernel(**inputs):
    import numpy as _np
    import concourse.bacc as _bacc
    from concourse import mybir as _mybir
    from concourse.bass_utils import run_bass_kernel_spmd as _run

    nc = _bacc.Bacc("TRN2", target_bir_lowering=False, num_devices=1)
    arrays, args = {}, []
    for name in _INS:
        a = _np.ascontiguousarray(inputs[name])
        arrays[f"in_{name}_dram"] = a
        args.append(nc.dram_tensor(f"in_{name}_dram", a.shape, _mybir.dt.from_np(a.dtype), kind="ExternalInput").ap())
    dt = _mybir.dt.from_np(_np.dtype("float32"))
    args.append(nc.dram_tensor("out_0_dram", inputs["x"].shape, dt, kind="ExternalOutput").ap())
    flamingo(nc, *args)
    r = _run(nc, [arrays], core_ids=[0])
    return r.results[0]["out_0_dram"]
```
